# Optimizing a Trainium2 kernel written in Bass

```python
import numpy as np
import jax
import jax.numpy as jnp

def _softmax(x, axis=-1):
    return jax.nn.softmax(x, axis=axis)

def _gelu(x):
    return jax.nn.gelu(x, approximate=True)

def _silu(x):
    return jax.nn.silu(x)

def _sigmoid(x):
    return jax.nn.sigmoid(x)

def _layernorm(x, axis=-1, eps=1e-05):
    m = jnp.mean(x, axis=axis, keepdims=True)
    v = jnp.var(x, axis=axis, keepdims=True)
    return (x - m) / jnp.sqrt(v + eps)

def _scatter_add(tgt, idx, src, axis=0):
    return tgt.at[idx].add(src)

def _segment_sum(src, seg, n):
    return jax.ops.segment_sum(src, seg, n)
kernel_name = 'mk_xattn_ffn_d2_seqx_r4_952b55'

def setup_inputs(seed: int=0):
    np.random.seed(seed)
    _w = jnp.asarray

    def _rec_inputs():
        import jax
        import jax.numpy as jnp
        _rk = jax.random.key(seed)
        x = -0.000125 + 0.9999 * jax.random.normal(jax.random.fold_in(_rk, 1), (8, 256, 256), jnp.float32)
        _lenS = 256 - jax.random.randint(jax.random.fold_in(_rk, 7), (8,), 0, max(1, 256 // 4) + 1, jnp.int32)
        _lenS2 = 256 - jax.random.randint(jax.random.fold_in(_rk, 8), (8,), 0, max(1, 256 // 4) + 1, jnp.int32)
        _ctx_1024P = jax.random.normal(jax.random.fold_in(_rk, 11), (8, 16, 256), jnp.float32)
        _ctx_1024c = jax.random.dirichlet(jax.random.fold_in(_rk, 511), 0.3 * jnp.ones((16,), jnp.float32), (8, 256))
        _ctx_1024t = jnp.einsum('bsk,bkd->bsd', _ctx_1024c, _ctx_1024P)
        _ctx_1024t = _ctx_1024t * jax.lax.rsqrt(jnp.mean(jnp.square(_ctx_1024t)) + 1e-12) * 0.953939
        ctx_1024 = -1.52775e-05 + 0.999936 * (_ctx_1024t + 0.3 * jax.random.normal(jax.random.fold_in(_rk, 611), (8, 256, 256), jnp.float32))
        return (x, ctx_1024)
    x, ctx_1024 = _rec_inputs()

    def _L0_xattn_setup():
        import jax, jax.numpy as jnp
        import numpy as np
        import math
        NHEADS = 16
        CAUSAL = True
        NEG_INF = -1e+18
        key = jax.random.key(seed)
        kq, kk, kv = jax.random.split(key, 3)
        B, S, D = (4, 2048, 256)
        q = jax.random.normal(kq, (B, S, D), dtype=jnp.float32)
        k = jax.random.normal(kk, (B, S, D), dtype=jnp.float32)
        v = jax.random.normal(kv, (B, S, D), dtype=jnp.float32)
        return {'q': q, 'k': k, 'v': v}
    _L0_xattn_all = _L0_xattn_setup()
    _L0_xattn_in = {k: v for k, v in _L0_xattn_all.items() if k in ()}
    del _L0_xattn_all

    def _L0_ffn_setup():
        import jax, jax.numpy as jnp
        import numpy as np
        BLOCK = 32
        W_BITS = 4
        ACT_BITS = 16

        def act_qdq(x):
            qmax = 2.0 ** (ACT_BITS - 1) - 1.0
            scale = jnp.maximum(jnp.max(jnp.abs(x)) / qmax, 1e-12)
            return jnp.clip(jnp.round(x / scale), -qmax - 1.0, qmax) * scale

        def fixed_qdq_u16(x):
            scale = 1.0 / 65536.0
            return jnp.clip(jnp.round(x / scale), 0.0, 65535.0) * scale

        def lpbq_dequant(w):
            O, I = w.shape
            qmax = 2.0 ** (W_BITS - 1) - 1.0
            wb = w.reshape(O, I // BLOCK, BLOCK)
            s = jnp.maximum(jnp.max(jnp.abs(wb), axis=-1, keepdims=True) / qmax, 1e-12)
            wq = jnp.clip(jnp.round(wb / s), -qmax - 1.0, qmax) * s
            return wq.reshape(O, I)
        key = jax.random.key(seed)
        k1, k2, k3, k4 = jax.random.split(key, 4)
        B, S, H, I = (2, 1024, 256, 768)
        x = jax.random.normal(k1, (B, S, H), jnp.float32)
        w_gate = jax.random.normal(k2, (I, H), jnp.float32) * 0.02
        w_up = jax.random.normal(k3, (I, H), jnp.float32) * 0.02
        w_down = jax.random.normal(k4, (H, I), jnp.float32) * 0.02
        return {'x': x, 'w_gate': w_gate, 'w_up': w_up, 'w_down': w_down}
    _L0_ffn_all = _L0_ffn_setup()
    _L0_ffn_in = {k: v for k, v in _L0_ffn_all.items() if k in ('w_gate', 'w_up', 'w_down')}
    del _L0_ffn_all

    def _L1_xattn_setup():
        import jax, jax.numpy as jnp
        import numpy as np
        D_MODEL = 256
        NUM_HEADS = 16
        D_K = D_MODEL // NUM_HEADS
        key = jax.random.key(seed)
        ks = jax.random.split(key, 12)
        B, S, D = (2, 512, D_MODEL)
        scale = 1.0 / np.sqrt(D)
        inp = {'q': jax.random.normal(ks[0], (B, S, D), jnp.float32), 'k': jax.random.normal(ks[1], (B, S, D), jnp.float32), 'v': jax.random.normal(ks[2], (B, S, D), jnp.float32), 'Wq': jax.random.normal(ks[3], (D, D), jnp.float32) * scale, 'bq': jnp.zeros((D,), jnp.float32), 'Wk': jax.random.normal(ks[4], (D, D), jnp.float32) * scale, 'bk': jnp.zeros((D,), jnp.float32), 'Wv': jax.random.normal(ks[5], (D, D), jnp.float32) * scale, 'bv': jnp.zeros((D,), jnp.float32), 'Wo': jax.random.normal(ks[6], (D, D), jnp.float32) * scale, 'bo': jnp.zeros((D,), jnp.float32), 'mask': 0}
        return inp
    _L1_xattn_all = _L1_xattn_setup()
    _L1_xattn_in = {k: v for k, v in _L1_xattn_all.items() if k in ('Wq', 'bq', 'Wk', 'bk', 'Wv', 'bv', 'Wo', 'bo')}
    del _L1_xattn_all

    def _L1_ffn_setup():
        import jax, jax.numpy as jnp
        import numpy as np
        B, S, D, F, E = (2, 256, 256, 512, 8)
        key = jax.random.key(seed)
        ks = jax.random.split(key, 6)
        scale = 0.02
        return {'x': jax.random.normal(ks[0], (B, S, D), dtype=jnp.float32), 'W1': jax.random.normal(ks[1], (E, D, F), dtype=jnp.float32) * scale, 'b1': jnp.zeros((E, F), dtype=jnp.float32), 'W2': jax.random.normal(ks[2], (E, F, D), dtype=jnp.float32) * scale, 'b2': jnp.zeros((E, D), dtype=jnp.float32), 'Wr': jax.random.normal(ks[3], (D, E), dtype=jnp.float32) * scale, 'br': jnp.zeros((E,), dtype=jnp.float32)}
    _L1_ffn_all = _L1_ffn_setup()
    _L1_ffn_in = {k: v for k, v in _L1_ffn_all.items() if k in ('W1', 'b1', 'W2', 'b2', 'Wr', 'br')}
    del _L1_ffn_all
    return {'x': x, 'ctx_1024': ctx_1024, 'L0_ffn_w_gate': _L0_ffn_in['w_gate'], 'L0_ffn_w_up': _L0_ffn_in['w_up'], 'L0_ffn_w_down': _L0_ffn_in['w_down'], 'L1_xattn_Wq': _L1_xattn_in['Wq'], 'L1_xattn_bq': _L1_xattn_in['bq'], 'L1_xattn_Wk': _L1_xattn_in['Wk'], 'L1_xattn_bk': _L1_xattn_in['bk'], 'L1_xattn_Wv': _L1_xattn_in['Wv'], 'L1_xattn_bv': _L1_xattn_in['bv'], 'L1_xattn_Wo': _L1_xattn_in['Wo'], 'L1_xattn_bo': _L1_xattn_in['bo'], 'L1_ffn_W1': _L1_ffn_in['W1'], 'L1_ffn_b1': _L1_ffn_in['b1'], 'L1_ffn_W2': _L1_ffn_in['W2'], 'L1_ffn_b2': _L1_ffn_in['b2'], 'L1_ffn_Wr': _L1_ffn_in['Wr'], 'L1_ffn_br': _L1_ffn_in['br']}

def reference(x, ctx_1024, L0_ffn_w_gate, L0_ffn_w_up, L0_ffn_w_down, L1_xattn_Wq, L1_xattn_bq, L1_xattn_Wk, L1_xattn_bk, L1_xattn_Wv, L1_xattn_bv, L1_xattn_Wo, L1_xattn_bo, L1_ffn_W1, L1_ffn_b1, L1_ffn_W2, L1_ffn_b2, L1_ffn_Wr, L1_ffn_br):
    import jax
    import jax.numpy as jnp

    def _L0_xattn_ref(q, k, v):
        import jax, jax.numpy as jnp
        import numpy as np
        import math
        NHEADS = 16
        CAUSAL = True
        NEG_INF = -1e+18
        B, S, D = q.shape
        hd = D // NHEADS
        qh = q.reshape(B, S, NHEADS, hd)
        kh = k.reshape(B, S, NHEADS, hd)
        vh = v.reshape(B, S, NHEADS, hd)
        scores = jnp.einsum('bsqd,bskd->bsqk', qh, kh) / math.sqrt(hd)
        if CAUSAL:
            mask = jnp.tril(jnp.ones((NHEADS, NHEADS), dtype=bool))
            scores = jnp.where(mask, scores, jnp.asarray(NEG_INF, scores.dtype))
        attn = jax.nn.softmax(scores, axis=-1)
        out = jnp.einsum('bsqk,bskd->bsqd', attn, vh)
        return out.reshape(B, S, D)

    def _L0_ffn_ref(x, w_gate, w_up, w_down):
        import jax, jax.numpy as jnp
        import numpy as np
        BLOCK = 32
        W_BITS = 4
        ACT_BITS = 16

        def act_qdq(x):
            qmax = 2.0 ** (ACT_BITS - 1) - 1.0
            scale = jnp.maximum(jnp.max(jnp.abs(x)) / qmax, 1e-12)
            return jnp.clip(jnp.round(x / scale), -qmax - 1.0, qmax) * scale

        def fixed_qdq_u16(x):
            scale = 1.0 / 65536.0
            return jnp.clip(jnp.round(x / scale), 0.0, 65535.0) * scale

        def lpbq_dequant(w):
            O, I = w.shape
            qmax = 2.0 ** (W_BITS - 1) - 1.0
            wb = w.reshape(O, I // BLOCK, BLOCK)
            s = jnp.maximum(jnp.max(jnp.abs(wb), axis=-1, keepdims=True) / qmax, 1e-12)
            wq = jnp.clip(jnp.round(wb / s), -qmax - 1.0, qmax) * s
            return wq.reshape(O, I)
        x = act_qdq(x)
        up = act_qdq(x @ lpbq_dequant(w_up).T)
        gate = act_qdq(x @ lpbq_dequant(w_gate).T)
        sig = fixed_qdq_u16(jax.nn.sigmoid(gate))
        gate = act_qdq(gate * sig)
        o = act_qdq(gate * up)
        return o @ lpbq_dequant(w_down).T

    def _L1_xattn_ref(q, k, v, Wq, bq, Wk, bk, Wv, bv, Wo, bo, mask):
        import jax, jax.numpy as jnp
        import numpy as np
        D_MODEL = 256
        NUM_HEADS = 16
        D_K = D_MODEL // NUM_HEADS
        B, S, D = q.shape
        H, dk = (NUM_HEADS, D_K)

        def proj(x, W, b):
            return (x @ W.T + b).reshape(B, S, H, dk).transpose(0, 2, 1, 3)
        Q = proj(q, Wq, bq)
        K = proj(k, Wk, bk)
        V = proj(v, Wv, bv)
        scores = jnp.einsum('bhqd,bhkd->bhqk', Q, K) / jnp.sqrt(jnp.float32(dk))
        attn = jax.nn.softmax(scores, axis=-1)
        out = jnp.einsum('bhqk,bhkd->bhqd', attn, V)
        concat = out.transpose(0, 2, 1, 3).reshape(B, S, D)
        return concat @ Wo.T + bo

    def _L1_ffn_ref(x, W1, b1, W2, b2, Wr, br):
        import jax, jax.numpy as jnp
        import numpy as np
        B, S, D, F, E = (2, 256, 256, 512, 8)
        router_logits = jnp.einsum('bsd,de->bse', x, Wr) + br
        expert_idx = jnp.argmax(router_logits, axis=-1)
        h = jax.nn.relu(jnp.einsum('bsd,edf->ebsf', x, W1) + b1[:, None, None, :])
        y = jnp.einsum('ebsf,efd->ebsd', h, W2) + b2[:, None, None, :]
        onehot = jax.nn.one_hot(expert_idx, E, dtype=x.dtype)
        out = jnp.einsum('ebsd,bse->bsd', y, onehot)
        return out
    x = x + _L0_xattn_ref(_layernorm(x, axis=-1), ctx_1024, ctx_1024)
    x = x + _L0_ffn_ref(_layernorm(x, axis=-1), L0_ffn_w_gate, L0_ffn_w_up, L0_ffn_w_down)
    x = x + _L1_xattn_ref(_layernorm(x, axis=-1), ctx_1024, ctx_1024, L1_xattn_Wq, L1_xattn_bq, L1_xattn_Wk, L1_xattn_bk, L1_xattn_Wv, L1_xattn_bv, L1_xattn_Wo, L1_xattn_bo, 0)
    x = x + _L1_ffn_ref(_layernorm(x, axis=-1), L1_ffn_W1, L1_ffn_b1, L1_ffn_W2, L1_ffn_b2, L1_ffn_Wr, L1_ffn_br)
    return x

_drawn_inputs = setup_inputs


def setup_inputs(seed=0):
    import zlib

    import numpy as np

    out = dict(_drawn_inputs(seed))
    spreads = {'L1_xattn_bq': (0.0, 0.345),
     'L1_xattn_bk': (0.0, 0.8),
     'L1_xattn_bv': (0.0, 0.1),
     'L1_xattn_bo': (0.0, 0.1),
     'L1_ffn_b1': (0.0, 0.353),
     'L1_ffn_b2': (0.0, 0.1),
     'L1_ffn_br': (0.0, 0.1)}
    factors = {}
    for name, (base, spread) in spreads.items():
        noise = np.random.default_rng([zlib.crc32(name.encode()), seed]).standard_normal(out[name].shape)
        drawn = base * np.exp(spread * noise) if base else spread * noise
        out[name] = jnp.asarray(drawn.astype(out[name].dtype))
    for name, factor in factors.items():
        out[name] = (out[name] * factor).astype(out[name].dtype)
    return out
```

```python
from contextlib import ExitStack

import concourse.bass as bass
from concourse import mybir

F32 = mybir.dt.float32
BF16 = mybir.dt.bfloat16
I32 = mybir.dt.int32
ALU = mybir.AluOpType
ACT = mybir.ActivationFunctionType
AX = mybir.AxisListType
RED = bass.bass_isa.ReduceOp
ds = bass.ds

P = 128
EPS = 1e-5
MASKED = -1e18


class Count:

    def __init__(self, eng, sem):
        self.eng, self.sem, self.base, self.n = eng, sem, 0, 0

    def mark(self, ins):
        ins.then_inc(self.sem, 1)
        self.n += 1

    def wait(self):
        self.eng.wait_ge(self.sem, self.base + self.n)

    def enter(self, i, first, per):
        self.start = self.base + self.n
        self.base, self.n, self.per = self.start + (i - first) * per, 0, per

    def leave(self, times):
        assert self.n == self.per, self.n
        self.base, self.n = self.start + times * self.per, 0


def wait(eng, sem, value):
    if isinstance(value, int) and value <= 0:
        return
    eng.wait_ge(sem, value)


def build(nc, A, out, stop=9):
    x, ctx_in = A["x"], A["ctx_1024"]
    B, S, D = x.shape
    T = B * S // P
    N = B * S
    H, HD = 16, D // 16
    KD = D // P
    F0 = A["L0_ffn_w_gate"].shape[0]
    KF = F0 // P
    QB = 32
    CH = 512
    NCH = N // CH
    UNITS = NCH * KF
    MAGIC = 1.5 * 2.0 ** 23
    QMAX = 32767.0

    es = ExitStack()
    with es:
        def sb(name, shape, dt=F32):
            return es.enter_context(nc.sbuf_tensor(name, shape, dt))

        def sem(name):
            return es.enter_context(nc.semaphore(name))

        x_dram = x.rearrange("b (h p) d -> p (b h) d", p=P)
        out_dram = out.rearrange("b (h p) d -> p (b h) d", p=P)
        ctx_dram = ctx_in.rearrange("b (h p) d -> p (b h) d", p=P)

        PS = es.enter_context(nc.psum_tensor("PS", [P, 8, 512], F32))
        X = sb("X", [P, T, D])
        ident = sb("ident", [P, P])
        identb = sb("identb", [P, P], BF16)
        causal = sb("causal", [P, H * H])
        magic = sb("magic", [P, 1])
        stats = sb("stats", [P, T, 6])
        mean = sb("mean", [P, T])
        var = sb("var", [P, T])
        rstd = sb("rstd", [P, T])
        tmp = sb("tmp", [P, T])
        z = [sb(f"z{i}", [P, D]) for i in range(2)]
        wspace = sb("wspace", [P, 3 * KD * F0])
        gateT = wspace[:, 0:KD * F0].rearrange("p (i f) -> p i f", i=KD)
        upT = wspace[:, KD * F0:2 * KD * F0].rearrange("p (i f) -> p i f", i=KD)
        downT = wspace[:, 2 * KD * F0:3 * KD * F0].rearrange("p (f o) -> p f o", f=KF)
        attnT = sb("attnT", [P, 4, KD, D])
        zT = sb("zT", [P, KD, N])
        amax = sb("amax", [P, 4, 64])
        gmax = sb("gmax", [P, 4])
        gall = sb("gall", [P, 4])
        qs = sb("qs", [P, 16])
        arena = sb("arena", [P, 2 * KF * N])
        U = arena[:, 0:KF * N].rearrange("p (f n) -> p f n", f=KF)
        G = arena[:, KF * N:2 * KF * N].rearrange("p (f n) -> p f n", f=KF)

        s_const = sem("s_const")
        s_gp = sem("s_gp")
        x_in = sem("x_in")
        c_in = sem("c_in")
        w_in = sem("w_in")
        wa_in = sem("wa_in")
        dve_step = sem("dve_step")
        var_ready = sem("var_ready")
        sd_ready = sem("sd_ready")
        block = es.enter_context(nc.Block())

        def apart(eng):
            eng.nop(nofuse=True)

        QR = 4
        NB = H // QR
        C = arena[:, 0:T * D].rearrange("p (t d) -> p t d", t=T)
        a0 = T * D
        prod = []
        for b in range(NB):
            n = QR * QR * (b + 1) * HD
            prod.append(arena[:, a0:a0 + n].rearrange("p (q k d) -> p q k d", q=QR, d=HD))
            a0 += n
        prod2 = []
        for b in range(NB):
            n = QR * QR * (b + 1) * HD
            prod2.append(arena[:, a0:a0 + n].rearrange("p (q d k) -> p q d k", q=QR, d=HD))
            a0 += n
        raw = arena[:, a0:a0 + 3 * KD * F0].rearrange("p (g w) -> p g w", w=QB)
        rawg = arena[:, a0:a0 + KD * F0].rearrange("p (f i) -> p f i", f=KF)
        rawu = arena[:, a0 + KD * F0:a0 + 2 * KD * F0].rearrange("p (f i) -> p f i", f=KF)
        rawd = arena[:, a0 + 2 * KD * F0:a0 + 3 * KD * F0].rearrange("p (o i) -> p o i", o=KD)
        NQ = 3 * KD * F0 // QB
        a0 += 3 * KD * F0
        rawa = arena[:, a0:a0 + 4 * KD * D].rearrange("p (w o i) -> p w o i", w=4, o=KD)
        a0 += 4 * KD * D
        wscale = arena[:, a0:a0 + NQ]
        winv = arena[:, a0 + NQ:a0 + 2 * NQ]
        a0 += 2 * NQ
        assert a0 <= 2 * KF * N
        sraw = sb("sraw", [P, H, H])
        sm = sb("sm", [P, H, H])
        pr = sb("pr", [P, H, H])
        rmax = sb("rmax", [P, H])
        rsum = sb("rsum", [P, H])
        rinv = sb("rinv", [P, H])
        ov = sb("ov", [P, H, HD])
        pre_ready = sem("pre_ready")
        exp_ready = sem("exp_ready")
        p_ready = sem("p_ready")
        pv_used = sem("pv_used")
        pv_pool = sem("pv_pool")
        x1_done = sem("x1_done")
        stored = sem("stored")
        w_ready = sem("w_ready")
        wt_done = sem("wt_done")
        wt_copied = sem("wt_copied")

        z_ready = sem("z_ready")
        zt_done = sem("zt_done")
        zt_copied = sem("zt_copied")
        amax_ready = sem("amax_ready")
        gall_ready = sem("gall_ready")
        scale_ready = sem("scale_ready")
        xm_ready = sem("xm_ready")
        xq_ready = sem("xq_ready")
        mm_done = sem("mm_done")
        mm_copied = sem("mm_copied")
        mm_maxed = sem("mm_maxed")
        gm_ready = sem("gm_ready")
        gk_ready = sem("gk_ready")
        sig_ready = sem("sig_ready")
        n_ready = sem("n_ready")
        g2_ready = sem("g2_ready")
        pm_ready = sem("pm_ready")
        o_ready = sem("o_ready")
        om_ready = sem("om_ready")
        ok_ready = sem("ok_ready")
        down_done = sem("down_done")
        x2_done = sem("x2_done")
        sig = sb("sig", [P, 4, CH])
        om = [sb(f"om{i}", [P, KF, P]) for i in range(2)]
        ok = [sb(f"ok{i}", [P, KF, P]) for i in range(2)]

        HP = S // P
        NP6 = 6 * HD
        QPOS = {"high": (0, 3, 2), "mid": (3, 2, 2), "low": (1, 1, 1)}
        KPOS = {"high": (1, 3, 1), "mid": (0, 2, 5), "low": (4, 1, 1)}
        stackT = [[arena[0:NP6, 2048 * (2 * par + w):2048 * (2 * par + w) + 2048].bitcast(BF16)
                   .rearrange("p (h n) -> p h n", h=H) for w in range(2)] for par in range(2)]
        zTb = zT[:, 0, 0:KD * S].rearrange("p (k n) -> p k n", k=KD)
        cTb = zT[:, 0, KD * S:2 * KD * S].rearrange("p (k n) -> p k n", k=KD)
        zflat = zT[:].rearrange("p k n -> p (k n)")
        stack = zflat[:, 1024:1024 + 3072].bitcast(BF16).rearrange("p (w j c d) -> p w j c d", w=2, c=6, d=HD)
        qkf = wspace[:, 0:1024].rearrange("p (w h d) -> p w h d", w=2, h=HP)
        rest = wspace[:, 1024:2048]
        VW = HD + 1
        V = [wspace[:, 2048 + 544 * par:2048 + 544 * par + 544].rearrange("p (k h v) -> p k h v", k=HP, v=VW)
             for par in range(2)]
        PT = [sig[:].rearrange("p a b -> p (a b)")[:, 512 * k:512 * k + 512].rearrange("p (k n) -> p k n", k=HP)
              for k in range(2)]
        negT = sig[:].rearrange("p a b -> p (a b)")[0:96, 1024:1152].bitcast(BF16)
        zz = wspace[:, 3136:3648].rearrange("p (h d) -> p h d", h=HP)
        ct = [wspace[:, 3648:4160].rearrange("p (h d) -> p h d", h=HP),
              om[0][:].rearrange("p a b -> p (a b)")[:, 0:512].rearrange("p (h d) -> p h d", h=HP)]
        on = om[1][:].rearrange("p a b -> p (a b)")[:, 0:512].rearrange("p (h d) -> p h d", h=HP)
        oT = ok[0][:].rearrange("p a b -> p (a b)")[:, 0:512].rearrange("p (k n) -> p k n", k=KD)
        yo = ok[1][:].rearrange("p a b -> p (a b)")[:, 0:512].rearrange("p (h d) -> p h d", h=HP)
        select_row = sb("select_row", [96, H, P], BF16)
        bqk = sb("bqk", [P, 2, D])
        bvo = sb("bvo", [P, 2, D])
        negm = sb("negm", [P, HP, H])
        nrest = sb("nrest", [P, HP, H])
        nst = sb("nst", [P, HP, 96], BF16)
        den = sb("den", [P, HP, H])
        b_in = sem("b_in")
        ct_in = [sem(f"ct_in{k}") for k in range(2)]
        init_ready = sem("init_ready")
        zz_ready = sem("zz_ready")
        pe6, pe7, ev6, ev7 = sem("pe6"), sem("pe7"), sem("ev6"), sem("ev7")
        high_ready = sem("high_ready")
        rest_ready = sem("rest_ready")
        mid_ready = sem("mid_ready")
        low_ready = sem("low_ready")
        s1_done = sem("s1_done")
        max_done = sem("max_done")
        neg_ready = sem("neg_ready")
        s2_done = sem("s2_done")
        e_done = sem("e_done")
        pv_done = sem("pv_done")
        on_ready = sem("on_ready")
        x3_done = sem("x3_done")
        st_bank = [PS[:, k, :].rearrange("p (k n) -> p k n", k=HP) for k in range(2)]
        s_bank = [PS[:, 2 + k, :].rearrange("p (h n) -> p h n", h=HP) for k in range(2)]
        o_bank = PS[:, 4:6, :]
        side = [PS[:, 6 + k, :] for k in range(2)]

        def side_count(v):
            return 0 if isinstance(v, int) and v == 0 else 8 * v - 1

        def parts(w, name):
            first, n, step = (QPOS, KPOS)[w][name]
            return stack[:, w, :, first:first + step * (n - 1) + 1:step, :]

        def unit(buf, f, cc):
            return buf[:, f, ds(cc * CH, CH)]

        E, _, F1 = A["L1_ffn_W1"].shape
        K1 = F1 // P
        J = T + E - 1
        W1 = arena[:, 8192:8192 + E * KD * F1].rearrange("p (n f) -> p n f", f=F1)
        W2 = arena[:, 8192 + E * KD * F1:8192 + E * KD * F1 + E * K1 * D].rearrange("p (n d) -> p n d", d=D)
        b1B = arena[:, 0:E * F1].rearrange("p (e f) -> p e f", e=E)
        b2B = arena[:, E * F1:E * F1 + E * D].rearrange("p (e d) -> p e d", e=E)
        Z = zflat.rearrange("p (t d) -> p t d", d=D)
        Y = Z
        rows_z = nc.dram_tensor("rows_z", [J * P, D], F32, kind="Internal").ap()
        rows_y = nc.dram_tensor("rows_y", [J * P, D], F32, kind="Internal").ap()
        Wr = sb("Wr", [P, KD, E])
        brB = sb("brB", [P, E])
        zero = sb("zero", [P, D])
        before = sb("before", [P, P])
        ones = sb("ones", [P, P])
        iota_e = sb("iota_e", [P, E])
        iota_j = sb("iota_j", [P, J])
        sigf = sig[:].rearrange("p a b -> p (a b)")
        zr = [sigf[:, 256 * k:256 * k + 256].rearrange("p (k n) -> p k n", k=KD) for k in range(2)]
        lg, eq, onehot, cum_a, cum_b, place = [
            sigf[:, 512 + 128 * k:640 + 128 * k].rearrange("p (t e) -> p t e", e=E) for k in range(6)]
        over = sigf[:, 1280:1280 + J * E].rearrange("p (j e) -> p j e", e=E)
        top = sb("top", [P, T])
        first = sb("first", [P, T])
        tiles = sb("tiles", [P, 4, E])
        posf = sb("posf", [P, T])
        pos = sb("pos", [P, T], I32)
        ef = sb("ef", [P, J])
        expert = sb("expert", [P, J], I32)
        ez = [om[k][:].rearrange("p a b -> p (a b)")[:, 0:D] for k in range(2)]
        ezT = [om[k][:].rearrange("p a b -> p (a b)")[:, D:2 * D].rearrange("p (k n) -> p k n", k=KD) for k in range(2)]
        ys = [om[k][:].rearrange("p a b -> p (a b)")[:, 2 * D:3 * D] for k in range(2)]
        hn = [ok[k][:].rearrange("p a b -> p (a b)")[:, 0:F1] for k in range(2)]
        hT = [wspace[:, F1 * k:F1 * k + F1].rearrange("p (f n) -> p f n", f=K1) for k in range(2)]
        e_in = sem("e_in")
        be_in = sem("be_in")
        zero_set = sem("zero_set")
        zero_out = sem("zero_out")
        zr_ready, zrt_done, zrt_copied, lg_done = sem("zr_ready"), sem("zrt_done"), sem("zrt_copied"), sem("lg_done")
        onehot_ready, rank_done, pos_ready = sem("onehot_ready"), sem("rank_done"), sem("pos_ready")
        sent = sem("sent")
        ez_in = [sem(f"ez_in{k}") for k in range(2)]
        et_done, et_copied, h_done, h_copied = sem("et_done"), sem("et_copied"), sem("h_done"), sem("h_copied")
        ht_done, ht_copied, y_done, y_copied = sem("ht_done"), sem("ht_copied"), sem("y_done"), sem("y_copied")
        y_out = [sem(f"y_out{k}") for k in range(2)]
        back = [sem(f"back{k}") for k in range(4)]
        x4_done = sem("x4_done")

        def turned_copy(copy, par, m, k):
            return copy(stackT[par][m // 4][:, 4 * (m % 4):4 * (m % 4) + 4, :].rearrange("p h n -> p (h n)"),
                        side[k][0:NP6, :].bitcast(BF16))

        @block.gpsimd
        def _(pool):
            g = Count(pool, s_gp)
            g.mark(pool.memset(ident[:], 0.0))
            g.mark(pool.memset(causal[:], 0.0))
            g.wait()
            g.mark(pool.affine_select(out=ident[:], in_=ident[:], compare_op=ALU.not_equal, fill=1.0, base=0,
                                      pattern=[[-1, P]], channel_multiplier=1))
            cz = causal[:].rearrange("p (q k) -> p q k", q=H)
            g.mark(pool.affine_select(out=cz, in_=cz, compare_op=ALU.is_ge, fill=MASKED, base=0,
                                      pattern=[[1, H], [-1, H]], channel_multiplier=0))
            g.mark(pool.memset(magic[:], MAGIC))
            g.mark(pool.memset(select_row[:], 0.0))
            g.wait()
            for k in range(3):
                g.mark(pool.affine_select(out=select_row[:], in_=select_row[:], compare_op=ALU.not_equal, fill=1.0,
                                          base=-32 * k, pattern=[[-1, H], [0, P]], channel_multiplier=1))
                g.wait()
            pool.memset(zero[:], 0.0).then_inc(zero_set, 1)
            g.mark(pool.memset(before[:], 1.0))
            g.mark(pool.memset(ones[:], 1.0))
            g.wait()
            g.mark(pool.affine_select(out=before[:], in_=before[:], compare_op=ALU.is_ge, fill=0.0, base=-1,
                                      pattern=[[1, P]], channel_multiplier=-1))
            g.mark(pool.iota(iota_e[:], [[1, E]], base=0, channel_multiplier=0, allow_small_or_imprecise_dtypes=True))
            g.mark(pool.iota(iota_j[:], [[1, J]], base=0, channel_multiplier=0, allow_small_or_imprecise_dtypes=True))
            g.wait()
            pool.tensor_copy(identb[:], ident[:]).then_inc(s_const, 1)

            with pool.Fori(0, T) as t:
                pool.wait_ge(p_ready, t + 1)
                for b in range(2, NB):
                    nk = QR * (b + 1)
                    ins = pool.tensor_tensor(
                        prod2[b], pr[:, QR * b:QR * b + QR, 0:nk].unsqueeze(2).broadcast_to((P, QR, HD, nk)),
                        C[:, ds(t, 1), 0:HD * nk].rearrange("p a (k d) -> p a d k", d=HD).broadcast_to((P, QR, HD, nk)),
                        ALU.mult)
                ins.then_inc(pv_pool, 1)

            if stop < 2:
                return

            def all_max(k):
                pool.wait_ge(amax_ready, k + 1)
                pool.partition_all_reduce(gall[:, k:k + 1], gmax[:, k:k + 1], P, RED.absmax).then_inc(gall_ready, 1)

            for k in range(2):
                all_max(k)
            def sixteen(cc, f, u):
                pool.wait_ge(sig_ready, u + 1)
                sg = sig[:, f % 2, :]
                apart(pool)
                pool.tensor_scalar(sg, sg, 65536.0, MAGIC, ALU.mult, ALU.add).then_inc(s_gp, 1)
                pool.wait_ge(s_gp, g.n + u + 1)
                apart(pool)
                pool.tensor_scalar(sg, sg, MAGIC, 65535.0, ALU.subtract, ALU.min).then_inc(n_ready, 1)

            with pool.Fori(0, NCH) as cc:
                for f in range(KF):
                    sixteen(cc, f, cc * KF + f)
            for k in range(2, 4):
                all_max(k)
            pool.wait_ge(amax_ready, 5)
            pool.partition_all_reduce(gall[:, 0:1], gmax[:, 0:1], P, RED.absmax).then_inc(gall_ready, 1)

            if stop < 4:
                return
            pool.wait_ge(pos_ready, 1)
            pool.wait_ge(zero_out, 16)
            for t in range(T):
                pool.indirect_dma_start(rows_z, bass.IndirectOffsetOnAxis(ap=pos[:, t:t + 1], axis=0), Z[:, t, :],
                                        None).then_inc(sent, 16)
            pool.wait_ge(sent, 16 * T)
            pool.wait_ge(y_out[0], 16 * ((J + 1) // 2))
            pool.wait_ge(y_out[1], 16 * (J // 2))
            for t in range(T):
                pool.indirect_dma_start(Y[:, t, :], None, rows_y,
                                        bass.IndirectOffsetOnAxis(ap=pos[:, t:t + 1], axis=0)).then_inc(back[t // 4], 16)

        @block.sync
        def _(sp):
            for q in range(4):
                sp.dma_start(X[:, 4 * q:4 * q + 4, :], x_dram[:, 4 * q:4 * q + 4, :]).then_inc(x_in, 16)
            for q in range(4):
                sp.dma_start(C[:, 4 * q:4 * q + 4, :], ctx_dram[:, 4 * q:4 * q + 4, :]).then_inc(c_in, 16)
            sp.dma_start(rawg, A["L0_ffn_w_gate"].rearrange("(f p) i -> p f i", p=P)).then_inc(w_in, 16)
            sp.dma_start(rawu, A["L0_ffn_w_up"].rearrange("(f p) i -> p f i", p=P)).then_inc(w_in, 16)
            sp.dma_start(rawd, A["L0_ffn_w_down"].rearrange("(o p) i -> p o i", p=P)).then_inc(w_in, 16)
            for k, name in enumerate(("Wq", "Wk", "Wv", "Wo")):
                sp.dma_start(rawa[:, k], A["L1_xattn_" + name].rearrange("(o p) i -> p o i", p=P)).then_inc(wa_in, 16)

            for k, name in enumerate(("bq", "bk")):
                sp.dma_start(bqk[:, k, :], A["L1_xattn_" + name].partition_broadcast(P)).then_inc(b_in, 16)
            for k, name in enumerate(("bv", "bo")):
                sp.dma_start(bvo[:, k, :], A["L1_xattn_" + name].partition_broadcast(P)).then_inc(b_in, 16)

            sp.dma_start(Wr[:], A["L1_ffn_Wr"].rearrange("(k p) e -> p k e", p=P)).then_inc(b_in, 16)
            sp.dma_start(brB[:], A["L1_ffn_br"].partition_broadcast(P)).then_inc(b_in, 16)
            sp.wait_ge(zero_set, 1)
            sp.dma_start(rows_z.rearrange("(j p) d -> p j d", p=P), zero[:].unsqueeze(1).broadcast_to((P, J, D)))\
              .then_inc(zero_out, 16)

            if stop > 2:
                def load_ctx(b, par):
                    if not (isinstance(b, int) and b < 2):
                        sp.wait_ge(pe7, side_count(b - 2) + 1)
                    sp.dma_start(ct[par], ctx_dram[:, ds(HP * b, HP), :]).then_inc(ct_in[par], 16)

                sp.wait_ge(x2_done, T)
                load_ctx(0, 0)
                load_ctx(1, 1)
                w1_dram = A["L1_ffn_W1"].rearrange("e (k p) f -> p (e k) f", p=P)
                w2_dram = A["L1_ffn_W2"].rearrange("e (k p) d -> p (e k) d", p=P)
                if stop > 3:
                    sp.dma_start(W1, w1_dram).then_inc(e_in, 16)
                    sp.dma_start(W2, w2_dram).then_inc(e_in, 16)
                sp.wait_ge(pe7, 1)
                load_ctx(2, 0)
                load_ctx(3, 1)
                with sp.Fori(2, B // 2) as i:
                    load_ctx(2 * i, 0)
                    load_ctx(2 * i + 1, 1)

            if stop >= 4:
                sp.wait_ge(e_done, H * B)
                sp.dma_start(b1B.rearrange("p e f -> p (e f)"),
                             A["L1_ffn_b1"].rearrange("e f -> (e f)").partition_broadcast(P)).then_inc(be_in, 16)
                sp.dma_start(b2B.rearrange("p e d -> p (e d)"),
                             A["L1_ffn_b2"].rearrange("e d -> (e d)").partition_broadcast(P)).then_inc(be_in, 16)

                def fetch(j, i, par):
                    wait(sp, et_done, j - 1)
                    sp.dma_start(ez[par], rows_z[ds(j * P, P), :]).then_inc(ez_in[par], 16)

                def store(j, par):
                    sp.wait_ge(y_copied, j + 1)
                    sp.dma_start(rows_y[ds(j * P, P), :], ys[par]).then_inc(y_out[par], 16)

                sp.wait_ge(sent, 16 * T)
                for j in range(3):
                    fetch(j, 0, j % 2)
                store(0, 0)
                with sp.Fori(1, J // 2) as i:
                    fetch(2 * i + 1, i, 1)
                    store(2 * i - 1, 1)
                    fetch(2 * i + 2, i, 0)
                    store(2 * i, 0)
                store(J - 2, 1)
                store(J - 1, 0)
                for q in range(4):
                    sp.wait_ge(x4_done, q + 1)
                    sp.dma_start(out_dram[:, 4 * q:4 * q + 4, :], X[:, 4 * q:4 * q + 4, :]).then_inc(stored, 16)
                sp.wait_ge(stored, 64)

            if stop < 4:
                if stop < 3:
                    sp.wait_ge(x1_done if stop == 1 else x2_done, T)
                else:
                    sp.wait_ge(x3_done, B)
                sp.dma_start(out_dram, X[:]).then_inc(stored, 16)
                sp.wait_ge(stored, 16)

        TW = [(attnT[:, w, i, P * o:P * o + P], rawa[:, w, o, P * i:P * i + P])
              for w in range(4) for i in range(KD) for o in range(KD)]
        NA = len(TW) // 4
        for dst, src in ((gateT, rawg), (upT, rawu)):
            TW += [(dst[:, i, P * f:P * f + P], src[:, f, P * i:P * i + P]) for i in range(KD) for f in range(KF)]
        TW += [(downT[:, f, P * o:P * o + P], rawd[:, o, P * f:P * f + P]) for f in range(KF) for o in range(KD)]
        NW = len(TW) // 4
        flat = {0: attnT[:].rearrange("p w i o -> p (w i o)"), NA * 512: gateT.rearrange("p i f -> p (i f)"),
                NA * 512 + KD * F0: upT.rearrange("p i f -> p (i f)"),
                NA * 512 + 2 * KD * F0: downT.rearrange("p f o -> p (f o)")}

        def weight_group(n):
            start = max(s for s in flat if s <= 512 * n)
            return flat[start][:, 512 * n - start:512 * n - start + 512]

        @block.scalar
        def _(act):
            act.wait_ge(var_ready, 1)
            act.activation(rstd[:], var[:], ACT.Sqrt).then_inc(sd_ready, 1)
            for n in range(NA):
                act.wait_ge(wt_done, n + 1)
                act.copy(weight_group(n), PS[:, n % 8, :]).then_inc(wt_copied, 1)

            def exp(t):
                act.wait_ge(pre_ready, t + 1)
                act.activation(sm[:], sm[:], ACT.Exp).then_inc(exp_ready, 1)

            with act.Fori(0, T) as t:
                exp(t)
            for n in range(NA, NW):
                act.wait_ge(wt_done, n + 1)
                act.copy(weight_group(n), PS[:, n % 8, :]).then_inc(wt_copied, 1)
            if stop < 2:
                return

            act.wait_ge(var_ready, 2)
            act.activation(rstd[:], var[:], ACT.Sqrt).then_inc(sd_ready, 1)
            with act.Fori(0, T // 4) as i:
                for h in range(2):
                    act.wait_ge(zt_done, 2 * i + h + 1)
                    act.copy(zT[:, :, ds((2 * i + h) * 2 * P, 2 * P)],
                             PS[:, h, :].rearrange("p (k n) -> p k n", k=KD)).then_inc(zt_copied, 1)
            act.wait_ge(scale_ready, 1)
            act.wait_ge(zt_copied, T // 2)
            for cc in range(NCH):
                v = zT[:, :, cc * CH:cc * CH + CH]
                act.activation(v, v, ACT.Identity, bias=magic[:], scale=qs[:, 1:2]).then_inc(xm_ready, 1)

            def evacuate(buf, u, cc, f):
                act.wait_ge(mm_done, u + 1)
                apart(act)
                act.activation(unit(buf, f, cc), PS[:, f, :], ACT.Copy, scale=qs[:, 0:1]).then_inc(mm_copied, 1)

            with act.Fori(0, NCH) as cc:
                for f in range(KF):
                    evacuate(G, cc * KF + f, cc, f)
            act.wait_ge(scale_ready, 2)
            act.wait_ge(mm_copied, UNITS)

            def gate_part(cc, f, u):
                v = unit(G, f, cc)
                act.activation(v, v, ACT.Identity, bias=magic[:], scale=qs[:, 3:4]).then_inc(gm_ready, 1)

            def sigmoid(cc, f, u):
                act.wait_ge(gk_ready, u + 1)
                wait(act, g2_ready, u - 1)
                apart(act)
                act.activation(sig[:, f % 2, :], unit(G, f, cc), ACT.Sigmoid, scale=qs[:, 2:3]).then_inc(sig_ready, 1)

            def up_step(cc, f, u, before=True):
                evacuate(U, UNITS + u, cc, f)
                gate_part(cc, f, u)
                if before:
                    sigmoid(cc if f else cc - 1, (f - 1) % KF, u - 1)

            for f in range(KF):
                up_step(0, f, f, before=f > 0)
            with act.Fori(1, NCH) as cc:
                for f in range(KF):
                    up_step(cc, f, cc * KF + f)
            sigmoid(NCH - 1, KF - 1, UNITS - 1)

            act.wait_ge(scale_ready, 4)
            act.wait_ge(mm_copied, 2 * UNITS)
            with act.Fori(0, NCH) as cc:
                for f in range(KF):
                    v = unit(U, f, cc)
                    act.activation(v, v, ACT.Identity, bias=magic[:], scale=qs[:, 5:6]).then_inc(pm_ready, 1)
                    v = unit(G, f, cc)
                    act.activation(v, v, ACT.Identity, bias=magic[:], scale=qs[:, 7:8]).then_inc(pm_ready, 1)
            act.wait_ge(scale_ready, 5)

            def product(i, par):
                t = 2 * i + par
                wait(act, ok_ready, t - 1)
                apart(act)
                act.activation(om[par][:], G[:, :, ds(t * P, P)], ACT.Identity, bias=magic[:],
                               scale=qs[:, 9:10]).then_inc(om_ready, 1)

            product(0, 0)
            product(0, 1)
            with act.Fori(1, T // 2) as i:
                product(i, 0)
                product(i, 1)

            if stop < 3:
                return

            act.wait_ge(var_ready, 3)
            act.activation(rstd[:], var[:], ACT.Sqrt).then_inc(sd_ready, 1)

            def prepare(v, par):
                n = side_count(v)
                act.wait_ge(pe6, n + 1)
                act.copy(zTb, side[0].rearrange("p (k n) -> p k n", k=KD)).then_inc(ev6, 1)
                act.wait_ge(pe7, n + 1)
                act.copy(cTb, side[1].rearrange("p (k n) -> p k n", k=KD)).then_inc(ev7, 1)
                act.wait_ge(ev6, n + 2)
                act.wait_ge(ev7, n + 2)
                for w in range(2):
                    act.copy(parts(w, "high"), qkf[:, w].rearrange("p h (j d) -> p (h j) d", d=HD).unsqueeze(2)
                             .broadcast_to((P, HP * H, 3, HD))).then_inc(high_ready, 1)
                act.wait_ge(rest_ready, v + 1)
                for w in range(2):
                    act.copy(parts(w, "mid"), rest[:, 512 * w:512 * w + 512].rearrange("p (j d) -> p j d", d=HD)
                             .unsqueeze(2).broadcast_to((P, HP * H, 2, HD))).then_inc(mid_ready, 1)
                for m in range(4):
                    act.wait_ge(pe7, n + 3 + m)
                    turned_copy(act.copy, par, 2 * m, 1).then_inc(ev7, 1)

            def exps(b):
                def one(h, hb):
                    c = H * b + h
                    act.wait_ge(s2_done, c + 1)
                    wait(act, pv_done, c - 1)
                    act.activation(PT[hb], st_bank[hb], ACT.Exp, scale=float(HD) ** -0.5).then_inc(e_done, 1)

                one(0, 0)
                one(1, 1)
                with act.Fori(1, H // 2) as hp:
                    one(2 * hp, 0)
                    one(2 * hp + 1, 1)

            def finish(v):
                act.wait_ge(pe6, side_count(v) + 8)
                act.copy(oT, side[0].rearrange("p (k n) -> p k n", k=KD)).then_inc(ev6, 1)

            def round_(v, par):
                prepare(v, par)
                exps(v - 1)
                finish(v)

            prepare(0, 0)
            round_(1, 1)
            with act.Fori(1, B // 2 - 1) as i:
                round_(2 * i, 0)
                round_(2 * i + 1, 1)
            round_(B - 2, 0)
            round_(B - 1, 1)
            exps(B - 1)
            act.wait_ge(pe6, side_count(B) + 1)
            act.copy(oT, side[0].rearrange("p (k n) -> p k n", k=KD)).then_inc(ev6, 1)
            if stop < 4:
                return

            act.wait_ge(var_ready, 4)
            act.activation(rstd[:], var[:], ACT.Sqrt).then_inc(sd_ready, 1)

            def router(t, par):
                act.wait_ge(zrt_done, t + 1)
                wait(act, lg_done, t - 1)
                act.copy(zr[par], PS[:, par, 0:D].rearrange("p (k n) -> p k n", k=KD)).then_inc(zrt_copied, 1)

            router(0, 0)
            router(1, 1)
            with act.Fori(1, T // 2) as i:
                router(2 * i, 0)
                router(2 * i + 1, 1)

            def rows(j, par):
                act.wait_ge(et_done, j + 1)
                wait(act, h_done, j - 1)
                act.copy(ezT[par], PS[:, par, 0:D].rearrange("p (k n) -> p k n", k=KD)).then_inc(et_copied, 1)

            def hidden(j, par):
                act.wait_ge(ht_done, j + 1)
                wait(act, y_done, j - 1)
                act.activation(hT[par], PS[:, 4 + par, :].rearrange("p (f n) -> p f n", f=K1), ACT.Relu)\
                   .then_inc(ht_copied, 1)

            rows(0, 0)
            rows(1, 1)
            hidden(0, 0)
            rows(2, 0)
            hidden(1, 1)
            with act.Fori(1, J // 2) as i:
                rows(2 * i + 1, 1)
                hidden(2 * i, 0)
                rows(2 * i + 2, 0)
                hidden(2 * i + 1, 1)
            hidden(J - 1, 0)

        @block.vector
        def _(dve):
            st = Count(dve, dve_step)

            def norm_stats(k):
                st.wait()
                st.mark(dve.tensor_tensor(mean[:], stats[:, :, 1], stats[:, :, 4], ALU.add))
                st.mark(dve.tensor_tensor(tmp[:], stats[:, :, 1], stats[:, :, 4], ALU.subtract))
                st.mark(dve.tensor_tensor(var[:], stats[:, :, 2], stats[:, :, 5], ALU.add))
                st.wait()
                st.mark(dve.tensor_tensor(tmp[:], tmp[:], tmp[:], ALU.mult))
                st.mark(dve.tensor_scalar(mean[:], mean[:], 0.5, None, ALU.mult))
                st.mark(dve.tensor_scalar(var[:], var[:], 1.0 / D, EPS, ALU.mult, ALU.add))
                st.wait()
                dve.scalar_tensor_tensor(out=var[:], in0=tmp[:], scalar=0.25, in1=var[:], op0=ALU.mult,
                                         op1=ALU.add).then_inc(var_ready, 1)
                dve.wait_ge(sd_ready, k)
                st.mark(dve.reciprocal(rstd[:], rstd[:]))
                st.wait()
                st.mark(dve.tensor_tensor(tmp[:], rstd[:], rstd[:], ALU.mult))
                st.wait()
                st.mark(dve.tensor_tensor(tmp[:], tmp[:], var[:], ALU.mult))
                st.wait()
                st.mark(dve.tensor_scalar(tmp[:], tmp[:], -0.5, 1.5, ALU.mult, ALU.add))
                st.wait()
                st.mark(dve.tensor_tensor(rstd[:], rstd[:], tmp[:], ALU.mult))
                st.wait()

            def normalise(t, dst):
                return dve.tensor_scalar(dst, X[:, ds(t, 1), :].rearrange("p a d -> p (a d)"), mean[:, ds(t, 1)],
                                         rstd[:, ds(t, 1)], ALU.subtract, ALU.mult)

            def x_tile(t):
                return X[:, ds(t, 1), :].rearrange("p a d -> p (a d)")

            st.mark(dve.memset(sraw[:], MASKED))
            dve.wait_ge(x_in, 64)
            for t in range(T):
                st.mark(dve.bn_stats(stats[:, t, :], X[:, t, :]))
            norm_stats(1)
            dve.wait_ge(s_const, 1)
            dve.wait_ge(c_in, 64)

            def scores(t):
                st.mark(normalise(t, z[0][:]))
                st.wait()
                zt = z[0][:].rearrange("p (q d) -> p q d", q=H)
                for b in range(NB):
                    nk = QR * (b + 1)
                    st.mark(dve.tensor_tensor(
                        prod[b], zt[:, QR * b:QR * b + QR, :].unsqueeze(2).broadcast_to((P, QR, nk, HD)),
                        C[:, ds(t, 1), 0:HD * nk].rearrange("p a (k d) -> p a k d", d=HD).broadcast_to((P, QR, nk, HD)),
                        ALU.mult))
                st.wait()
                for b in range(NB):
                    nk = QR * (b + 1)
                    st.mark(dve.tensor_reduce(sraw[:, QR * b:QR * b + QR, 0:nk], prod[b], AX.X, ALU.add))
                st.wait()
                st.mark(dve.scalar_tensor_tensor(out=sm[:].rearrange("p q k -> p (q k)"),
                                                 in0=sraw[:].rearrange("p q k -> p (q k)"), scalar=float(HD) ** -0.5,
                                                 in1=causal[:], op0=ALU.mult, op1=ALU.add))
                st.wait()
                st.mark(dve.tensor_reduce(rmax[:], sm[:], AX.X, ALU.max))
                st.wait()
                dve.tensor_tensor(sm[:], sm[:], rmax[:].unsqueeze(2).broadcast_to((P, H, H)),
                                  ALU.subtract).then_inc(pre_ready, 1)

            def finish(t):
                dve.wait_ge(pv_pool, t + 1)
                st.wait()
                for b in range(NB):
                    st.mark(dve.tensor_reduce(ov[:, QR * b:QR * b + QR, :], prod2[b], AX.X, ALU.add))
                st.wait()
                dve.tensor_tensor(x_tile(t), ov[:].rearrange("p q d -> p (q d)"), x_tile(t), ALU.add).then_inc(x1_done, 1)
                dve.wait_ge(x1_done, t + 1)
                st.mark(dve.bn_stats(stats[:, ds(t, 1), :].rearrange("p a d -> p (a d)"), x_tile(t)))

            def weights(t):
                dve.wait_ge(exp_ready, t + 1)
                st.mark(dve.tensor_reduce(rsum[:], sm[:], AX.X, ALU.add))
                st.wait()
                st.mark(dve.reciprocal(rinv[:], rsum[:]))
                st.wait()
                dve.tensor_tensor(pr[:], sm[:], rinv[:].unsqueeze(2).broadcast_to((P, H, H)), ALU.mult).then_inc(p_ready, 1)
                dve.wait_ge(p_ready, t + 1)
                for b in range(2):
                    nk = QR * (b + 1)
                    st.mark(dve.tensor_tensor(
                        prod2[b], pr[:, QR * b:QR * b + QR, 0:nk].unsqueeze(2).broadcast_to((P, QR, HD, nk)),
                        C[:, ds(t, 1), 0:HD * nk].rearrange("p a (k d) -> p a d k", d=HD).broadcast_to((P, QR, HD, nk)),
                        ALU.mult))

            scores(0)
            dve.wait_ge(w_in, 48)
            st.mark(dve.tensor_reduce(wscale, raw, AX.X, ALU.max, apply_absolute_value=True))
            st.wait()
            st.mark(dve.tensor_scalar(wscale, wscale, 1.0 / 7.0, 1e-12, ALU.mult, ALU.max))
            st.wait()
            st.mark(dve.reciprocal(winv, wscale))
            st.wait()
            wb = wscale.unsqueeze(2).broadcast_to((P, NQ, QB))
            st.mark(dve.tensor_tensor(raw, raw, winv.unsqueeze(2).broadcast_to((P, NQ, QB)), ALU.mult))
            st.wait()
            st.mark(dve.tensor_scalar(raw, raw, MAGIC, MAGIC, ALU.add, ALU.subtract))
            st.wait()
            dve.tensor_tensor(raw, raw, wb, ALU.mult).then_inc(w_ready, 1)
            weights(0)
            with dve.Fori(1, T) as t:
                st.enter(t, 1, 1 + NB + NB + 2 + NB + 1 + 2 + 2)
                scores(t)
                finish(t - 1)
                weights(t)
                st.leave(T - 1)
            finish(T - 1)
            if stop < 2:
                return

            norm_stats(2)

            def norm_part(i, j):
                t = 4 * i + j
                wait(dve, zt_done, 2 * i + (j // 2) if j % 2 == 0 else 2 * i + j // 2)
                st.mark(normalise(t, z[j % 2][:]))
                st.wait()
                dve.tensor_reduce(amax[:, 0, ds(t, 1)], z[j % 2][:], AX.X, ALU.max,
                                  apply_absolute_value=True).then_inc(z_ready, 1)

            for j in range(4):
                norm_part(0, j)
            with dve.Fori(1, T // 4) as i:
                st.enter(i, 1, 4)
                for j in range(4):
                    norm_part(i, j)
                st.leave(T // 4 - 1)
            dve.wait_ge(z_ready, T)

            def quant_scale(k, slot, n, factor=None, col=None):
                dve.tensor_reduce(gmax[:, slot:slot + 1], amax[:, slot, 0:n], AX.X, ALU.max).then_inc(amax_ready, 1)
                dve.wait_ge(gall_ready, k + 1)
                s, inv = qs[:, 2 * k:2 * k + 1], qs[:, 2 * k + 1:2 * k + 2]
                if factor is not None:
                    st.mark(dve.tensor_tensor(gall[:, slot:slot + 1], gall[:, slot:slot + 1], factor, ALU.mult))
                    st.wait()
                st.mark(dve.tensor_scalar(s, gall[:, slot:slot + 1], 1.0 / QMAX, 1e-12, ALU.mult, ALU.max))
                st.wait()
                if factor is None:
                    dve.reciprocal(inv, s).then_inc(scale_ready, 1)
                else:
                    st.mark(dve.reciprocal(inv, s))
                    st.wait()
                    dve.tensor_tensor(inv, inv, factor, ALU.mult).then_inc(scale_ready, 1)

            quant_scale(0, 0, T)
            for cc in range(NCH):
                dve.wait_ge(xm_ready, cc + 1)
                v = zT[:, :, cc * CH:cc * CH + CH]
                dve.tensor_scalar(v, v, MAGIC, None, ALU.subtract).then_inc(xq_ready, 1)

            def largest(slot, buf, u, cc, f):
                dve.wait_ge(mm_copied, u + 1)
                dve.tensor_reduce(amax[:, slot, ds(cc * KF + f, 1)], unit(buf, f, cc), AX.X, ALU.max,
                                  apply_absolute_value=True).then_inc(mm_maxed, 1)

            with dve.Fori(0, NCH) as cc:
                for f in range(KF):
                    largest(1, G, cc * KF + f, cc, f)
            dve.wait_ge(mm_maxed, UNITS)
            dve.tensor_reduce(gmax[:, 1:2], amax[:, 1, 0:UNITS], AX.X, ALU.max).then_inc(amax_ready, 1)
            dve.wait_ge(gall_ready, 2)
            st.mark(dve.tensor_scalar(qs[:, 2:3], gall[:, 1:2], 1.0 / QMAX, 1e-12, ALU.mult, ALU.max))
            st.wait()
            dve.reciprocal(qs[:, 3:4], qs[:, 2:3]).then_inc(scale_ready, 1)

            def gate_int(cc, f, u):
                dve.wait_ge(gm_ready, u + 1)
                v = unit(G, f, cc)
                dve.tensor_scalar(v, v, MAGIC, None, ALU.subtract).then_inc(gk_ready, 1)

            def gated(cc, f, u):
                dve.wait_ge(n_ready, u + 1)
                v = unit(G, f, cc)
                dve.tensor_tensor(v, v, sig[:, f % 2, :], ALU.mult).then_inc(g2_ready, 1)
                dve.wait_ge(g2_ready, u + 1)
                st.mark(dve.tensor_reduce(amax[:, 2, ds(u, 1)], v, AX.X, ALU.max, apply_absolute_value=True))

            def up_step(cc, f, u, before=True):
                largest(3, U, UNITS + u, cc, f)
                gate_int(cc, f, u)
                if before:
                    gated(cc if f > 1 else cc - 1, (f - 2) % KF, u - 2)

            for f in range(KF):
                up_step(0, f, f, before=f > 1)
            with dve.Fori(1, NCH) as cc:
                st.enter(cc, 1, KF)
                for f in range(KF):
                    up_step(cc, f, cc * KF + f)
                st.leave(NCH - 1)
            for f in (KF - 2, KF - 1):
                gated(NCH - 1, f, UNITS - KF + f)
            st.wait()
            st.mark(dve.tensor_scalar(qs[:, 11:12], qs[:, 2:3], 2.0 ** -16, None, ALU.mult))
            dve.tensor_reduce(gmax[:, 2:3], amax[:, 2, 0:UNITS], AX.X, ALU.max).then_inc(amax_ready, 1)
            dve.wait_ge(mm_maxed, 2 * UNITS)
            dve.tensor_reduce(gmax[:, 3:4], amax[:, 3, 0:UNITS], AX.X, ALU.max).then_inc(amax_ready, 1)
            dve.wait_ge(gall_ready, 4)
            st.wait()
            st.mark(dve.tensor_tensor(gall[:, 2:3], gall[:, 2:3], qs[:, 11:12], ALU.mult))
            st.wait()
            st.mark(dve.tensor_scalar(qs[:, 6:7], gall[:, 2:3], 1.0 / QMAX, 1e-12, ALU.mult, ALU.max))
            st.mark(dve.tensor_scalar(qs[:, 4:5], gall[:, 3:4], 1.0 / QMAX, 1e-12, ALU.mult, ALU.max))
            st.wait()
            st.mark(dve.reciprocal(qs[:, 7:8], qs[:, 6:7]))
            dve.reciprocal(qs[:, 5:6], qs[:, 4:5]).then_inc(scale_ready, 1)
            st.wait()
            dve.tensor_tensor(qs[:, 7:8], qs[:, 7:8], qs[:, 11:12], ALU.mult).then_inc(scale_ready, 1)

            def join(cc, f, u):
                dve.wait_ge(pm_ready, 2 * u + 2)
                vu, vg = unit(U, f, cc), unit(G, f, cc)
                st.mark(dve.tensor_scalar(vu, vu, MAGIC, None, ALU.subtract))
                st.wait()
                st.mark(dve.scalar_tensor_tensor(out=vg, in0=vg, scalar=MAGIC, in1=vu, op0=ALU.subtract, op1=ALU.mult))
                st.wait()
                dve.tensor_reduce(amax[:, 0, ds(u, 1)], vg, AX.X, ALU.max, apply_absolute_value=True).then_inc(o_ready, 1)

            with dve.Fori(0, NCH) as cc:
                st.enter(cc, 0, 2 * KF)
                for f in range(KF):
                    join(cc, f, cc * KF + f)
                st.leave(NCH)
            st.mark(dve.tensor_tensor(qs[:, 12:13], qs[:, 4:5], qs[:, 6:7], ALU.mult))
            st.wait()
            dve.wait_ge(o_ready, UNITS)
            quant_scale(4, 0, UNITS, factor=qs[:, 12:13])

            def product_int(i, par):
                t = 2 * i + par
                dve.wait_ge(om_ready, t + 1)
                wait(dve, down_done, t - 1)
                dve.tensor_scalar(ok[par][:], om[par][:], MAGIC, None, ALU.subtract).then_inc(ok_ready, 1)

            def residual(t, par):
                dve.wait_ge(down_done, t + 1)
                dve.scalar_tensor_tensor(out=x_tile(t), in0=PS[:, 6 + par, 0:D], scalar=qs[:, 8:9], in1=x_tile(t),
                                         op0=ALU.mult, op1=ALU.add).then_inc(x2_done, 1)
                dve.wait_ge(x2_done, t + 1)
                st.mark(dve.bn_stats(stats[:, ds(t, 1), :].rearrange("p a d -> p (a d)"), x_tile(t)))

            product_int(0, 0)
            product_int(0, 1)
            residual(0, 0)
            with dve.Fori(1, T // 2) as i:
                st.enter(i, 1, 2)
                product_int(i, 0)
                residual(2 * i - 1, 1)
                product_int(i, 1)
                residual(2 * i, 0)
                st.leave(T // 2 - 1)
            residual(T - 1, 1)

            if stop < 3:
                return

            for par in range(2):
                dve.memset(V[par][:, :, :, HD:VW], 1.0).then_inc(init_ready, 1)
            dve.memset(nst[:], 0.0).then_inc(init_ready, 1)
            norm_stats(3)
            dve.wait_ge(b_in, 96)

            def zs(b):
                if not (isinstance(b, int) and b == 0):
                    dve.wait_ge(pe6, side_count(b - 1) + 1)
                for h in range(HP):
                    ins = dve.tensor_scalar(zz[:, h, :], x_tile(HP * b + h), mean[:, ds(HP * b + h, 1)],
                                            rstd[:, ds(HP * b + h, 1)], ALU.subtract, ALU.mult)
                ins.then_inc(zz_ready, 1)

            def prepare(v, par):
                n = side_count(v)
                if not (isinstance(v, int) and v == 0):
                    dve.wait_ge(high_ready, 2 * v)
                for k, (pe_s, ev_s) in enumerate(((pe6, ev6), (pe7, ev7))):
                    dve.wait_ge(pe_s, n + 2)
                    dve.tensor_tensor(qkf[:, :, k, :], side[k].rearrange("p (w d) -> p w d", w=2), bqk[:], ALU.add)\
                       .then_inc(ev_s, 1)
                dve.wait_ge(pe6, n + 3)
                if not (isinstance(v, int) and v < 2):
                    dve.wait_ge(pv_done, H * (v - 1))
                dve.tensor_tensor(V[par][:, :, :, 0:HD], side[0].rearrange("p (k h d) -> p k h d", k=HP, h=H),
                                  bvo[:, 0, :].rearrange("p (h d) -> p h d", h=H).unsqueeze(1)
                                  .broadcast_to((P, HP, H, HD)), ALU.add).then_inc(ev6, 1)
                dve.wait_ge(high_ready, 2 * v + 2)
                both = rest.rearrange("p (j d) -> p j d", d=HD)
                dve.tensor_tensor(both, qkf.rearrange("p w h (j d) -> p (w h j) d", d=HD),
                                  stack[:, :, :, 2, :].rearrange("p w j d -> p (w j) d"), ALU.subtract)\
                   .then_inc(rest_ready, 1)
                dve.wait_ge(mid_ready, 2 * v + 2)
                dve.wait_ge(rest_ready, v + 1)
                for w in range(2):
                    dve.tensor_tensor(parts(w, "low")[:, :, 0, :], both[:, 32 * w:32 * w + 32, :],
                                      stack[:, w, :, 5, :], ALU.subtract).then_inc(low_ready, 1)
                for m in range(4):
                    dve.wait_ge(pe6, n + 4 + m)
                    turned_copy(dve.tensor_copy, par, 2 * m + 1, 0).then_inc(ev6, 1)

            def maxima(v):
                def one(h, hb):
                    dve.wait_ge(s1_done, H * v + h + 1)
                    dve.tensor_reduce(negm[:, :, ds(h, 1)].rearrange("p h o -> p (h o)"), s_bank[hb], AX.X, ALU.max,
                                      negate=True).then_inc(max_done, 1)

                with dve.Fori(0, H // 2) as hp:
                    one(2 * hp, 0)
                    one(2 * hp + 1, 1)
                dve.wait_ge(max_done, H * (v + 1))
                st.mark(dve.tensor_copy(nst[:, :, 0:H], negm[:]))
                st.wait()
                st.mark(dve.tensor_tensor(nrest[:], negm[:], nst[:, :, 0:H], ALU.subtract))
                st.wait()
                st.mark(dve.tensor_copy(nst[:, :, 32:32 + H], nrest[:]))
                st.wait()
                dve.tensor_tensor(nst[:, :, 64:64 + H], nrest[:], nst[:, :, 32:32 + H], ALU.subtract)\
                   .then_inc(neg_ready, 1)
                dve.wait_ge(pe7, side_count(v) + 7)
                if not (isinstance(v, int) and v == 0):
                    dve.wait_ge(s2_done, H * v)
                dve.tensor_copy(negT, side[1][0:96, 0:P * HP // 2].bitcast(BF16)).then_inc(ev7, 1)

            def finish(v, last=False):
                b = v - 1
                dve.wait_ge(pv_done, H * v)
                st.mark(dve.reciprocal(den[:], o_heads[:, :, :, HD]))
                st.wait()
                dve.tensor_tensor(on.rearrange("p h (j d) -> p h j d", d=HD), o_heads[:, :, :, 0:HD],
                                  den[:].unsqueeze(3).broadcast_to((P, HP, H, HD)), ALU.mult).then_inc(on_ready, 1)
                n = side_count(v) + (1 if last else 8)
                dve.wait_ge(pe7, n)
                dve.tensor_tensor(yo, side[1].rearrange("p (h d) -> p h d", h=HP),
                                  bvo[:, 1:2, :].broadcast_to((P, HP, D)), ALU.add).then_inc(ev7, 1)
                dve.wait_ge(ev7, n)
                xb = X[:, ds(HP * b, HP), :]
                dve.tensor_tensor(xb, xb, yo, ALU.add).then_inc(x3_done, 1)
                dve.wait_ge(x3_done, v)
                for h in range(HP):
                    st.mark(dve.bn_stats(stats[:, ds(HP * b + h, 1), :].rearrange("p a d -> p (a d)"),
                                         x_tile(HP * b + h)))

            o_heads = o_bank[:, :, 0:H * VW].rearrange("p q (h v) -> p q h v", v=VW)

            def round_(v, par):
                prepare(v, par)
                zs(v + 1)
                maxima(v)
                finish(v)

            zs(0)
            prepare(0, 0)
            zs(1)
            maxima(0)
            round_(1, 1)
            with dve.Fori(1, B // 2 - 1) as i:
                st.enter(i, 1, 2 * (3 + 1 + HP))
                round_(2 * i, 0)
                round_(2 * i + 1, 1)
                st.leave(B // 2 - 2)
            round_(B - 2, 0)
            prepare(B - 1, 1)
            maxima(B - 1)
            finish(B - 1)
            finish(B, last=True)
            if stop < 4:
                return

            norm_stats(4)

            def router(t, par):
                wait(dve, zrt_done, t - 1)
                normalise(t, z[par][:])
                dve.tensor_scalar(Z[:, ds(t, 1), :].rearrange("p a d -> p (a d)"), x_tile(t), mean[:, ds(t, 1)],
                                  rstd[:, ds(t, 1)], ALU.subtract, ALU.mult).then_inc(zr_ready, 1)

            router(0, 0)
            router(1, 1)
            with dve.Fori(1, T // 2) as i:
                router(2 * i, 0)
                router(2 * i + 1, 1)
            dve.wait_ge(b_in, 96)
            dve.wait_ge(lg_done, T)
            st.mark(dve.tensor_tensor(lg, PS[:, 2, 0:T * E].rearrange("p (t e) -> p t e", e=E),
                                      brB[:].unsqueeze(1).broadcast_to((P, T, E)), ALU.add))
            st.wait()
            st.mark(dve.tensor_reduce(top[:], lg, AX.X, ALU.max))
            st.wait()
            st.mark(dve.tensor_tensor(eq, lg, top[:].unsqueeze(2).broadcast_to((P, T, E)), ALU.is_ge))
            st.wait()
            st.mark(dve.scalar_tensor_tensor(out=eq, in0=eq, scalar=-float(E), in1=iota_e[:].unsqueeze(1)
                                             .broadcast_to((P, T, E)), op0=ALU.mult, op1=ALU.add))
            st.wait()
            st.mark(dve.tensor_reduce(first[:], eq, AX.X, ALU.min))
            st.wait()
            st.mark(dve.tensor_scalar(first[:], first[:], float(E), None, ALU.add))
            st.wait()
            dve.tensor_tensor(onehot, iota_e[:].unsqueeze(1).broadcast_to((P, T, E)),
                              first[:].unsqueeze(2).broadcast_to((P, T, E)), ALU.is_equal).then_inc(onehot_ready, 1)
            dve.wait_ge(rank_done, 1)
            st.mark(dve.tensor_copy(cum_a, PS[:, 3, P:2 * P].rearrange("p (t e) -> p t e", e=E)))
            st.wait()
            st.mark(dve.tensor_copy(place, cum_a))
            a, b = cum_a, cum_b
            step = 1
            while step < T:
                st.mark(dve.tensor_copy(b[:, 0:step, :], a[:, 0:step, :]))
                st.mark(dve.tensor_tensor(b[:, step:T, :], a[:, step:T, :], a[:, 0:T - step, :], ALU.add))
                st.wait()
                a, b = b, a
                step *= 2
            st.mark(dve.tensor_tensor(place, a, place, ALU.subtract))
            n_tiles, n_cum, n_tmp, n_base = (tiles[:, k, :] for k in range(4))
            st.mark(dve.tensor_scalar(n_tiles, a[:, T - 1, :], 1.0 / P, (P - 1.0) / P - 0.5 + 0.5 / P, ALU.mult, ALU.add))
            st.wait()
            st.mark(dve.tensor_scalar(n_tiles, n_tiles, MAGIC, MAGIC, ALU.add, ALU.subtract))
            st.wait()
            st.mark(dve.tensor_copy(n_cum, n_tiles))
            st.wait()
            a, b = n_cum, n_tmp
            step = 1
            while step < E:
                st.mark(dve.tensor_copy(b[:, 0:step], a[:, 0:step]))
                st.mark(dve.tensor_tensor(b[:, step:E], a[:, step:E], a[:, 0:E - step], ALU.add))
                st.wait()
                a, b = b, a
                step *= 2
            st.mark(dve.tensor_tensor(n_base, a, n_tiles, ALU.subtract))
            st.mark(dve.tensor_tensor(over, a.unsqueeze(1).broadcast_to((P, J, E)),
                                      iota_j[:].unsqueeze(2).broadcast_to((P, J, E)), ALU.is_le))
            st.wait()
            st.mark(dve.tensor_scalar(n_base, n_base, float(P), None, ALU.mult))
            st.mark(dve.tensor_tensor(place, place, PS[:, 3, 0:P].rearrange("p (t e) -> p t e", e=E), ALU.add))
            st.mark(dve.tensor_reduce(ef[:], over, AX.X, ALU.add))
            st.wait()
            st.mark(dve.tensor_tensor(place, place, n_base.unsqueeze(1).broadcast_to((P, T, E)), ALU.add))
            st.mark(dve.tensor_scalar(ef[:], ef[:], E - 1.0, None, ALU.min))
            st.wait()
            st.mark(dve.tensor_tensor(place, place, onehot, ALU.mult))
            st.mark(dve.tensor_copy(expert[:], ef[:]))
            st.wait()
            st.mark(dve.tensor_reduce(posf[:], place, AX.X, ALU.add))
            st.wait()
            dve.tensor_copy(pos[:], posf[:]).then_inc(pos_ready, 1)
            dve.wait_ge(be_in, 32)

            def expert_of(j):
                return dve.value_load(expert[0:1, ds(j, 1)], min_val=0, max_val=E - 1)

            def hidden(j, par):
                e = expert_of(j)
                dve.wait_ge(h_done, j + 1)
                wait(dve, ht_done, j - 1)
                dve.tensor_tensor(hn[par], PS[:, 2 + par, :], b1B[:, ds(e, 1), :].rearrange("p a f -> p (a f)"),
                                  ALU.add).then_inc(h_copied, 1)

            def result(j, i, par):
                e = expert_of(j)
                dve.wait_ge(y_done, j + 1)
                if not (isinstance(j, int) and j < 2):
                    dve.wait_ge(y_out[par], 16 * i)
                dve.tensor_tensor(ys[par], PS[:, 6 + par, 0:D], b2B[:, ds(e, 1), :].rearrange("p a f -> p (a f)"),
                                  ALU.add).then_inc(y_copied, 1)

            hidden(0, 0)
            hidden(1, 1)
            result(0, 0, 0)
            hidden(2, 0)
            result(1, 0, 1)
            hidden(3, 1)
            result(2, 1, 0)
            with dve.Fori(2, J // 2) as i:
                hidden(2 * i, 0)
                result(2 * i - 1, i - 1, 1)
                hidden(2 * i + 1, 1)
                result(2 * i, i, 0)
            hidden(J - 1, 0)
            result(J - 2, J // 2 - 1, 1)
            result(J - 1, J // 2, 0)
            for q in range(4):
                dve.wait_ge(back[q], 64)
                xq = X[:, 4 * q:4 * q + 4, :]
                dve.tensor_tensor(xq, xq, Y[:, 4 * q:4 * q + 4, :], ALU.add).then_inc(x4_done, 1)

        @block.tensor
        def _(pe):
            pe.wait_ge(s_const, 1)
            pe.wait_ge(wa_in, 64)
            for n in range(NW):
                if n == NA:
                    pe.wait_ge(w_ready, 1)
                wait(pe, wt_copied, n - 7)
                for m in range(4):
                    ins = pe.transpose(PS[:, n % 8, P * m:P * m + P], TW[4 * n + m][1], ident[:])
                ins.then_inc(wt_done, 1)
            if stop < 2:
                return

            pe.wait_ge(wt_copied, NW)

            def turn(i, j):
                t = 4 * i + j
                pe.wait_ge(z_ready, t + 1)
                bank = PS[:, j // 2, :].rearrange("p (k h n) -> p k h n", k=KD, h=2)
                if j % 2 == 0:
                    wait(pe, zt_copied, 2 * i + j // 2 - 1)
                for k in range(KD):
                    ins = pe.transpose(bank[:, k, j % 2, :], z[j % 2][:, P * k:P * k + P], ident[:])
                if j % 2:
                    ins.then_inc(zt_done, 1)

            for j in range(4):
                turn(0, j)
            with pe.Fori(1, T // 4) as i:
                for j in range(4):
                    turn(i, j)

            def project(wT, cc, f, u):
                wait(pe, mm_copied, u - KF + 1)
                for k in range(KD):
                    ins = pe.matmul(PS[:, f, :], wT[:, k, P * f:P * f + P], zT[:, k, ds(cc * CH, CH)],
                                    start=(k == 0), stop=(k == KD - 1))
                ins.then_inc(mm_done, 1)

            pe.wait_ge(zt_copied, T // 2)
            for f in range(KF):
                pe.wait_ge(xq_ready, 1)
                project(gateT, 0, f, f)
            with pe.Fori(1, NCH) as cc:
                pe.wait_ge(xq_ready, cc + 1)
                for f in range(KF):
                    project(gateT, cc, f, cc * KF + f)
            with pe.Fori(0, NCH) as cc:
                for f in range(KF):
                    project(upT, cc, f, UNITS + cc * KF + f)

            def down(i, par):
                t = 2 * i + par
                pe.wait_ge(ok_ready, t + 1)
                wait(pe, x2_done, t - 1)
                for f in range(KF):
                    ins = pe.matmul(PS[:, 6 + par, 0:D], ok[par][:, f, :], downT[:, f, :], start=(f == 0),
                                    stop=(f == KF - 1))
                ins.then_inc(down_done, 1)

            down(0, 0)
            down(0, 1)
            with pe.Fori(1, T // 2) as i:
                down(i, 0)
                down(i, 1)
            if stop < 3:
                return

            def prepare(v, par, i):
                n = side_count(v)
                zero = isinstance(v, int) and v == 0
                pe.wait_ge(zz_ready, v + 1)
                if not zero:
                    pe.wait_ge(ev6, n)
                for k in range(KD):
                    for h in range(HP):
                        ins = pe.transpose(side[0][:, S * k + P * h:S * k + P * h + P], zz[:, h, P * k:P * k + P], ident[:])
                ins.then_inc(pe6, 1)
                pe.wait_ge(ct_in[par], 16 * (i + 1))
                if not zero:
                    pe.wait_ge(ev7, n)
                for k in range(KD):
                    for h in range(HP):
                        ins = pe.transpose(side[1][:, S * k + P * h:S * k + P * h + P], ct[par][:, h, P * k:P * k + P],
                                           ident[:])
                ins.then_inc(pe7, 1)
                pe.wait_ge(ev6, n + 1)
                pe.wait_ge(ev7, n + 1)
                for h, pe_s in ((0, pe6), (1, pe7)):
                    for w, src in ((0, zTb), (1, cTb)):
                        for k in range(KD):
                            ins = pe.matmul(side[h][:, D * w:D * w + D], src[:, k, P * h:P * h + P], attnT[:, w, k, :],
                                            start=(k == 0), stop=(k == KD - 1))
                    ins.then_inc(pe_s, 1)
                pe.wait_ge(ev6, n + 2)
                for h in range(HP):
                    for k in range(KD):
                        ins = pe.matmul(side[0][:, D * h:D * h + D], cTb[:, k, P * h:P * h + P], attnT[:, 2, k, :],
                                        start=(k == 0), stop=(k == KD - 1))
                ins.then_inc(pe6, 1)
                pe.wait_ge(mid_ready, 2 * v + 2)
                pe.wait_ge(low_ready, 2 * v + 2)
                for m in range(8):
                    k, pe_s, ev_s = (1, pe7, ev7) if m % 2 == 0 else (0, pe6, ev6)
                    pe.wait_ge(ev_s, n + (2 if m % 2 == 0 else 3) + m // 2)
                    bank = side[k][0:NP6, :].bitcast(BF16)
                    for q in range(4):
                        for h in range(HP):
                            j = h * H + 4 * (m % 4) + q
                            ins = pe.transpose(bank[:, S * q + P * h:S * q + P * h + P],
                                               stack[:, m // 4, j, :, :].rearrange("p c d -> p (c d)"), identb[:])
                    ins.then_inc(pe_s, 1)
                pe.wait_ge(ev7, n + 6)
                pe.wait_ge(ev6, n + 7)

            def first_scores(v, par, h, hb):
                c = H * v + h
                wait(pe, max_done, c - 1)
                for q in range(HP):
                    ins = pe.matmul(s_bank[hb][:, q, :], stackT[par][0][:, ds(h, 1), P * q:P * q + P].rearrange("p a n -> p (a n)"),
                                    stackT[par][1][:, ds(h, 1), :].rearrange("p a n -> p (a n)"), start=True, stop=True)
                ins.then_inc(s1_done, 1)

            def second_scores(b, par, h, hb):
                c = H * b + h
                wait(pe, e_done, c - 1)
                for k in range(HP):
                    pe.matmul(st_bank[hb][:, k, :], stackT[par][1][:, ds(h, 1), P * k:P * k + P].rearrange("p a n -> p (a n)"),
                              stackT[par][0][:, ds(h, 1), :].rearrange("p a n -> p (a n)"), start=True, stop=False)
                    ins = pe.matmul(st_bank[hb][:, k, :], select_row[:, ds(h, 1), :].rearrange("p a n -> p (a n)"), negT,
                                    start=False, stop=True)
                ins.then_inc(s2_done, 1)

            def weigh(b, par, h, hb):
                pe.wait_ge(e_done, H * b + h + 1)
                for q in range(HP):
                    for k in range(HP):
                        ins = pe.matmul(o_bank[:, q, ds(VW * h, VW)], PT[hb][:, k, P * q:P * q + P],
                                        V[par][:, k, ds(h, 1), :].rearrange("p a v -> p (a v)"), start=(k == 0),
                                        stop=(k == HP - 1))
                ins.then_inc(pv_done, 1)

            def heads(v, par, first=True, second=True):
                def one(h, hb, lag=True):
                    if second:
                        second_scores(v - 1, 1 - par, h, hb)
                    if first:
                        first_scores(v, par, h, hb)
                    if second and lag:
                        weigh(v - 1, 1 - par, h - 1, 1 - hb)

                if second:
                    wait(pe, on_ready, v - 1)
                one(0, 0, lag=False)
                one(1, 1)
                with pe.Fori(1, H // 2) as hp:
                    one(2 * hp, 0)
                    one(2 * hp + 1, 1)
                if second:
                    weigh(v - 1, 1 - par, H - 1, 1)

            def turn_maxima(v):
                n = side_count(v)
                pe.wait_ge(neg_ready, v + 1)
                pe.wait_ge(ev7, n + 6)
                bank = side[1][0:96, 0:P * HP // 2].bitcast(BF16)
                for h in range(HP):
                    ins = pe.transpose(bank[:, P * h:P * h + P], nst[:, h, :], identb[:])
                ins.then_inc(pe7, 1)

            def finish(v, last=False):
                n = side_count(v) + (0 if last else 7)
                pe.wait_ge(on_ready, v)
                pe.wait_ge(ev6, n)
                for k in range(KD):
                    for h in range(HP):
                        ins = pe.transpose(side[0][:, S * k + P * h:S * k + P * h + P], on[:, h, P * k:P * k + P], ident[:])
                ins.then_inc(pe6, 1)
                pe.wait_ge(ev6, n + 1)
                pe.wait_ge(ev7, n)
                for h in range(HP):
                    for k in range(KD):
                        ins = pe.matmul(side[1][:, D * h:D * h + D], oT[:, k, P * h:P * h + P], attnT[:, 3, k, :],
                                        start=(k == 0), stop=(k == KD - 1))
                ins.then_inc(pe7, 1)

            def round_(v, par, i):
                prepare(v, par, i)
                heads(v, par)
                turn_maxima(v)
                finish(v)

            pe.wait_ge(init_ready, 3)
            prepare(0, 0, 0)
            heads(0, 0, second=False)
            turn_maxima(0)
            round_(1, 1, 0)
            with pe.Fori(1, B // 2 - 1) as i:
                round_(2 * i, 0, i)
                round_(2 * i + 1, 1, i)
            round_(B - 2, 0, B // 2 - 1)
            round_(B - 1, 1, B // 2 - 1)
            heads(B, 0, first=False)
            finish(B, last=True)
            if stop < 4:
                return

            def turn(t, par):
                pe.wait_ge(zr_ready, t + 1)
                wait(pe, zrt_copied, t - 1)
                for k in range(KD):
                    ins = pe.transpose(PS[:, par, P * k:P * k + P], z[par][:, P * k:P * k + P], ident[:])
                ins.then_inc(zrt_done, 1)

            def logits(t, par):
                pe.wait_ge(zrt_copied, t + 1)
                for k in range(KD):
                    ins = pe.matmul(PS[:, 2, ds(E * t, E)], zr[par][:, k, :], Wr[:, k, :], start=(k == 0),
                                    stop=(k == KD - 1))
                ins.then_inc(lg_done, 1)

            pe.wait_ge(b_in, 96)
            turn(0, 0)
            turn(1, 1)
            logits(0, 0)
            with pe.Fori(1, T // 2) as i:
                turn(2 * i, 0)
                logits(2 * i - 1, 1)
                turn(2 * i + 1, 1)
                logits(2 * i, 0)
            logits(T - 1, 1)
            pe.wait_ge(onehot_ready, 1)
            oh = onehot.rearrange("p t e -> p (t e)")
            pe.matmul(PS[:, 3, 0:P], before[:], oh, start=True, stop=True)
            pe.matmul(PS[:, 3, P:2 * P], ones[:], oh, start=True, stop=True).then_inc(rank_done, 1)

            def rows(j, i, par):
                pe.wait_ge(ez_in[par], 16 * (i + 1))
                wait(pe, et_copied, j - 1)
                for k in range(KD):
                    ins = pe.transpose(PS[:, par, P * k:P * k + P], ez[par][:, P * k:P * k + P], ident[:])
                ins.then_inc(et_done, 1)

            def hidden(j, par):
                e = pe.value_load(expert[0:1, ds(j, 1)], min_val=0, max_val=E - 1)
                pe.wait_ge(et_copied, j + 1)
                wait(pe, h_copied, j - 1)
                for k in range(KD):
                    ins = pe.matmul(PS[:, 2 + par, :], ezT[par][:, k, :], W1[:, ds(e * KD + k, 1), :].rearrange("p a f -> p (a f)"),
                                    start=(k == 0), stop=(k == KD - 1))
                ins.then_inc(h_done, 1)

            def turn_hidden(j, par):
                pe.wait_ge(h_copied, j + 1)
                wait(pe, ht_copied, j - 1)
                for f in range(K1):
                    ins = pe.transpose(PS[:, 4 + par, P * f:P * f + P], hn[par][:, P * f:P * f + P], ident[:])
                ins.then_inc(ht_done, 1)

            def result(j, par):
                e = pe.value_load(expert[0:1, ds(j, 1)], min_val=0, max_val=E - 1)
                pe.wait_ge(ht_copied, j + 1)
                wait(pe, y_copied, j - 1)
                for f in range(K1):
                    ins = pe.matmul(PS[:, 6 + par, 0:D], hT[par][:, f, :], W2[:, ds(e * K1 + f, 1), :].rearrange("p a d -> p (a d)"),
                                    start=(f == 0), stop=(f == K1 - 1))
                ins.then_inc(y_done, 1)

            pe.wait_ge(e_in, 32)
            pe.wait_ge(pos_ready, 1)
            rows(0, 0, 0)
            hidden(0, 0)
            rows(1, 0, 1)
            turn_hidden(0, 0)
            hidden(1, 1)
            rows(2, 1, 0)
            result(0, 0)
            turn_hidden(1, 1)
            with pe.Fori(1, J // 2) as i:
                hidden(2 * i, 0)
                rows(2 * i + 1, i, 1)
                result(2 * i - 1, 1)
                turn_hidden(2 * i, 0)
                hidden(2 * i + 1, 1)
                rows(2 * i + 2, i + 1, 0)
                result(2 * i, 0)
                turn_hidden(2 * i + 1, 1)
            hidden(J - 1, 0)
            result(J - 2, 1)
            turn_hidden(J - 1, 0)
            result(J - 1, 0)


_INS = ['x', 'ctx_1024', 'L0_ffn_w_gate', 'L0_ffn_w_up', 'L0_ffn_w_down', 'L1_xattn_Wq', 'L1_xattn_bq', 'L1_xattn_Wk',
        'L1_xattn_bk', 'L1_xattn_Wv', 'L1_xattn_bv', 'L1_xattn_Wo', 'L1_xattn_bo', 'L1_ffn_W1', 'L1_ffn_b1',
        'L1_ffn_W2', 'L1_ffn_b2', 'L1_ffn_Wr', 'L1_ffn_br']


def kernel(**inputs):
    import numpy as _np
    import concourse.bacc as _bacc
    from concourse import mybir as _mybir
    from concourse.bass_utils import run_bass_kernel_spmd as _run

    nc = _bacc.Bacc("TRN2", target_bir_lowering=False, num_devices=1)
    arrays, args = {}, {}
    for name in _INS:
        a = _np.ascontiguousarray(inputs[name])
        arrays[f"in_{name}_dram"] = a
        args[name] = nc.dram_tensor(f"in_{name}_dram", a.shape, _mybir.dt.from_np(a.dtype), kind="ExternalInput").ap()
    out = nc.dram_tensor("out_0_dram", inputs["x"].shape, _mybir.dt.float32, kind="ExternalOutput").ap()
    build(nc, args, out, stop=STOP)
    r = _run(nc, [arrays], core_ids=[0])
    return r.results[0]["out_0_dram"]


STOP = 4
```

```python
from contextlib import ExitStack

import concourse.bass as bass
from concourse import mybir

F32 = mybir.dt.float32
BF16 = mybir.dt.bfloat16
I32 = mybir.dt.int32
ALU = mybir.AluOpType
ACT = mybir.ActivationFunctionType
AX = mybir.AxisListType
RED = bass.bass_isa.ReduceOp
ds = bass.ds

P = 128
EPS = 1e-5
MASKED = -1e18


class Count:

    def __init__(self, eng, sem):
        self.eng, self.sem, self.base, self.n = eng, sem, 0, 0

    def mark(self, ins):
        ins.then_inc(self.sem, 1)
        self.n += 1
        return self.base + self.n

    def wait(self):
        self.eng.wait_ge(self.sem, self.base + self.n)

    def enter(self, i, first, per):
        self.start = self.base + self.n
        self.base, self.n, self.per = self.start + (i - first) * per, 0, per

    def leave(self, times):
        assert self.n == self.per, self.n
        self.base, self.n = self.start + times * self.per, 0


class Steps:

    def __init__(self):
        self.base, self.n = 0, 0

    def now(self):
        return self.base + self.n

    def next(self):
        self.n += 1
        return self.now()

    def enter(self, i, per):
        self.start = self.now()
        self.base, self.n, self.per = self.start + i * per, 0, per

    def leave(self, times):
        assert self.n == self.per, self.n
        self.base, self.n = self.start + times * self.per, 0


def wait(eng, sem, value):
    if isinstance(value, int) and value <= 0:
        return
    eng.wait_ge(sem, value)


def build(nc, A, out, stop=9):
    x, ctx_in = A["x"], A["ctx_1024"]
    B, S, D = x.shape
    T = B * S // P
    N = B * S
    H, HD = 16, D // 16
    KD = D // P
    F0 = A["L0_ffn_w_gate"].shape[0]
    KF = F0 // P
    QB = 32
    CH = 512
    NCH = N // CH
    UNITS = NCH * KF
    MAGIC = 1.5 * 2.0 ** 23
    QMAX = 32767.0

    es = ExitStack()
    with es:
        def sb(name, shape, dt=F32):
            return es.enter_context(nc.sbuf_tensor(name, shape, dt))

        def sem(name):
            return es.enter_context(nc.semaphore(name))

        x_dram = x.rearrange("b (h p) d -> p (b h) d", p=P)
        out_dram = out.rearrange("b (h p) d -> p (b h) d", p=P)
        ctx_dram = ctx_in.rearrange("b (h p) d -> p (b h) d", p=P)

        PS = es.enter_context(nc.psum_tensor("PS", [P, 8, 512], F32))
        X = sb("X", [P, T, D])
        ident = sb("ident", [P, P])
        identb = sb("identb", [P, P], BF16)
        small = sb("small", [P, 5 * H * H])
        causal = small[:, 0:H * H]
        magic = sb("magic", [P, 1])
        stats = sb("stats", [P, T, 6])
        mean = sb("mean", [P, T])
        var = sb("var", [P, T])
        rstd = sb("rstd", [P, T])
        tmp = sb("tmp", [P, T])
        z = [sb(f"z{i}", [P, D]) for i in range(2)]
        wspace = sb("wspace", [P, 3 * KD * F0])
        gateT = wspace[:, 0:KD * F0].rearrange("p (i f) -> p i f", i=KD)
        upT = wspace[:, KD * F0:2 * KD * F0].rearrange("p (i f) -> p i f", i=KD)
        downT = wspace[:, 2 * KD * F0:3 * KD * F0].rearrange("p (f o) -> p f o", f=KF)
        attnT = sb("attnT", [P, 4, KD, D])
        zT = sb("zT", [P, KD, N])
        amax = sb("amax", [P, 4, 64])
        gmax = sb("gmax", [P, 4])
        gall = sb("gall", [P, 4])
        qs = sb("qs", [P, 16])
        arena = sb("arena", [P, 2 * KF * N])
        U = arena[:, 0:KF * N].rearrange("p (f n) -> p f n", f=KF)
        G = arena[:, KF * N:2 * KF * N].rearrange("p (f n) -> p f n", f=KF)

        s_const = sem("s_const")
        s_gp = sem("s_gp")
        x_in = [sem(f"x_in{q}") for q in range(4)]
        c_in = [sem(f"c_in{q}") for q in range(4)]
        w_in = sem("w_in")
        wa_in = sem("wa_in")
        dve_step = sem("dve_step")
        var_ready = sem("var_ready")
        sd_ready = sem("sd_ready")
        block = es.enter_context(nc.Block())

        def apart(eng):
            eng.nop(nofuse=True)

        QR = 4
        NB = H // QR
        PAIRS = [QR * QR * b * (b + 1) // 2 for b in range(NB + 1)]
        C = arena[:, 0:T * D].rearrange("p (t d) -> p t d", t=T)
        a0 = T * D
        prod, prod2 = [], []
        for k in range(2):
            n = HD * PAIRS[NB]
            prod.append(arena[:, a0:a0 + n].rearrange("p (d j) -> p d j", d=HD))
            a0 += n
        for k in range(2):
            prod2.append(arena[:, a0:a0 + H * D].rearrange("p (k j) -> p k j", k=H))
            a0 += H * D
        raw = arena[:, a0:a0 + 3 * KD * F0].rearrange("p (g w) -> p g w", w=QB)
        rawg = arena[:, a0:a0 + KD * F0].rearrange("p (f i) -> p f i", f=KF)
        rawu = arena[:, a0 + KD * F0:a0 + 2 * KD * F0].rearrange("p (f i) -> p f i", f=KF)
        rawd = arena[:, a0 + 2 * KD * F0:a0 + 3 * KD * F0].rearrange("p (o i) -> p o i", o=KD)
        NQ = 3 * KD * F0 // QB
        a0 += 3 * KD * F0
        rawa = arena[:, a0:a0 + 4 * KD * D].rearrange("p (w o i) -> p w o i", w=4, o=KD)
        a0 += 4 * KD * D
        wscale = arena[:, a0:a0 + NQ]
        winv = arena[:, a0 + NQ:a0 + 2 * NQ]
        a0 += 2 * NQ
        assert a0 <= 2 * KF * N
        sraw, sm = [[small[:, H * H * (1 + 2 * a + k):H * H * (2 + 2 * a + k)].rearrange("p (q k) -> p q k", q=H)
                     for k in range(2)] for a in range(2)]
        rmax = sb("rmax", [P, H])
        rsum = sb("rsum", [P, H])
        rinv = sb("rinv", [P, 2, H])
        shift = sb("shift", [P, T])
        back_ready = sem("back_ready")
        z0_done = sem("z0_done")
        prod_done = sem("prod_done")
        sum_done = sem("sum_done")
        raw_done = sem("raw_done")
        pre_ready = sem("pre_ready")
        exp_ready = sem("exp_ready")
        rinv_done = sem("rinv_done")
        p_ready = sem("p_ready")
        pool_product = sem("pool_product")
        pv_pool = sem("pv_pool")
        pv_dve = sem("pv_dve")
        total_done = sem("total_done")
        x1_done = sem("x1_done")
        s_bn = sem("s_bn")

        def valid(t):
            return not isinstance(t, int) or 0 <= t < T

        def pairs(par, b):
            return prod[par][:, :, PAIRS[b]:PAIRS[b + 1]].rearrange("p d (q k) -> p q k d", q=QR)

        def ctx_tile(t, nk):
            return C[:, ds(t, 1), 0:HD * nk].rearrange("p a (k d) -> p (a k) d", d=HD)

        def weighted(eng, t, par, blocks):
            for b in blocks:
                nk = QR * (b + 1)
                ins = eng.tensor_tensor(
                    prod2[par][:, 0:nk, QR * HD * b:QR * HD * (b + 1)].rearrange("p k (q d) -> p k q d", q=QR),
                    sm[par][:, QR * b:QR * (b + 1), 0:nk].rearrange("p q k -> p k q").unsqueeze(3)
                    .broadcast_to((P, nk, QR, HD)),
                    ctx_tile(t, nk).unsqueeze(2).broadcast_to((P, nk, QR, HD)), ALU.mult)
            return ins

        def add_pairs(eng, par, blocks):
            for b in blocks:
                v = prod2[par][:, 0:QR * (b + 1), QR * HD * b:QR * HD * (b + 1)].rearrange("p (k o) j -> p k o j", o=2)
                ins = eng.tensor_tensor(v[:, :, 0, :], v[:, :, 0, :], v[:, :, 1, :], ALU.add)
            return ins

        DVE_BLOCKS, POOL_BLOCKS = (0, 1), (2, 3)
        FILL = 4
        stored = sem("stored")
        w_ready = sem("w_ready")
        wt_done = sem("wt_done")
        wt_copied = sem("wt_copied")

        z_ready = sem("z_ready")
        zt_done = sem("zt_done")
        zt_copied = sem("zt_copied")
        amax_ready = sem("amax_ready")
        gall_ready = sem("gall_ready")
        scale_ready = sem("scale_ready")
        xm_ready = sem("xm_ready")
        xq_ready = sem("xq_ready")
        mm_done = sem("mm_done")
        mm_copied = sem("mm_copied")
        mm_maxed = sem("mm_maxed")
        gm_ready = sem("gm_ready")
        gk_ready = sem("gk_ready")
        sig_ready = sem("sig_ready")
        n_ready = sem("n_ready")
        g2_ready = sem("g2_ready")
        pm_ready = sem("pm_ready")
        j_ready = sem("j_ready")
        o_ready = sem("o_ready")
        om_ready = sem("om_ready")
        ok_ready = sem("ok_ready")
        down_done = sem("down_done")
        x2_done = sem("x2_done")
        sig = sb("sig", [P, 4, CH])
        Zall = arena[:, 0:T * D].rearrange("p (t d) -> p t d", t=T)
        pool_step = sem("pool_step")
        up_ready = sem("up_ready")
        work = sb("work", [P, 4 * KF * P])
        om, ok = [[work[:, KF * P * (2 * a + i):KF * P * (2 * a + i + 1)].rearrange("p (f n) -> p f n", f=KF)
                   for i in range(2)] for a in range(2)]
        gq = [work[:, CH * f:CH * f + CH] for f in range(KF)]

        HP = S // P
        NP6 = 6 * HD
        QPOS = {"high": (0, 3, 2), "mid": (3, 2, 2), "low": (1, 1, 1)}
        KPOS = {"high": (1, 3, 1), "mid": (0, 2, 5), "low": (4, 1, 1)}
        stackT = [[arena[0:NP6, 2048 * (2 * par + w):2048 * (2 * par + w) + 2048].bitcast(BF16)
                   .rearrange("p (h n) -> p h n", h=H) for w in range(2)] for par in range(2)]
        zTb = zT[:, 0, 0:KD * S].rearrange("p (k n) -> p k n", k=KD)
        cTb = zT[:, 0, KD * S:2 * KD * S].rearrange("p (k n) -> p k n", k=KD)
        zflat = zT[:].rearrange("p k n -> p (k n)")
        stack = zflat[:, 1024:1024 + 3072].bitcast(BF16).rearrange("p (w j c d) -> p w j c d", w=2, c=6, d=HD)
        qkf = wspace[:, 0:1024].rearrange("p (w h d) -> p w h d", w=2, h=HP)
        rest = wspace[:, 1024:2048]
        VW = 32
        V = [wspace[:, 2048 + KD * H * VW * par:2048 + KD * H * VW * (par + 1)]
             .rearrange("p (k h v) -> p k h v", k=HP, v=VW) for par in range(2)]
        sigw = sig[:].rearrange("p a b -> p (a b)")
        PT = [sigw[:, 512 * k:512 * k + 512].rearrange("p (k n) -> p k n", k=HP) for k in range(2)]
        negT = [sigw[0:96, 1024 + 128 * k:1152 + 128 * k].bitcast(BF16) for k in range(2)]
        zz = wspace[:, 4096:4608].rearrange("p (h d) -> p h d", h=HP)
        ct = [sigw[:, 1536:2048].rearrange("p (h d) -> p h d", h=HP),
              om[0].rearrange("p a b -> p (a b)")[:, 0:512].rearrange("p (h d) -> p h d", h=HP)]
        OT = small[:, 0:4 * S].rearrange("p (g n) -> p g n", g=4)
        on = om[1].rearrange("p a b -> p (a b)")[:, 0:512].rearrange("p (h d) -> p h d", h=HP)
        oT = ok[0].rearrange("p a b -> p (a b)")[:, 0:512].rearrange("p (k n) -> p k n", k=KD)
        yo = ok[1].rearrange("p a b -> p (a b)")[:, 0:512].rearrange("p (h d) -> p h d", h=HP)
        select_row = sb("select_row", [96, H, P], BF16)
        bqk = sb("bqk", [P, 2, D])
        bvo = sb("bvo", [P, 2, D])
        negm = sb("negm", [P, HP, H])
        nst = sb("nst", [P, HP, 96], BF16)
        den = sb("den", [P, HP, H])
        b_in = sem("b_in")
        ct_in = [sem(f"ct_in{k}") for k in range(2)]
        init_ready = sem("init_ready")
        zz_ready = sem("zz_ready")
        pe6, pe7, ev6, ev7 = sem("pe6"), sem("pe7"), sem("ev6"), sem("ev7")
        high_ready = sem("high_ready")
        rest_ready = sem("rest_ready")
        mid_ready = sem("mid_ready")
        low_ready = sem("low_ready")
        k_high, k_mid = sem("k_high"), sem("k_mid")
        s1_done = sem("s1_done")
        max_done = sem("max_done")
        neg_ready = sem("neg_ready")
        neg_turned = sem("neg_turned")
        negt_ready = sem("negt_ready")
        s2_done = sem("s2_done")
        e_done = sem("e_done")
        pv_done = sem("pv_done")
        ot_ready = sem("ot_ready")
        x3_done = sem("x3_done")
        st_bank = [PS[:, k, :].rearrange("p (k n) -> p k n", k=HP) for k in range(2)]
        s_bank = [PS[:, 2 + k, :].rearrange("p (h n) -> p h n", h=HP) for k in range(2)]
        side = [PS[:, 6 + k, :] for k in range(2)]

        PLAN = {1: ("turn z", "turn ctx"), 3: ("project 0", "project 1"), 5: ("back 0", "back 1"),
                7: ("turn out", "values"), 8: ("output", "parts 0"), 9: ("parts 1",),
                10: ("parts 2",), 11: ("parts 3", "parts 4"), 12: ("parts 5",), 13: ("parts 6",), 15: ("parts 7",)}
        FINISH = ("back 0", "back 1", "turn out", "output")
        FIRST = [step for h in PLAN for step in PLAN[h] if step not in FINISH]
        BANK = {"turn z": 0, "turn ctx": 1, "project 0": 0, "project 1": 1, "back 0": 0, "back 1": 1, "values": 0,
                "turn out": 1, "output": 0}
        BANK.update({f"parts {m}": 1 - m % 2 for m in range(8)})
        PER = [sum(BANK[step] == k for h in PLAN for step in PLAN[h]) for k in range(2)]
        LAG = 4
        NG = H // LAG

        def planned(h, before, after):
            return [step for step in PLAN.get(h, ()) if (before if step in FINISH else after)]

        def ctx_turned(u):
            n1 = sum(BANK[step] for step in FIRST)
            n = sum(BANK[step] for h in PLAN for step in PLAN[h])
            if isinstance(u, int) and u < 2:
                return 1 + n1 * u
            return 2 * n1 + n * (u - 2) + 1

        def o_part(h):
            return PS[VW * (h % 4):VW * (h % 4) + VW, 4 + h // 8, S * (h // 4 % 2):S * (h // 4 % 2) + S]

        def lagged(v, par, h, lag):
            return (v, par, h - lag) if h >= lag else (v - 1, 1 - par, h - lag + H)

        NEGB = s_bank[1].rearrange("p h n -> p (h n)")[0:96, 0:P * HP // 2].bitcast(BF16)

        def parts(w, name):
            first, n, step = (QPOS, KPOS)[w][name]
            return stack[:, w, :, first:first + step * (n - 1) + 1:step, :]

        def pair(buf, f, cc):
            return buf[:, 2 * f:2 * f + 2, ds(cc * CH, CH)]

        def unit(buf, f, cc):
            return buf[:, f, ds(cc * CH, CH)]

        E, _, F1 = A["L1_ffn_W1"].shape
        K1 = F1 // P
        J = T + E - 1
        W1 = arena[:, 8192:8192 + E * KD * F1].rearrange("p (n f) -> p n f", f=F1)
        W2 = arena[:, 8192 + E * KD * F1:8192 + E * KD * F1 + E * K1 * D].rearrange("p (n d) -> p n d", d=D)
        b1B = arena[:, 0:E * F1].rearrange("p (e f) -> p e f", e=E)
        b2B = arena[:, E * F1:E * F1 + E * D].rearrange("p (e d) -> p e d", e=E)
        Z = zflat.rearrange("p (t d) -> p t d", d=D)
        Y = Z
        rows_z = nc.dram_tensor("rows_z", [J * P, D], F32, kind="Internal").ap()
        rows_y = nc.dram_tensor("rows_y", [J * P, D], F32, kind="Internal").ap()
        Wr = sb("Wr", [P, KD, E])
        brB = sb("brB", [P, E])
        zero = sb("zero", [P, D])
        before = sb("before", [P, P])
        ones = sb("ones", [P, P])
        iota_e = sb("iota_e", [P, E])
        iota_j = sb("iota_j", [P, J])
        sigf = sig[:].rearrange("p a b -> p (a b)")
        zr = [sigf[:, 256 * k:256 * k + 256].rearrange("p (k n) -> p k n", k=KD) for k in range(2)]
        lg, eq, onehot, cum_a, cum_b, place = [
            sigf[:, 512 + 128 * k:640 + 128 * k].rearrange("p (t e) -> p t e", e=E) for k in range(6)]
        over = sigf[:, 1280:1280 + J * E].rearrange("p (j e) -> p j e", e=E)
        top = sb("top", [P, T])
        first = sb("first", [P, T])
        tiles = sb("tiles", [P, 4, E])
        posf = sb("posf", [P, T])
        pos = sb("pos", [P, T], I32)
        ef = sb("ef", [P, J])
        expert = sb("expert", [P, J], I32)
        ez = [om[k].rearrange("p a b -> p (a b)")[:, 0:D] for k in range(2)]
        ezT = [om[k].rearrange("p a b -> p (a b)")[:, D:2 * D].rearrange("p (k n) -> p k n", k=KD) for k in range(2)]
        ys = [om[k].rearrange("p a b -> p (a b)")[:, 2 * D:3 * D] for k in range(2)]
        hn = [ok[k].rearrange("p a b -> p (a b)")[:, 0:F1] for k in range(2)]
        hT = [wspace[:, F1 * k:F1 * k + F1].rearrange("p (f n) -> p f n", f=K1) for k in range(2)]
        e_in = sem("e_in")
        be_in = sem("be_in")
        zero_set = sem("zero_set")
        zero_out = sem("zero_out")
        zr_ready, zrt_done, zrt_copied, lg_done = sem("zr_ready"), sem("zrt_done"), sem("zrt_copied"), sem("lg_done")
        onehot_ready, rank_done, pos_ready = sem("onehot_ready"), sem("rank_done"), sem("pos_ready")
        sent = sem("sent")
        ez_in = [sem(f"ez_in{k}") for k in range(2)]
        et_done, et_copied, h_done, h_copied = sem("et_done"), sem("et_copied"), sem("h_done"), sem("h_copied")
        ht_done, ht_copied, y_done, y_copied = sem("ht_done"), sem("ht_copied"), sem("y_done"), sem("y_copied")
        y_out = [sem(f"y_out{k}") for k in range(2)]
        back = [sem(f"back{k}") for k in range(4)]
        x4_done = sem("x4_done")

        def turned_copy(copy, par, m, k):
            return copy(stackT[par][m // 4][:, 4 * (m % 4):4 * (m % 4) + 4, :].rearrange("p h n -> p (h n)"),
                        side[k][0:NP6, :].bitcast(BF16))

        @block.gpsimd
        def _(pool):
            g = Count(pool, s_gp)
            g.mark(pool.memset(ident[:], 0.0))
            g.mark(pool.memset(causal, 0.0))
            g.wait()
            g.mark(pool.affine_select(out=ident[:], in_=ident[:], compare_op=ALU.not_equal, fill=1.0, base=0,
                                      pattern=[[-1, P]], channel_multiplier=1))
            for b in range(NB):
                cz = causal[:, PAIRS[b]:PAIRS[b + 1]].rearrange("p (q k) -> p q k", q=QR)
                g.mark(pool.affine_select(out=cz, in_=cz, compare_op=ALU.is_ge, fill=MASKED, base=QR * b,
                                          pattern=[[1, QR], [-1, QR * (b + 1)]], channel_multiplier=0))
            g.mark(pool.memset(magic[:], MAGIC))
            assert NQ % T == 0
            g.mark(pool.memset(select_row[:], 0.0))
            g.wait()
            for k in range(2):
                g.mark(pool.affine_select(out=select_row[:], in_=select_row[:], compare_op=ALU.not_equal, fill=1.0,
                                          base=-32 * k, pattern=[[-1, H], [0, P]], channel_multiplier=1))
                g.wait()
            pool.memset(zero[:], 0.0).then_inc(zero_set, 1)
            g.mark(pool.memset(before[:], 1.0))
            g.mark(pool.memset(ones[:], 1.0))
            g.wait()
            g.mark(pool.affine_select(out=before[:], in_=before[:], compare_op=ALU.is_ge, fill=0.0, base=-1,
                                      pattern=[[1, P]], channel_multiplier=-1))
            g.mark(pool.iota(iota_e[:], [[1, E]], base=0, channel_multiplier=0, allow_small_or_imprecise_dtypes=True))
            g.mark(pool.iota(iota_j[:], [[1, J]], base=0, channel_multiplier=0, allow_small_or_imprecise_dtypes=True))
            g.wait()
            pool.tensor_copy(identb[:], ident[:]).then_inc(s_const, 1)

            def weight_values(t, par):
                if not valid(t):
                    return
                pool.wait_ge(rinv_done, t + 1)
                pool.tensor_tensor(sm[par], sm[par], rinv[:, par, :].unsqueeze(2).broadcast_to((P, H, H)),
                                   ALU.mult).then_inc(p_ready, 1)
                wait(pool, total_done, t - 1)
                pool.wait_ge(p_ready, t + 1)
                weighted(pool, t, par, POOL_BLOCKS).then_inc(pool_product, 1)
                pool.wait_ge(pool_product, t + 1)
                add_pairs(pool, par, POOL_BLOCKS).then_inc(pv_pool, 1)

            for t in range(2):
                weight_values(t, t % 2)
            with pool.Fori(1, T // 2) as i:
                for k in range(2):
                    weight_values(2 * i + k, k)

            if stop < 2:
                return

            def all_max(k, slot):
                pool.wait_ge(amax_ready, k + 1)
                pool.partition_all_reduce(gall[:, slot:slot + 1], gmax[:, slot:slot + 1], P,
                                          RED.absmax).then_inc(gall_ready, 1)

            all_max(0, 0)
            all_max(1, 1)

            def gate_int(cc, f, u):
                pool.wait_ge(gm_ready, u + 1)
                apart(pool)
                pool.tensor_scalar(gq[f], gq[f], -MAGIC, 1.0, ALU.add, ALU.mult).then_inc(gk_ready, 1)

            def sixteen(f, u):
                pool.wait_ge(sig_ready, u + 1)
                sg = sig[:, f % 3, :]
                apart(pool)
                pool.tensor_scalar(sg, sg, 65536.0, MAGIC, ALU.mult, ALU.add).then_inc(pool_step, 1)
                pool.wait_ge(pool_step, u + 1)
                apart(pool)
                pool.tensor_scalar(sg, sg, -MAGIC, 1.0, ALU.add, ALU.mult).then_inc(n_ready, 1)

            def up_step(cc, f, u, before=True):
                gate_int(cc, f, u)
                if before:
                    sixteen((f - 2) % KF, u - 2)

            for f in range(KF):
                up_step(0, f, f, before=f > 1)
            with pool.Fori(1, NCH) as cc:
                for f in range(KF):
                    up_step(cc, f, cc * KF + f)
            for f in (KF - 2, KF - 1):
                sixteen(f, UNITS - KF + f)
            all_max(2, 3)
            all_max(3, 2)
            pool.wait_ge(scale_ready, 3)
            for cc in range(NCH):
                for f in range(KF // 2):
                    u = cc * (KF // 2) + f
                    v = pair(U, f, cc)
                    pool.tensor_scalar(v, v, qs[:, 5:6], magic[:], ALU.mult, ALU.add).then_inc(up_ready, 1)
                    pool.wait_ge(up_ready, 2 * u + 1)
                    pool.tensor_scalar(v, v, -MAGIC, 1.0, ALU.add, ALU.mult).then_inc(up_ready, 1)
            all_max(4, 0)

            if stop < 3:
                return
            steps = Steps(), Steps()

            def key_parts(v):
                pool.wait_ge(ev6, steps[0].now())
                pool.wait_ge(ev7, steps[1].now())
                apart(pool)
                pool.tensor_copy(parts(1, "high"), qkf[:, 1].rearrange("p h (j d) -> p (h j) d", d=HD).unsqueeze(2)
                                 .broadcast_to((P, HP * H, 3, HD))).then_inc(k_high, 1)
                pool.wait_ge(rest_ready, 2 * v + 2)
                apart(pool)
                pool.tensor_copy(parts(1, "mid"), rest[:, 512:1024].rearrange("p (j d) -> p j d", d=HD)
                                 .unsqueeze(2).broadcast_to((P, HP * H, 2, HD))).then_inc(k_mid, 1)

            def round_(v, before=True, after=True):
                for h in range(H):
                    for step in planned(h, before, after):
                        steps[BANK[step]].next()
                    if after and h == 4:
                        key_parts(v + 1)

            for step in FIRST:
                steps[BANK[step]].next()
                if step == "project 1":
                    key_parts(0)
            round_(0, before=False)
            with pool.Fori(0, B // 2 - 1) as i:
                for k in range(2):
                    steps[k].enter(i, 2 * PER[k])
                round_(2 * i + 1)
                round_(2 * i + 2)
                for k in range(2):
                    steps[k].leave(B // 2 - 1)

            if stop < 4:
                return
            pool.wait_ge(pos_ready, 1)
            pool.wait_ge(zero_out, 16)
            for t in range(T):
                pool.indirect_dma_start(rows_z, bass.IndirectOffsetOnAxis(ap=pos[:, t:t + 1], axis=0), Z[:, t, :],
                                        None).then_inc(sent, 16)
            pool.wait_ge(sent, 16 * T)
            pool.wait_ge(y_out[0], 16 * ((J + 1) // 2))
            pool.wait_ge(y_out[1], 16 * (J // 2))
            for t in range(T):
                pool.indirect_dma_start(Y[:, t, :], None, rows_y,
                                        bass.IndirectOffsetOnAxis(ap=pos[:, t:t + 1], axis=0)).then_inc(back[t // 4], 16)

        @block.sync
        def _(sp):
            for q in range(4):
                sp.dma_start(X[:, 4 * q:4 * q + 4, :], x_dram[:, 4 * q:4 * q + 4, :]).then_inc(x_in[q], 16)
            for q in range(4):
                sp.dma_start(C[:, 4 * q:4 * q + 4, :], ctx_dram[:, 4 * q:4 * q + 4, :]).then_inc(c_in[q], 16)
            sp.dma_start(rawg, A["L0_ffn_w_gate"].rearrange("(f p) i -> p f i", p=P)).then_inc(w_in, 16)
            sp.dma_start(rawu, A["L0_ffn_w_up"].rearrange("(f p) i -> p f i", p=P)).then_inc(w_in, 16)
            sp.dma_start(rawd, A["L0_ffn_w_down"].rearrange("(o p) i -> p o i", p=P)).then_inc(w_in, 16)
            for k, name in enumerate(("Wq", "Wk", "Wv", "Wo")):
                sp.dma_start(rawa[:, k], A["L1_xattn_" + name].rearrange("(o p) i -> p o i", p=P)).then_inc(wa_in, 16)

            for k, name in enumerate(("bq", "bk")):
                sp.dma_start(bqk[:, k, :], A["L1_xattn_" + name].partition_broadcast(P)).then_inc(b_in, 16)
            for k, name in enumerate(("bv", "bo")):
                sp.dma_start(bvo[:, k, :], A["L1_xattn_" + name].partition_broadcast(P)).then_inc(b_in, 16)

            sp.dma_start(Wr[:], A["L1_ffn_Wr"].rearrange("(k p) e -> p k e", p=P)).then_inc(b_in, 16)
            sp.dma_start(brB[:], A["L1_ffn_br"].partition_broadcast(P)).then_inc(b_in, 16)
            sp.wait_ge(zero_set, 1)
            sp.dma_start(rows_z.rearrange("(j p) d -> p j d", p=P), zero[:].unsqueeze(1).broadcast_to((P, J, D)))\
              .then_inc(zero_out, 16)

            if stop > 2:
                def load_ctx(b, par):
                    if not (isinstance(b, int) and b < 2):
                        sp.wait_ge(pe7, ctx_turned(b - 2))
                    sp.dma_start(ct[par], ctx_dram[:, ds(HP * b, HP), :]).then_inc(ct_in[par], 16)

                sp.wait_ge(x2_done, T)
                load_ctx(0, 0)
                load_ctx(1, 1)
                w1_dram = A["L1_ffn_W1"].rearrange("e (k p) f -> p (e k) f", p=P)
                w2_dram = A["L1_ffn_W2"].rearrange("e (k p) d -> p (e k) d", p=P)
                if stop > 3:
                    sp.dma_start(W1, w1_dram).then_inc(e_in, 16)
                    sp.dma_start(W2, w2_dram).then_inc(e_in, 16)
                load_ctx(2, 0)
                load_ctx(3, 1)
                with sp.Fori(2, B // 2) as i:
                    load_ctx(2 * i, 0)
                    load_ctx(2 * i + 1, 1)

            if stop >= 4:
                sp.wait_ge(e_done, H * B)
                sp.dma_start(b1B.rearrange("p e f -> p (e f)"),
                             A["L1_ffn_b1"].rearrange("e f -> (e f)").partition_broadcast(P)).then_inc(be_in, 16)
                sp.dma_start(b2B.rearrange("p e d -> p (e d)"),
                             A["L1_ffn_b2"].rearrange("e d -> (e d)").partition_broadcast(P)).then_inc(be_in, 16)

                def fetch(j, par):
                    wait(sp, et_done, j - 1)
                    sp.dma_start(ez[par], rows_z[ds(j * P, P), :]).then_inc(ez_in[par], 16)

                sp.wait_ge(sent, 16 * T)
                fetch(0, 0)
                fetch(1, 1)
                with sp.Fori(1, J // 2) as i:
                    fetch(2 * i, 0)
                    fetch(2 * i + 1, 1)
                fetch(J - 1, 0)
                for q in range(4):
                    sp.wait_ge(x4_done, q + 1)
                    sp.dma_start(out_dram[:, 4 * q:4 * q + 4, :], X[:, 4 * q:4 * q + 4, :]).then_inc(stored, 16)
                sp.wait_ge(stored, 64)

            if stop < 4:
                if stop < 3:
                    sp.wait_ge(x1_done if stop == 1 else x2_done, T)
                else:
                    sp.wait_ge(x3_done, B)
                sp.dma_start(out_dram, X[:]).then_inc(stored, 16)
                sp.wait_ge(stored, 16)

        TW = [(attnT[:, w, i, P * o:P * o + P], rawa[:, w, o, P * i:P * i + P])
              for w in range(4) for i in range(KD) for o in range(KD)]
        NA = len(TW) // 4
        for dst, src in ((gateT, rawg), (upT, rawu)):
            TW += [(dst[:, i, P * f:P * f + P], src[:, f, P * i:P * i + P]) for i in range(KD) for f in range(KF)]
        TW += [(downT[:, f, P * o:P * o + P], rawd[:, o, P * f:P * f + P]) for f in range(KF) for o in range(KD)]
        NW = len(TW) // 4
        flat = {0: attnT[:].rearrange("p w i o -> p (w i o)"), NA * 512: gateT.rearrange("p i f -> p (i f)"),
                NA * 512 + KD * F0: upT.rearrange("p i f -> p (i f)"),
                NA * 512 + 2 * KD * F0: downT.rearrange("p f o -> p (f o)")}

        def weight_group(n):
            start = max(s for s in flat if s <= 512 * n)
            return flat[start][:, 512 * n - start:512 * n - start + 512]

        @block.scalar
        def _(act):
            act.wait_ge(var_ready, 1)
            act.activation(rstd[:], var[:], ACT.Sqrt).then_inc(sd_ready, 1)

            def z_tile(t, par):
                if not valid(t):
                    return
                wait(act, prod_done, t - 1)
                act.activation(z[par][:], X[:, ds(t, 1), :].rearrange("p a d -> p (a d)"), ACT.Identity,
                               bias=shift[:, ds(t, 1)], scale=rstd[:, ds(t, 1)]).then_inc(z0_done, 1)

            def unpack(t, par):
                if not valid(t):
                    return
                act.wait_ge(sum_done, t + 1)
                wait(act, pre_ready, t - 1)
                for b in range(NB):
                    ins = act.activation(sraw[par][:, QR * b:QR * (b + 1), 0:QR * (b + 1)],
                                         PS[:, par, PAIRS[b]:PAIRS[b + 1]].rearrange("p (q k) -> p q k", q=QR),
                                         ACT.Identity, scale=float(HD) ** -0.5)
                ins.then_inc(raw_done, 1)

            def exp(t, par):
                if valid(t):
                    act.wait_ge(pre_ready, t + 1)
                    act.activation(sm[par], sm[par], ACT.Exp).then_inc(exp_ready, 1)

            def keep(t, par):
                if valid(t):
                    act.wait_ge(total_done, t + 1)
                    act.activation(X[:, ds(t, 1), :].rearrange("p a d -> p (a d)"), PS[:, 2 + par, 0:D],
                                   ACT.Identity).then_inc(x1_done, 1)

            def step(i, k):
                unpack(i - 1, 1 - k)
                z_tile(i + 1, 1 - k)
                exp(i - 1, 1 - k)
                keep(i - 3, 1 - k)

            act.wait_ge(back_ready, 1)
            act.wait_ge(init_ready, 1)
            z_tile(0, 0)
            for i in range(FILL):
                step(i, i % 2)
            with act.Fori(FILL // 2, T // 2 - 1) as i:
                for k in range(2):
                    step(2 * i + k, k)
            def copy_weights(n):
                act.wait_ge(wt_done, n + 1)
                act.copy(weight_group(n), PS[:, 4 + n % 4, :]).then_inc(wt_copied, 1)

            for i in range(T - 2, T + 1):
                step(i, i % 2)
            for n in range(NA):
                copy_weights(n)
            for i in range(T + 1, T + FILL):
                step(i, i % 2)
            if stop < 2:
                return

            act.wait_ge(var_ready, 2)
            act.activation(rstd[:], var[:], ACT.Sqrt).then_inc(sd_ready, 1)
            for n in range(NA, NW):
                copy_weights(n)
            for h in range(T // 2):
                act.wait_ge(zt_done, h + 1)
                act.copy(zT[:, :, h * 2 * P:(h + 1) * 2 * P],
                         PS[:, h % 4, :].rearrange("p (k n) -> p k n", k=KD)).then_inc(zt_copied, 1)
            act.wait_ge(scale_ready, 1)
            act.wait_ge(zt_copied, T // 2)
            for cc in range(NCH):
                v = zT[:, :, cc * CH:cc * CH + CH]
                act.activation(v, v, ACT.Identity, bias=magic[:], scale=qs[:, 1:2]).then_inc(xm_ready, 1)

            def evacuate(buf, u, cc, f):
                act.wait_ge(mm_done, u + 1)
                apart(act)
                act.activation(unit(buf, f, cc), PS[:, f, :], ACT.Copy, scale=qs[:, 0:1]).then_inc(mm_copied, 1)

            with act.Fori(0, NCH) as cc:
                for f in range(KF):
                    evacuate(G, cc * KF + f, cc, f)
            act.wait_ge(scale_ready, 2)
            act.wait_ge(mm_copied, UNITS)

            def gate_part(cc, f, u):
                wait(act, g2_ready, u - KF + 1)
                act.activation(gq[f], unit(G, f, cc), ACT.Identity, bias=magic[:], scale=qs[:, 3:4])\
                   .then_inc(gm_ready, 1)

            def sigmoid(cc, f, u):
                act.wait_ge(gk_ready, u + 1)
                wait(act, g2_ready, u - 2)
                apart(act)
                act.activation(sig[:, f % 3, :], gq[f], ACT.Sigmoid, scale=qs[:, 2:3]).then_inc(sig_ready, 1)

            def up_step(cc, f, u, before=True):
                evacuate(U, UNITS + u, cc, f)
                gate_part(cc, f, u)
                if before:
                    sigmoid(cc if f else cc - 1, (f - 1) % KF, u - 1)

            for f in range(KF):
                up_step(0, f, f, before=f > 0)
            with act.Fori(1, NCH) as cc:
                for f in range(KF):
                    up_step(cc, f, cc * KF + f)
            sigmoid(NCH - 1, KF - 1, UNITS - 1)

            act.wait_ge(scale_ready, 4)
            act.wait_ge(mm_copied, 2 * UNITS)
            with act.Fori(0, NCH) as cc:
                for f in range(KF // 2):
                    v = pair(G, f, cc)
                    act.activation(v, v, ACT.Identity, bias=magic[:], scale=qs[:, 7:8]).then_inc(pm_ready, 1)
            act.wait_ge(scale_ready, 5)

            def product(i, par):
                t = 2 * i + par
                wait(act, ok_ready, t - 1)
                apart(act)
                act.activation(om[par], G[:, :, ds(t * P, P)], ACT.Identity, bias=magic[:],
                               scale=qs[:, 9:10]).then_inc(om_ready, 1)

            product(0, 0)
            product(0, 1)
            with act.Fori(1, T // 2) as i:
                product(i, 0)
                product(i, 1)

            if stop < 3:
                return

            act.wait_ge(var_ready, 3)
            act.activation(rstd[:], var[:], ACT.Sqrt).then_inc(sd_ready, 1)

            steps = Steps(), Steps()
            pe_side, ev_side = (pe6, pe7), (ev6, ev7)

            def side_step(step, v, par):
                k = BANK[step]
                n = steps[k].next()
                if step == "turn z":
                    act.wait_ge(pe6, n)
                    act.copy(zTb, side[0].rearrange("p (k n) -> p k n", k=KD)).then_inc(ev6, 1)
                elif step == "turn ctx":
                    act.wait_ge(pe7, n)
                    act.copy(cTb, side[1].rearrange("p (k n) -> p k n", k=KD)).then_inc(ev7, 1)
                elif step == "turn out":
                    act.wait_ge(pe7, n)
                    act.copy(oT, side[1].rearrange("p (k n) -> p k n", k=KD)).then_inc(ev7, 1)
                elif step.startswith("parts") and k == 1:
                    act.wait_ge(pe7, n)
                    turned_copy(act.copy, par, int(step[6:]), 1).then_inc(ev7, 1)

            def high_parts(h):
                act.wait_ge(ev6, steps[0].now())
                act.wait_ge(ev7, steps[1].now())
                act.copy(parts(0, "high")[:, H * h:H * (h + 1)], qkf[:, 0, h].rearrange("p (j d) -> p j d", d=HD)
                         .unsqueeze(2).broadcast_to((P, H, 3, HD))).then_inc(high_ready, 1)

            def mid_parts(v):
                act.wait_ge(rest_ready, 2 * v + 1)
                act.copy(parts(0, "mid"), rest[:, 0:512].rearrange("p (j d) -> p j d", d=HD)
                         .unsqueeze(2).broadcast_to((P, HP * H, 2, HD))).then_inc(mid_ready, 1)

            def exp(b, h):
                c = H * b + h
                act.wait_ge(s2_done, c + 1)
                wait(act, pv_done, c - 1)
                act.activation(PT[h % 2], st_bank[h % 2], ACT.Exp, scale=float(HD) ** -0.5).then_inc(e_done, 1)

            def take_half(b, half):
                act.wait_ge(pv_done, H * b + 8 * (half + 1))
                act.copy(OT[:, 2 * half:2 * half + 2, :].rearrange("p g n -> p (g n)"), PS[:, 4 + half, :])\
                   .then_inc(ot_ready, 1)

            def round_(v, par, before=True, after=True):
                for h in range(H):
                    b, _, hb = lagged(v, par, h, LAG)
                    if h >= LAG or before:
                        exp(b, hb)
                    for step in planned(h, before, after):
                        side_step(step, v + 1, 1 - par)
                    if h == 4 and before:
                        take_half(v - 1, 1)
                    if after and h in (3, 4):
                        high_parts(h - 3)
                    if after and h == 6:
                        mid_parts(v + 1)
                    if h == 12:
                        take_half(v, 0)

            for step in FIRST:
                side_step(step, 0, 0)
                if step == "project 1":
                    for h in range(HP):
                        high_parts(h)
                    mid_parts(0)
            round_(0, 0, before=False)
            with act.Fori(0, B // 2 - 1) as i:
                for k in range(2):
                    steps[k].enter(i, 2 * PER[k])
                round_(2 * i + 1, 1)
                round_(2 * i + 2, 0)
                for k in range(2):
                    steps[k].leave(B // 2 - 1)
            round_(B - 1, 1, after=False)
            for h in range(H - LAG, H):
                exp(B - 1, h)
            take_half(B - 1, 1)
            for step in FINISH:
                side_step(step, B + 1, 1)
            if stop < 4:
                return

            act.wait_ge(var_ready, 4)
            act.activation(rstd[:], var[:], ACT.Sqrt).then_inc(sd_ready, 1)

            def router(t, par):
                act.wait_ge(zrt_done, t + 1)
                wait(act, lg_done, t - 1)
                act.copy(zr[par], PS[:, par, 0:D].rearrange("p (k n) -> p k n", k=KD)).then_inc(zrt_copied, 1)

            router(0, 0)
            router(1, 1)
            with act.Fori(1, T // 2) as i:
                router(2 * i, 0)
                router(2 * i + 1, 1)

            def rows(j, par):
                act.wait_ge(et_done, j + 1)
                wait(act, h_done, j - 1)
                act.copy(ezT[par], PS[:, par, 0:D].rearrange("p (k n) -> p k n", k=KD)).then_inc(et_copied, 1)

            def hidden(j, par):
                act.wait_ge(ht_done, j + 1)
                wait(act, y_done, j - 1)
                act.activation(hT[par], PS[:, 4 + par, :].rearrange("p (f n) -> p f n", f=K1), ACT.Relu)\
                   .then_inc(ht_copied, 1)

            def store(j, par):
                act.wait_ge(y_copied, j + 1)
                act.dma_start(rows_y[ds(j * P, P), :], ys[par]).then_inc(y_out[par], 16)

            rows(0, 0)
            rows(1, 1)
            hidden(0, 0)
            rows(2, 0)
            hidden(1, 1)
            store(0, 0)
            with act.Fori(1, J // 2) as i:
                rows(2 * i + 1, 1)
                hidden(2 * i, 0)
                store(2 * i - 1, 1)
                rows(2 * i + 2, 0)
                hidden(2 * i + 1, 1)
                store(2 * i, 0)
            hidden(J - 1, 0)
            store(J - 2, 1)
            store(J - 1, 0)

        @block.vector
        def _(dve):
            st = Count(dve, dve_step)

            def norm_stats(k):
                st.wait()
                st.mark(dve.tensor_tensor(mean[:], stats[:, :, 1], stats[:, :, 4], ALU.add))
                st.mark(dve.tensor_tensor(tmp[:], stats[:, :, 1], stats[:, :, 4], ALU.subtract))
                st.mark(dve.tensor_tensor(var[:], stats[:, :, 2], stats[:, :, 5], ALU.add))
                st.wait()
                st.mark(dve.tensor_tensor(tmp[:], tmp[:], tmp[:], ALU.mult))
                st.mark(dve.tensor_scalar(mean[:], mean[:], 0.5, None, ALU.mult))
                st.mark(dve.tensor_scalar(var[:], var[:], 1.0 / D, EPS, ALU.mult, ALU.add))
                st.wait()
                dve.scalar_tensor_tensor(out=var[:], in0=tmp[:], scalar=0.25, in1=var[:], op0=ALU.mult,
                                         op1=ALU.add).then_inc(var_ready, 1)
                dve.wait_ge(sd_ready, k)
                st.mark(dve.reciprocal(rstd[:], rstd[:]))
                st.wait()
                st.mark(dve.tensor_tensor(tmp[:], rstd[:], rstd[:], ALU.mult))
                st.wait()
                st.mark(dve.tensor_tensor(tmp[:], tmp[:], var[:], ALU.mult))
                st.wait()
                st.mark(dve.tensor_scalar(tmp[:], tmp[:], -0.5, 1.5, ALU.mult, ALU.add))
                st.wait()
                st.mark(dve.tensor_tensor(rstd[:], rstd[:], tmp[:], ALU.mult))
                st.wait()

            def normalise(t, dst):
                return dve.tensor_scalar(dst, X[:, ds(t, 1), :].rearrange("p a d -> p (a d)"), mean[:, ds(t, 1)],
                                         rstd[:, ds(t, 1)], ALU.subtract, ALU.mult)

            def x_tile(t):
                return X[:, ds(t, 1), :].rearrange("p a d -> p (a d)")

            for k in range(2):
                ins = dve.memset(sraw[k], MASKED)
            ins.then_inc(init_ready, 1)
            for t in range(T):
                if t % 4 == 0:
                    dve.wait_ge(x_in[t // 4], 16)
                st.mark(dve.bn_stats(stats[:, t, :], X[:, t, :]))
            norm_stats(1)
            dve.scalar_tensor_tensor(out=shift[:], in0=mean[:], scalar=-1.0, in1=rstd[:], op0=ALU.mult,
                                     op1=ALU.mult).then_inc(back_ready, 1)
            for q in range(4):
                dve.wait_ge(c_in[q], 16)

            def products(t, par):
                if not valid(t):
                    return
                dve.wait_ge(z0_done, t + 1)
                wait(dve, sum_done, t - 1)
                zt = z[par][:].rearrange("p (q d) -> p q d", q=H)
                for b in range(NB):
                    nk = QR * (b + 1)
                    ins = dve.tensor_tensor(
                        pairs(par, b), zt[:, QR * b:QR * b + QR, :].unsqueeze(2).broadcast_to((P, QR, nk, HD)),
                        ctx_tile(t, nk).unsqueeze(1).broadcast_to((P, QR, nk, HD)), ALU.mult)
                ins.then_inc(prod_done, 1)

            def bn(t):
                if valid(t):
                    dve.wait_ge(x1_done, t + 1)
                    dve.bn_stats(stats[:, ds(t, 1), :].rearrange("p a d -> p (a d)"), x_tile(t)).then_inc(s_bn, 1)

            GC = NQ // T

            def step(i, k):
                c, t, par = i - FILL, i - 1, 1 - k
                if valid(c):
                    chunk = raw[:, ds(GC * c, GC), :]
                    ws, wi = wscale[:, ds(GC * c, GC)], winv[:, ds(GC * c, GC)]
                    w = st.mark(dve.tensor_reduce(ws, chunk, AX.X, ALU.max, apply_absolute_value=True))
                products(i, k)
                if valid(c):
                    dve.wait_ge(dve_step, w)
                    w = st.mark(dve.tensor_scalar(ws, ws, 1.0 / 7.0, 1e-12, ALU.mult, ALU.max))
                if valid(t):
                    dve.wait_ge(raw_done, t + 1)
                    m = st.mark(dve.tensor_reduce(rmax[:], sraw[par], AX.X, ALU.max))
                if valid(c):
                    dve.wait_ge(dve_step, w)
                    w = st.mark(dve.reciprocal(wi, ws))
                if valid(t):
                    dve.wait_ge(dve_step, m)
                    wait(dve, pv_pool, t - 1)
                    dve.tensor_tensor(sm[par], sraw[par], rmax[:].unsqueeze(2).broadcast_to((P, H, H)),
                                      ALU.subtract).then_inc(pre_ready, 1)
                if valid(c):
                    dve.wait_ge(dve_step, w)
                    w = st.mark(dve.tensor_tensor(chunk, chunk, wi.unsqueeze(2).broadcast_to((P, GC, QB)), ALU.mult))
                if valid(i - 2):
                    dve.wait_ge(p_ready, i - 1)
                    wait(dve, total_done, i - 3)
                    v = st.mark(weighted(dve, i - 2, k, DVE_BLOCKS))
                if valid(c):
                    dve.wait_ge(dve_step, w)
                    w = st.mark(dve.tensor_scalar(chunk, chunk, MAGIC, MAGIC, ALU.add, ALU.subtract))
                if valid(t):
                    dve.wait_ge(exp_ready, t + 1)
                    m = st.mark(dve.tensor_reduce(rsum[:], sm[par], AX.X, ALU.add))
                if valid(i - 2):
                    dve.wait_ge(dve_step, v)
                    add_pairs(dve, k, DVE_BLOCKS).then_inc(pv_dve, 1)
                if valid(c):
                    dve.wait_ge(dve_step, w)
                    dve.tensor_tensor(chunk, chunk, ws.unsqueeze(2).broadcast_to((P, GC, QB)),
                                      ALU.mult).then_inc(w_ready, 1)
                if valid(t):
                    dve.wait_ge(dve_step, m)
                    wait(dve, p_ready, t - 1)
                    dve.reciprocal(rinv[:, par, :], rsum[:]).then_inc(rinv_done, 1)
                bn(i - FILL)

            for i in range(FILL):
                step(i, i % 2)
            dve.wait_ge(w_in, 48)
            with dve.Fori(FILL // 2, T // 2 - 1) as i:
                st.enter(i, FILL // 2, 2 * 8)
                for k in range(2):
                    step(2 * i + k, k)
                st.leave(T // 2 - 1 - FILL // 2)
            for i in range(T - 2, T + FILL):
                step(i, i % 2)
            dve.wait_ge(s_bn, T)
            if stop < 2:
                return

            norm_stats(2)

            for t in range(T):
                normalise(t, Zall[:, t, :]).then_inc(z_ready, 1)
                if t % 4 == 3:
                    dve.wait_ge(z_ready, t + 1)
                    st.mark(dve.tensor_reduce(amax[:, 0, t // 4:t // 4 + 1], Zall[:, t - 3:t + 1, :], AX.XY, ALU.max,
                                              apply_absolute_value=True))
            st.wait()

            def quant_scale(k, slot, n, factor=None, col=None):
                dve.tensor_reduce(gmax[:, slot:slot + 1], amax[:, slot, 0:n], AX.X, ALU.max).then_inc(amax_ready, 1)
                dve.wait_ge(gall_ready, k + 1)
                s, inv = qs[:, 2 * k:2 * k + 1], qs[:, 2 * k + 1:2 * k + 2]
                if factor is not None:
                    st.mark(dve.tensor_tensor(gall[:, slot:slot + 1], gall[:, slot:slot + 1], factor, ALU.mult))
                    st.wait()
                st.mark(dve.tensor_scalar(s, gall[:, slot:slot + 1], 1.0 / QMAX, 1e-12, ALU.mult, ALU.max))
                st.wait()
                if factor is None:
                    dve.reciprocal(inv, s).then_inc(scale_ready, 1)
                else:
                    st.mark(dve.reciprocal(inv, s))
                    st.wait()
                    dve.tensor_tensor(inv, inv, factor, ALU.mult).then_inc(scale_ready, 1)

            quant_scale(0, 0, T // 4)
            for cc in range(NCH):
                dve.wait_ge(xm_ready, cc + 1)
                v = zT[:, :, cc * CH:cc * CH + CH]
                dve.tensor_scalar(v, v, MAGIC, None, ALU.subtract).then_inc(xq_ready, 1)

            def largest(slot, buf, u, cc, f):
                dve.wait_ge(mm_copied, u + 1)
                dve.tensor_reduce(amax[:, slot, ds(cc * KF + f, 1)], unit(buf, f, cc), AX.X, ALU.max,
                                  apply_absolute_value=True).then_inc(mm_maxed, 1)

            with dve.Fori(0, NCH) as cc:
                for f in range(KF):
                    largest(1, G, cc * KF + f, cc, f)
            dve.wait_ge(mm_maxed, UNITS)
            dve.tensor_reduce(gmax[:, 1:2], amax[:, 1, 0:UNITS], AX.X, ALU.max).then_inc(amax_ready, 1)
            dve.wait_ge(gall_ready, 2)
            st.mark(dve.tensor_scalar(qs[:, 2:3], gall[:, 1:2], 1.0 / QMAX, 1e-12, ALU.mult, ALU.max))
            st.wait()
            dve.reciprocal(qs[:, 3:4], qs[:, 2:3]).then_inc(scale_ready, 1)

            def gated(cc, f, u):
                dve.wait_ge(n_ready, u + 1)
                dve.scalar_tensor_tensor(out=unit(G, f, cc), in0=sig[:, f % 3, :], scalar=65535.0, in1=gq[f],
                                         op0=ALU.min, op1=ALU.mult).then_inc(g2_ready, 1)

            def gated_max(cc, f, u):
                dve.wait_ge(g2_ready, u + 1)
                st.mark(dve.tensor_reduce(amax[:, 2, ds(u, 1)], unit(G, f, cc), AX.X, ALU.max,
                                          apply_absolute_value=True))

            def up_step(cc, f, u, before=True):
                late = cc if f > 2 else cc - 1, (f - 3) % KF, u - 3
                if before:
                    gated(*late)
                largest(3, U, UNITS + u, cc, f)
                if before:
                    gated_max(*late)

            for f in range(KF):
                up_step(0, f, f, before=f > 2)
            with dve.Fori(1, NCH) as cc:
                st.enter(cc, 1, KF)
                for f in range(KF):
                    up_step(cc, f, cc * KF + f)
                st.leave(NCH - 1)
            dve.wait_ge(mm_maxed, 2 * UNITS)
            dve.tensor_reduce(gmax[:, 3:4], amax[:, 3, 0:UNITS], AX.X, ALU.max).then_inc(amax_ready, 1)
            for f in (KF - 3, KF - 2, KF - 1):
                gated(NCH - 1, f, UNITS - KF + f)
                gated_max(NCH - 1, f, UNITS - KF + f)
            st.wait()
            st.mark(dve.tensor_scalar(qs[:, 11:12], qs[:, 2:3], 2.0 ** -16, None, ALU.mult))
            dve.tensor_reduce(gmax[:, 2:3], amax[:, 2, 0:UNITS], AX.X, ALU.max).then_inc(amax_ready, 1)
            dve.wait_ge(gall_ready, 4)
            st.wait()
            st.mark(dve.tensor_tensor(gall[:, 2:3], gall[:, 2:3], qs[:, 11:12], ALU.mult))
            st.wait()
            st.mark(dve.tensor_scalar(qs[:, 6:7], gall[:, 2:3], 1.0 / QMAX, 1e-12, ALU.mult, ALU.max))
            st.mark(dve.tensor_scalar(qs[:, 4:5], gall[:, 3:4], 1.0 / QMAX, 1e-12, ALU.mult, ALU.max))
            st.wait()
            st.mark(dve.reciprocal(qs[:, 7:8], qs[:, 6:7]))
            dve.reciprocal(qs[:, 5:6], qs[:, 4:5]).then_inc(scale_ready, 1)
            st.wait()
            dve.tensor_tensor(qs[:, 7:8], qs[:, 7:8], qs[:, 11:12], ALU.mult).then_inc(scale_ready, 1)

            def join(cc, f, u):
                dve.wait_ge(pm_ready, u + 1)
                dve.wait_ge(up_ready, 2 * u + 2)
                vg = pair(G, f, cc)
                dve.scalar_tensor_tensor(out=vg, in0=vg, scalar=MAGIC, in1=pair(U, f, cc), op0=ALU.subtract,
                                         op1=ALU.mult).then_inc(j_ready, 1)

            def join_max(cc, f, u):
                dve.wait_ge(j_ready, u + 1)
                dve.tensor_reduce(amax[:, 0, ds(u, 1)], pair(G, f, cc), AX.XY, ALU.max,
                                  apply_absolute_value=True).then_inc(o_ready, 1)

            def joined(cc, f, first=False):
                u = cc * (KF // 2) + f
                join(cc, f, u)
                if not first:
                    join_max(cc if f else cc - 1, (f - 1) % (KF // 2), u - 1)

            for f in range(KF // 2):
                joined(0, f, first=(f == 0))
            with dve.Fori(1, NCH) as cc:
                for f in range(KF // 2):
                    joined(cc, f)
            join_max(NCH - 1, KF // 2 - 1, UNITS // 2 - 1)
            st.mark(dve.tensor_tensor(qs[:, 12:13], qs[:, 4:5], qs[:, 6:7], ALU.mult))
            st.wait()
            dve.wait_ge(o_ready, UNITS // 2)
            quant_scale(4, 0, UNITS // 2, factor=qs[:, 12:13])

            def product_int(i, par):
                t = 2 * i + par
                dve.wait_ge(om_ready, t + 1)
                wait(dve, down_done, t - 1)
                dve.tensor_scalar(ok[par], om[par], MAGIC, None, ALU.subtract).then_inc(ok_ready, 1)

            def residual(t, par):
                dve.wait_ge(down_done, t + 1)
                dve.scalar_tensor_tensor(out=x_tile(t), in0=PS[:, 6 + par, 0:D], scalar=qs[:, 8:9], in1=x_tile(t),
                                         op0=ALU.mult, op1=ALU.add).then_inc(x2_done, 1)
                dve.wait_ge(x2_done, t + 1)
                st.mark(dve.bn_stats(stats[:, ds(t, 1), :].rearrange("p a d -> p (a d)"), x_tile(t)))

            product_int(0, 0)
            product_int(0, 1)
            residual(0, 0)
            with dve.Fori(1, T // 2) as i:
                st.enter(i, 1, 2)
                product_int(i, 0)
                residual(2 * i - 1, 1)
                product_int(i, 1)
                residual(2 * i, 0)
                st.leave(T // 2 - 1)
            residual(T - 1, 1)

            if stop < 3:
                return

            for par in range(2):
                st.mark(dve.memset(V[par], 0.0))
            st.wait()
            for par in range(2):
                dve.memset(V[par][:, :, :, HD:HD + 1], 1.0).then_inc(init_ready, 1)
            dve.memset(nst[:], 0.0).then_inc(init_ready, 1)
            norm_stats(3)
            dve.wait_ge(b_in, 96)

            steps = Steps(), Steps()
            pe_side, ev_side = (pe6, pe7), (ev6, ev7)

            def zs(b):
                wait(dve, pe6, steps[0].now())
                for h in range(HP):
                    ins = dve.tensor_scalar(zz[:, h, :], x_tile(HP * b + h), mean[:, ds(HP * b + h, 1)],
                                            rstd[:, ds(HP * b + h, 1)], ALU.subtract, ALU.mult)
                ins.then_inc(zz_ready, 1)

            def side_step(step, v, par):
                k = BANK[step]
                n = steps[k].next()
                if step in ("project 0", "project 1"):
                    wait(dve, high_ready, HP * v)
                    wait(dve, k_high, v)
                    dve.wait_ge(pe_side[k], n)
                    dve.tensor_tensor(qkf[:, :, k, :], side[k].rearrange("p (w d) -> p w d", w=2), bqk[:], ALU.add)\
                       .then_inc(ev_side[k], 1)
                elif step == "values":
                    dve.wait_ge(pe6, n)
                    dve.tensor_tensor(V[par][:, :, :, 0:HD], side[0].rearrange("p (k h d) -> p k h d", k=HP, h=H),
                                      bvo[:, 0, :].rearrange("p (h d) -> p h d", h=H).unsqueeze(1)
                                      .broadcast_to((P, HP, H, HD)), ALU.add).then_inc(ev6, 1)
                elif step in ("back 0", "back 1"):
                    dve.wait_ge(pe_side[k], n)
                    o = side[k].rearrange("p (h v) -> p h v", v=VW)
                    st.mark(dve.reciprocal(den[:, k, :], o[:, :, HD]))
                    st.wait()
                    dve.tensor_tensor(on[:, k, :].rearrange("p (j d) -> p j d", d=HD), o[:, :, 0:HD],
                                      den[:, k, :].unsqueeze(2).broadcast_to((P, H, HD)), ALU.mult)\
                       .then_inc(ev_side[k], 1)
                elif step == "output":
                    dve.wait_ge(pe6, n)
                    dve.tensor_tensor(yo, side[0].rearrange("p (h d) -> p h d", h=HP),
                                      bvo[:, 1:2, :].broadcast_to((P, HP, D)), ALU.add).then_inc(ev6, 1)
                    dve.wait_ge(ev6, n)
                    xb = X[:, ds(HP * (v - 2), HP), :]
                    dve.tensor_tensor(xb, xb, yo, ALU.add).then_inc(x3_done, 1)
                    dve.wait_ge(x3_done, v - 1)
                    for h in range(HP):
                        st.mark(dve.bn_stats(stats[:, ds(HP * (v - 2) + h, 1), :].rearrange("p a d -> p (a d)"),
                                             x_tile(HP * (v - 2) + h)))
                elif step.startswith("parts") and k == 0:
                    dve.wait_ge(pe6, n)
                    turned_copy(dve.tensor_copy, par, int(step[6:]), 0).then_inc(ev6, 1)

            both = rest.rearrange("p (j d) -> p j d", d=HD)

            def rest_parts(v, w):
                dve.wait_ge(high_ready, HP * (v + 1)) if w == 0 else dve.wait_ge(k_high, v + 1)
                dve.tensor_tensor(both[:, 32 * w:32 * w + 32, :], qkf[:, w].rearrange("p h (j d) -> p (h j) d", d=HD),
                                  stack[:, w, :, 2, :], ALU.subtract).then_inc(rest_ready, 1)

            def low_parts(v, w):
                dve.wait_ge((mid_ready, k_mid)[w], v + 1)
                dve.wait_ge(rest_ready, 2 * v + 1 + w)
                dve.tensor_tensor(parts(w, "low")[:, :, 0, :], both[:, 32 * w:32 * w + 32, :],
                                  stack[:, w, :, 5, :], ALU.subtract).then_inc(low_ready, 1)

            def row_max(v, h):
                dve.wait_ge(s1_done, H * v + h + 1)
                dve.tensor_reduce(negm[:, :, h], s_bank[h % 2], AX.X, ALU.max, negate=True).then_inc(max_done, 1)

            def max_parts(v, g):
                part = [nst[:, :, 32 * k + LAG * g:32 * k + LAG * (g + 1)] for k in range(2)]
                m = negm[:, :, LAG * g:LAG * (g + 1)]
                dve.wait_ge(max_done, H * v + LAG * (g + 1))
                st.mark(dve.tensor_copy(part[0], m))
                st.wait()
                dve.tensor_tensor(part[1], m, part[0], ALU.subtract).then_inc(neg_ready, 1)

            def round_(v, par, before=True, after=True):
                for h in range(H):
                    row_max(v, h)
                    if after and h == 0:
                        zs(v + 1)
                    g = h // LAG
                    if h % LAG == LAG - 1:
                        max_parts(v, g)
                    todo = planned(h, before, after)
                    first = len(todo) - 1 if h % LAG == LAG - 1 else len(todo)
                    first = max(first, 0)
                    for step in todo[:first]:
                        side_step(step, v + 1, 1 - par)
                    if h % LAG == LAG - 1:
                        dve.wait_ge(neg_turned, NG * v + g + 1)
                        dve.tensor_copy(negT[g % 2], NEGB).then_inc(negt_ready, 1)
                    for step in todo[first:]:
                        side_step(step, v + 1, 1 - par)
                    if after and h in (4, 5):
                        rest_parts(v + 1, h - 4)
                    if after and h in (6, 7):
                        low_parts(v + 1, h - 6)

            zs(0)
            for step in FIRST:
                side_step(step, 0, 0)
                if step == "project 1":
                    for w in range(2):
                        rest_parts(0, w)
                    for w in range(2):
                        low_parts(0, w)
            round_(0, 0, before=False)
            with dve.Fori(0, B // 2 - 1) as i:
                for k in range(2):
                    steps[k].enter(i, 2 * PER[k])
                st.enter(i, 0, 2 * (NG + 2 + HP))
                round_(2 * i + 1, 1)
                round_(2 * i + 2, 0)
                st.leave(B // 2 - 1)
                for k in range(2):
                    steps[k].leave(B // 2 - 1)
            round_(B - 1, 1, after=False)
            for step in FINISH:
                side_step(step, B + 1, 1)
            if stop < 4:
                return

            norm_stats(4)

            def router(t, par):
                wait(dve, zrt_done, t - 1)
                normalise(t, z[par][:])
                dve.tensor_scalar(Z[:, ds(t, 1), :].rearrange("p a d -> p (a d)"), x_tile(t), mean[:, ds(t, 1)],
                                  rstd[:, ds(t, 1)], ALU.subtract, ALU.mult).then_inc(zr_ready, 1)

            router(0, 0)
            router(1, 1)
            with dve.Fori(1, T // 2) as i:
                router(2 * i, 0)
                router(2 * i + 1, 1)
            dve.wait_ge(b_in, 96)
            dve.wait_ge(lg_done, T)
            st.mark(dve.tensor_tensor(lg, PS[:, 2, 0:T * E].rearrange("p (t e) -> p t e", e=E),
                                      brB[:].unsqueeze(1).broadcast_to((P, T, E)), ALU.add))
            st.wait()
            st.mark(dve.tensor_reduce(top[:], lg, AX.X, ALU.max))
            st.wait()
            st.mark(dve.tensor_tensor(eq, lg, top[:].unsqueeze(2).broadcast_to((P, T, E)), ALU.is_ge))
            st.wait()
            st.mark(dve.scalar_tensor_tensor(out=eq, in0=eq, scalar=-float(E), in1=iota_e[:].unsqueeze(1)
                                             .broadcast_to((P, T, E)), op0=ALU.mult, op1=ALU.add))
            st.wait()
            st.mark(dve.tensor_reduce(first[:], eq, AX.X, ALU.min))
            st.wait()
            st.mark(dve.tensor_scalar(first[:], first[:], float(E), None, ALU.add))
            st.wait()
            dve.tensor_tensor(onehot, iota_e[:].unsqueeze(1).broadcast_to((P, T, E)),
                              first[:].unsqueeze(2).broadcast_to((P, T, E)), ALU.is_equal).then_inc(onehot_ready, 1)
            dve.wait_ge(rank_done, 1)
            st.mark(dve.tensor_copy(cum_a, PS[:, 3, P:2 * P].rearrange("p (t e) -> p t e", e=E)))
            st.wait()
            st.mark(dve.tensor_copy(place, cum_a))
            a, b = cum_a, cum_b
            step = 1
            while step < T:
                st.mark(dve.tensor_copy(b[:, 0:step, :], a[:, 0:step, :]))
                st.mark(dve.tensor_tensor(b[:, step:T, :], a[:, step:T, :], a[:, 0:T - step, :], ALU.add))
                st.wait()
                a, b = b, a
                step *= 2
            st.mark(dve.tensor_tensor(place, a, place, ALU.subtract))
            n_tiles, n_cum, n_tmp, n_base = (tiles[:, k, :] for k in range(4))
            st.mark(dve.tensor_scalar(n_tiles, a[:, T - 1, :], 1.0 / P, (P - 1.0) / P - 0.5 + 0.5 / P, ALU.mult, ALU.add))
            st.wait()
            st.mark(dve.tensor_scalar(n_tiles, n_tiles, MAGIC, MAGIC, ALU.add, ALU.subtract))
            st.wait()
            st.mark(dve.tensor_copy(n_cum, n_tiles))
            st.wait()
            a, b = n_cum, n_tmp
            step = 1
            while step < E:
                st.mark(dve.tensor_copy(b[:, 0:step], a[:, 0:step]))
                st.mark(dve.tensor_tensor(b[:, step:E], a[:, step:E], a[:, 0:E - step], ALU.add))
                st.wait()
                a, b = b, a
                step *= 2
            st.mark(dve.tensor_tensor(n_base, a, n_tiles, ALU.subtract))
            st.mark(dve.tensor_tensor(over, a.unsqueeze(1).broadcast_to((P, J, E)),
                                      iota_j[:].unsqueeze(2).broadcast_to((P, J, E)), ALU.is_le))
            st.wait()
            st.mark(dve.tensor_scalar(n_base, n_base, float(P), None, ALU.mult))
            st.mark(dve.tensor_tensor(place, place, PS[:, 3, 0:P].rearrange("p (t e) -> p t e", e=E), ALU.add))
            st.mark(dve.tensor_reduce(ef[:], over, AX.X, ALU.add))
            st.wait()
            st.mark(dve.tensor_tensor(place, place, n_base.unsqueeze(1).broadcast_to((P, T, E)), ALU.add))
            st.mark(dve.tensor_scalar(ef[:], ef[:], E - 1.0, None, ALU.min))
            st.wait()
            st.mark(dve.tensor_tensor(place, place, onehot, ALU.mult))
            st.mark(dve.tensor_copy(expert[:], ef[:]))
            st.wait()
            st.mark(dve.tensor_reduce(posf[:], place, AX.X, ALU.add))
            st.wait()
            dve.tensor_copy(pos[:], posf[:]).then_inc(pos_ready, 1)
            dve.wait_ge(be_in, 32)

            def expert_of(j):
                return dve.value_load(expert[0:1, ds(j, 1)], min_val=0, max_val=E - 1)

            def hidden(j, par, e):
                dve.wait_ge(h_done, j + 1)
                wait(dve, ht_done, j - 1)
                dve.tensor_tensor(hn[par], PS[:, 2 + par, :], b1B[:, ds(e, 1), :].rearrange("p a f -> p (a f)"),
                                  ALU.add).then_inc(h_copied, 1)

            def result(j, i, par, e):
                dve.wait_ge(y_done, j + 1)
                if not (isinstance(j, int) and j < 2):
                    dve.wait_ge(y_out[par], 16 * i)
                dve.tensor_tensor(ys[par], PS[:, 6 + par, 0:D], b2B[:, ds(e, 1), :].rearrange("p a f -> p (a f)"),
                                  ALU.add).then_inc(y_copied, 1)

            hidden(0, 0, expert_of(0))
            hidden(1, 1, expert_of(1))
            result(0, 0, 0, expert_of(0))
            hidden(2, 0, expert_of(2))
            result(1, 0, 1, expert_of(1))
            hidden(3, 1, expert_of(3))
            result(2, 1, 0, expert_of(2))
            with dve.Fori(2, J // 2) as i:
                e_before, e_even, e_odd = (expert_of(2 * i + k) for k in (-1, 0, 1))
                hidden(2 * i, 0, e_even)
                result(2 * i - 1, i - 1, 1, e_before)
                hidden(2 * i + 1, 1, e_odd)
                result(2 * i, i, 0, e_even)
            hidden(J - 1, 0, expert_of(J - 1))
            result(J - 2, J // 2 - 1, 1, expert_of(J - 2))
            result(J - 1, J // 2, 0, expert_of(J - 1))
            for q in range(4):
                dve.wait_ge(back[q], 64)
                xq = X[:, 4 * q:4 * q + 4, :]
                dve.tensor_tensor(xq, xq, Y[:, 4 * q:4 * q + 4, :], ALU.add).then_inc(x4_done, 1)

        @block.tensor
        def _(pe):
            def turn_weights(n):
                wait(pe, wt_copied, n - 3)
                for m in range(4):
                    ins = pe.transpose(PS[:, 4 + n % 4, P * m:P * m + P], TW[4 * n + m][1], ident[:])
                ins.then_inc(wt_done, 1)

            pe.wait_ge(s_const, 1)

            def sum_products(t, par):
                if not valid(t):
                    return
                pe.wait_ge(prod_done, t + 1)
                wait(pe, raw_done, t - 1)
                pe.matmul(PS[:, par, 0:PAIRS[NB]], ident[:], causal[:, 0:PAIRS[NB]], start=True, stop=False)
                for d in range(HD):
                    ins = pe.matmul(PS[:, par, 0:PAIRS[NB]], ident[:], prod[par][:, d, :], start=False,
                                    stop=(d == HD - 1))
                ins.then_inc(sum_done, 1)

            def sum_values(t, par):
                if not valid(t):
                    return
                pe.wait_ge(pv_pool, t + 1)
                pe.wait_ge(pv_dve, t + 1)
                wait(pe, x1_done, t - 1)
                pe.matmul(PS[:, 2 + par, 0:D], ident[:], X[:, ds(t, 1), :].rearrange("p a d -> p (a d)"), start=True,
                          stop=False)
                for k in range(0, H, 2):
                    lo = QR * HD * (k // QR)
                    ins = pe.matmul(PS[:, 2 + par, lo:D], ident[:], prod2[par][:, k, lo:D], start=False,
                                    stop=(k == H - 2))
                ins.then_inc(total_done, 1)

            def step(i, k):
                sum_products(i, k)
                sum_values(i - 2, k)

            for i in range(FILL):
                step(i, i % 2)
            with pe.Fori(FILL // 2, T // 2) as i:
                for k in range(2):
                    step(2 * i + k, k)
            step(T, 0)
            pe.wait_ge(wa_in, 64)
            for n in range(NA):
                turn_weights(n)
            step(T + 1, 1)
            pe.wait_ge(w_ready, T)
            for n in range(NA, NW):
                turn_weights(n)
            if stop < 2:
                return

            for t in range(T):
                pe.wait_ge(z_ready, t + 1)
                bank = PS[:, t // 2 % 4, :].rearrange("p (k h n) -> p k h n", k=KD, h=2)
                if t % 2 == 0:
                    wait(pe, zt_copied, t // 2 - 3)
                for k in range(KD):
                    ins = pe.transpose(bank[:, k, t % 2, :], Zall[:, t, P * k:P * k + P], ident[:])
                if t % 2:
                    ins.then_inc(zt_done, 1)
            pe.wait_ge(wt_copied, NW)

            def project(wT, cc, f, u):
                wait(pe, mm_copied, u - KF + 1)
                for k in range(KD):
                    ins = pe.matmul(PS[:, f, :], wT[:, k, P * f:P * f + P], zT[:, k, ds(cc * CH, CH)],
                                    start=(k == 0), stop=(k == KD - 1))
                ins.then_inc(mm_done, 1)

            pe.wait_ge(zt_copied, T // 2)
            for f in range(KF):
                pe.wait_ge(xq_ready, 1)
                project(gateT, 0, f, f)
            with pe.Fori(1, NCH) as cc:
                pe.wait_ge(xq_ready, cc + 1)
                for f in range(KF):
                    project(gateT, cc, f, cc * KF + f)
            with pe.Fori(0, NCH) as cc:
                for f in range(KF):
                    project(upT, cc, f, UNITS + cc * KF + f)

            def down(i, par):
                t = 2 * i + par
                pe.wait_ge(ok_ready, t + 1)
                wait(pe, x2_done, t - 1)
                for f in range(KF):
                    ins = pe.matmul(PS[:, 6 + par, 0:D], ok[par][:, f, :], downT[:, f, :], start=(f == 0),
                                    stop=(f == KF - 1))
                ins.then_inc(down_done, 1)

            down(0, 0)
            down(0, 1)
            with pe.Fori(1, T // 2) as i:
                down(i, 0)
                down(i, 1)
            if stop < 3:
                return

            steps = Steps(), Steps()
            pe_side, ev_side = (pe6, pe7), (ev6, ev7)

            def turn_both(k, tiles):
                for c in range(KD):
                    for h in range(HP):
                        ins = pe.transpose(side[k][:, S * c + P * h:S * c + P * h + P], tiles[:, h, P * c:P * c + P],
                                           ident[:])
                return ins

            def side_step(step, v, par, loads):
                k = BANK[step]
                wait(pe, ev_side[k], steps[k].now())
                if step == "turn z":
                    pe.wait_ge(zz_ready, v + 1)
                    ins = turn_both(0, zz)
                elif step == "turn ctx":
                    pe.wait_ge(ct_in[par], 16 * loads)
                    ins = turn_both(1, ct[par])
                elif step in ("project 0", "project 1"):
                    if k == 0:
                        pe.wait_ge(ev7, steps[1].now())
                    for w, src in ((0, zTb), (1, cTb)):
                        for c in range(KD):
                            ins = pe.matmul(side[k][:, D * w:D * w + D], src[:, c, P * k:P * k + P], attnT[:, w, c, :],
                                            start=(c == 0), stop=(c == KD - 1))
                elif step == "values":
                    for h in range(HP):
                        for c in range(KD):
                            ins = pe.matmul(side[0][:, D * h:D * h + D], cTb[:, c, P * h:P * h + P], attnT[:, 2, c, :],
                                            start=(c == 0), stop=(c == KD - 1))
                elif step.startswith("parts"):
                    m = int(step[6:])
                    pe.wait_ge(low_ready, 2 * v + 1 + m // 4)
                    bank = side[k][0:NP6, :].bitcast(BF16)
                    for q in range(4):
                        for h in range(HP):
                            j = h * H + 4 * (m % 4) + q
                            ins = pe.transpose(bank[:, S * q + P * h:S * q + P * h + P],
                                               stack[:, m // 4, j, :, :].rearrange("p c d -> p (c d)"), identb[:])
                elif step in ("back 0", "back 1"):
                    pe.wait_ge(ot_ready, 2 * (v - 1))
                    for g in range(4):
                        ins = pe.transpose(side[k][:, P * g:P * g + P], OT[:, g, P * k:P * k + P], ident[:])
                elif step == "turn out":
                    pe.wait_ge(ev6, steps[0].now())
                    ins = turn_both(1, on)
                elif step == "output":
                    pe.wait_ge(ev7, steps[1].now())
                    for h in range(HP):
                        for c in range(KD):
                            ins = pe.matmul(side[0][:, D * h:D * h + D], oT[:, c, P * h:P * h + P], attnT[:, 3, c, :],
                                            start=(c == 0), stop=(c == KD - 1))
                ins.then_inc(pe_side[k], 1)
                steps[k].next()

            def first_scores(v, par, h):
                c = H * v + h
                wait(pe, max_done, c - 1)
                if h % LAG == 1:
                    wait(pe, negt_ready, NG * v + h // LAG)
                for q in range(HP):
                    ins = pe.matmul(s_bank[h % 2][:, q, :], stackT[par][0][:, h, P * q:P * q + P],
                                    stackT[par][1][:, h, :], start=True, stop=True)
                ins.then_inc(s1_done, 1)

            def second_scores(b, par, h):
                c = H * b + h
                wait(pe, e_done, c - 1)
                if h % LAG == 0:
                    pe.wait_ge(negt_ready, NG * b + h // LAG + 1)
                for k in range(HP):
                    pe.matmul(st_bank[h % 2][:, k, :], stackT[par][1][:, h, P * k:P * k + P], stackT[par][0][:, h, :],
                              start=True, stop=False)
                    ins = pe.matmul(st_bank[h % 2][:, k, :], select_row[:, h, :], negT[h // LAG % 2], start=False,
                                    stop=True)
                ins.then_inc(s2_done, 1)

            def weigh(b, par, h):
                pe.wait_ge(e_done, H * b + h + 1)
                if h % 8 == 0:
                    wait(pe, ot_ready, 2 * b - 1 + h // 8)
                for k in range(HP):
                    ins = pe.matmul(o_part(h), V[par][:, k, h, :], PT[h % 2][:, k, :], start=(k == 0),
                                    stop=(k == HP - 1))
                ins.then_inc(pv_done, 1)

            def turn_maxima(v, g):
                pe.wait_ge(neg_ready, NG * v + g + 1)
                for h in range(HP):
                    ins = pe.transpose(NEGB[:, P * h:P * h + P], nst[:, h, :], identb[:])
                ins.then_inc(neg_turned, 1)

            def round_(v, par, loads, before=True, after=True):
                for h in range(H):
                    first_scores(v, par, h)
                    if h % LAG == 0 and (h >= LAG + 1 or before):
                        weigh(*lagged(v, par, h, LAG + 1))
                    if h >= LAG or before:
                        second_scores(*lagged(v, par, h, LAG))
                    if h % LAG and (h >= LAG + 1 or before):
                        weigh(*lagged(v, par, h, LAG + 1))
                    todo = planned(h, before, after)
                    first = 1 if h == LAG - 1 else len(todo)
                    for step in todo[:first]:
                        side_step(step, v + 1, 1 - par, loads)
                    if h % LAG == LAG - 1:
                        turn_maxima(v, h // LAG)
                    for step in todo[first:]:
                        side_step(step, v + 1, 1 - par, loads)

            pe.wait_ge(init_ready, 4)
            for step in FIRST:
                side_step(step, 0, 0, 1)
            for k in range(2):
                pe.wait_ge(ev_side[k], steps[k].now())
            round_(0, 0, 1, before=False)
            with pe.Fori(0, B // 2 - 1) as i:
                for k in range(2):
                    steps[k].enter(i, 2 * PER[k])
                round_(2 * i + 1, 1, i + 2)
                round_(2 * i + 2, 0, i + 2)
                for k in range(2):
                    steps[k].leave(B // 2 - 1)
            for k in range(2):
                pe.wait_ge(ev_side[k], steps[k].now())
            round_(B - 1, 1, 0, after=False)
            for h in range(H - LAG, H):
                second_scores(B - 1, 1, h)
                weigh(B - 1, 1, h - 1)
            weigh(B - 1, 1, H - 1)
            for step in FINISH:
                side_step(step, B + 1, 1, 0)
            if stop < 4:
                return

            def turn(t, par):
                pe.wait_ge(zr_ready, t + 1)
                wait(pe, zrt_copied, t - 1)
                for k in range(KD):
                    ins = pe.transpose(PS[:, par, P * k:P * k + P], z[par][:, P * k:P * k + P], ident[:])
                ins.then_inc(zrt_done, 1)

            def logits(t, par):
                pe.wait_ge(zrt_copied, t + 1)
                for k in range(KD):
                    ins = pe.matmul(PS[:, 2, ds(E * t, E)], zr[par][:, k, :], Wr[:, k, :], start=(k == 0),
                                    stop=(k == KD - 1))
                ins.then_inc(lg_done, 1)

            pe.wait_ge(b_in, 96)
            turn(0, 0)
            turn(1, 1)
            logits(0, 0)
            with pe.Fori(1, T // 2) as i:
                turn(2 * i, 0)
                logits(2 * i - 1, 1)
                turn(2 * i + 1, 1)
                logits(2 * i, 0)
            logits(T - 1, 1)
            pe.wait_ge(onehot_ready, 1)
            oh = onehot.rearrange("p t e -> p (t e)")
            pe.matmul(PS[:, 3, 0:P], before[:], oh, start=True, stop=True)
            pe.matmul(PS[:, 3, P:2 * P], ones[:], oh, start=True, stop=True).then_inc(rank_done, 1)

            def rows(j, i, par):
                pe.wait_ge(ez_in[par], 16 * (i + 1))
                wait(pe, et_copied, j - 1)
                for k in range(KD):
                    ins = pe.transpose(PS[:, par, P * k:P * k + P], ez[par][:, P * k:P * k + P], ident[:])
                ins.then_inc(et_done, 1)

            def expert_of(j):
                return pe.value_load(expert[0:1, ds(j, 1)], min_val=0, max_val=E - 1)

            def hidden(j, par, e):
                pe.wait_ge(et_copied, j + 1)
                wait(pe, h_copied, j - 1)
                for k in range(KD):
                    ins = pe.matmul(PS[:, 2 + par, :], ezT[par][:, k, :], W1[:, ds(e * KD + k, 1), :].rearrange("p a f -> p (a f)"),
                                    start=(k == 0), stop=(k == KD - 1))
                ins.then_inc(h_done, 1)

            def turn_hidden(j, par):
                pe.wait_ge(h_copied, j + 1)
                wait(pe, ht_copied, j - 1)
                for f in range(K1):
                    ins = pe.transpose(PS[:, 4 + par, P * f:P * f + P], hn[par][:, P * f:P * f + P], ident[:])
                ins.then_inc(ht_done, 1)

            def result(j, par, e):
                pe.wait_ge(ht_copied, j + 1)
                wait(pe, y_copied, j - 1)
                for f in range(K1):
                    ins = pe.matmul(PS[:, 6 + par, 0:D], hT[par][:, f, :], W2[:, ds(e * K1 + f, 1), :].rearrange("p a d -> p (a d)"),
                                    start=(f == 0), stop=(f == K1 - 1))
                ins.then_inc(y_done, 1)

            pe.wait_ge(e_in, 32)
            pe.wait_ge(pos_ready, 1)
            rows(0, 0, 0)
            hidden(0, 0, expert_of(0))
            rows(1, 0, 1)
            turn_hidden(0, 0)
            hidden(1, 1, expert_of(1))
            rows(2, 1, 0)
            result(0, 0, expert_of(0))
            turn_hidden(1, 1)
            hidden(2, 0, expert_of(2))
            with pe.Fori(1, J // 2) as i:
                e_before, e_even = expert_of(2 * i - 1), expert_of(2 * i)
                rows(2 * i + 1, i, 1)
                result(2 * i - 1, 1, e_before)
                turn_hidden(2 * i, 0)
                e_odd = expert_of(2 * i + 1)
                hidden(2 * i + 1, 1, e_odd)
                rows(2 * i + 2, i + 1, 0)
                result(2 * i, 0, e_even)
                turn_hidden(2 * i + 1, 1)
                e_after = expert_of(2 * i + 2)
                hidden(2 * i + 2, 0, e_after)
            result(J - 2, 1, expert_of(J - 2))
            turn_hidden(J - 1, 0)
            result(J - 1, 0, expert_of(J - 1))


_INS = ['x', 'ctx_1024', 'L0_ffn_w_gate', 'L0_ffn_w_up', 'L0_ffn_w_down', 'L1_xattn_Wq', 'L1_xattn_bq', 'L1_xattn_Wk',
        'L1_xattn_bk', 'L1_xattn_Wv', 'L1_xattn_bv', 'L1_xattn_Wo', 'L1_xattn_bo', 'L1_ffn_W1', 'L1_ffn_b1',
        'L1_ffn_W2', 'L1_ffn_b2', 'L1_ffn_Wr', 'L1_ffn_br']


def kernel(**inputs):
    import numpy as _np
    import concourse.bacc as _bacc
    from concourse import mybir as _mybir
    from concourse.bass_utils import run_bass_kernel_spmd as _run

    nc = _bacc.Bacc("TRN2", target_bir_lowering=False, num_devices=1)
    arrays, args = {}, {}
    for name in _INS:
        a = _np.ascontiguousarray(inputs[name])
        arrays[f"in_{name}_dram"] = a
        args[name] = nc.dram_tensor(f"in_{name}_dram", a.shape, _mybir.dt.from_np(a.dtype), kind="ExternalInput").ap()
    out = nc.dram_tensor("out_0_dram", inputs["x"].shape, _mybir.dt.float32, kind="ExternalOutput").ap()
    build(nc, args, out, stop=STOP)
    r = _run(nc, [arrays], core_ids=[0])
    return r.results[0]["out_0_dram"]


STOP = 4
```

```python
from contextlib import ExitStack

import concourse.bass as bass
from concourse import mybir

F32 = mybir.dt.float32
BF16 = mybir.dt.bfloat16
I32 = mybir.dt.int32
ALU = mybir.AluOpType
ACT = mybir.ActivationFunctionType
AX = mybir.AxisListType
RED = bass.bass_isa.ReduceOp
ds = bass.ds

P = 128
EPS = 1e-5
MASKED = -1e18


class Count:

    def __init__(self, eng, sem):
        self.eng, self.sem, self.base, self.n = eng, sem, 0, 0

    def mark(self, ins):
        ins.then_inc(self.sem, 1)
        self.n += 1
        return self.base + self.n

    def wait(self):
        self.eng.wait_ge(self.sem, self.base + self.n)

    def enter(self, i, first, per):
        self.start = self.base + self.n
        self.base, self.n, self.per = self.start + (i - first) * per, 0, per

    def leave(self, times):
        assert self.n == self.per, self.n
        self.base, self.n = self.start + times * self.per, 0


class Steps:

    def __init__(self):
        self.base, self.n = 0, 0

    def now(self):
        return self.base + self.n

    def next(self):
        self.n += 1
        return self.now()

    def enter(self, i, per):
        self.start = self.now()
        self.base, self.n, self.per = self.start + i * per, 0, per

    def leave(self, times):
        assert self.n == self.per, self.n
        self.base, self.n = self.start + times * self.per, 0


def wait(eng, sem, value):
    if isinstance(value, int) and value <= 0:
        return
    eng.wait_ge(sem, value)


def build(nc, A, out):
    x, ctx_in = A["x"], A["ctx_1024"]
    B, S, D = x.shape
    T = B * S // P
    N = B * S
    H, HD = 16, D // 16
    KD = D // P
    F0 = A["L0_ffn_w_gate"].shape[0]
    KF = F0 // P
    QB = 32
    CH = 512
    NCH = N // CH
    UNITS = NCH * KF
    MAGIC = 1.5 * 2.0 ** 23
    QMAX = 32767.0

    es = ExitStack()
    with es:
        def sb(name, shape, dt=F32):
            return es.enter_context(nc.sbuf_tensor(name, shape, dt))

        def sem(name):
            return es.enter_context(nc.semaphore(name))

        x_dram = x.rearrange("b (h p) d -> p (b h) d", p=P)
        out_dram = out.rearrange("b (h p) d -> p (b h) d", p=P)
        ctx_dram = ctx_in.rearrange("b (h p) d -> p (b h) d", p=P)

        PS = es.enter_context(nc.psum_tensor("PS", [P, 8, 512], F32))
        X = sb("X", [P, T, D])
        ident = sb("ident", [P, P])
        identb = sb("identb", [P, P], BF16)
        small = sb("small", [P, 5 * H * H])
        causal = small[:, 0:H * H]
        magic = sb("magic", [P, 1])
        stats = sb("stats", [P, T, 6])
        mean = sb("mean", [P, T])
        var = sb("var", [P, T])
        rstd = sb("rstd", [P, T])
        tmp = sb("tmp", [P, T])
        z = [sb(f"z{i}", [P, D]) for i in range(2)]
        wspace = sb("wspace", [P, 3 * KD * F0])
        gateT = wspace[:, 0:KD * F0].rearrange("p (i f) -> p i f", i=KD)
        upT = wspace[:, KD * F0:2 * KD * F0].rearrange("p (i f) -> p i f", i=KD)
        downT = wspace[:, 2 * KD * F0:3 * KD * F0].rearrange("p (f o) -> p f o", f=KF)
        attnT = sb("attnT", [P, 4, KD, D])
        zT = sb("zT", [P, KD, N])
        amax = sb("amax", [P, 4, 64])
        gmax = sb("gmax", [P, 4])
        gall = sb("gall", [P, 4])
        qs = sb("qs", [P, 16])
        arena = sb("arena", [P, 2 * KF * N])
        U = arena[:, 0:KF * N].rearrange("p (f n) -> p f n", f=KF)
        G = arena[:, KF * N:2 * KF * N].rearrange("p (f n) -> p f n", f=KF)

        const_ready = sem("const_ready")
        pool_setup = sem("pool_setup")
        x_in = [sem(f"x_in{q}") for q in range(4)]
        c_in = [sem(f"c_in{q}") for q in range(4)]
        w_in = sem("w_in")
        wa_in = sem("wa_in")
        dve_step = sem("dve_step")
        var_ready = sem("var_ready")
        sd_ready = sem("sd_ready")
        block = es.enter_context(nc.Block())

        def apart(eng):
            eng.nop(nofuse=True)

        QR = 4
        NB = H // QR
        PAIRS = [QR * QR * b * (b + 1) // 2 for b in range(NB + 1)]
        C = arena[:, 0:T * D].rearrange("p (t d) -> p t d", t=T)
        a0 = T * D
        prod, prod2 = [], []
        for k in range(2):
            n = HD * PAIRS[NB]
            prod.append(arena[:, a0:a0 + n].rearrange("p (d j) -> p d j", d=HD))
            a0 += n
        for k in range(2):
            prod2.append(arena[:, a0:a0 + H * D].rearrange("p (k j) -> p k j", k=H))
            a0 += H * D
        raw = arena[:, a0:a0 + 3 * KD * F0].rearrange("p (g w) -> p g w", w=QB)
        rawg = arena[:, a0:a0 + KD * F0].rearrange("p (f i) -> p f i", f=KF)
        rawu = arena[:, a0 + KD * F0:a0 + 2 * KD * F0].rearrange("p (f i) -> p f i", f=KF)
        rawd = arena[:, a0 + 2 * KD * F0:a0 + 3 * KD * F0].rearrange("p (o i) -> p o i", o=KD)
        NQ = 3 * KD * F0 // QB
        a0 += 3 * KD * F0
        rawa = arena[:, a0:a0 + 4 * KD * D].rearrange("p (w o i) -> p w o i", w=4, o=KD)
        a0 += 4 * KD * D
        wscale = arena[:, a0:a0 + NQ]
        winv = arena[:, a0 + NQ:a0 + 2 * NQ]
        a0 += 2 * NQ
        assert a0 <= 2 * KF * N
        sraw, sm = [[small[:, H * H * (1 + 2 * a + k):H * H * (2 + 2 * a + k)].rearrange("p (q k) -> p q k", q=H)
                     for k in range(2)] for a in range(2)]
        rmax = sb("rmax", [P, H])
        rsum = sb("rsum", [P, H])
        rinv = sb("rinv", [P, 2, H])
        shift = sb("shift", [P, T])
        shift_ready = sem("shift_ready")
        z0_done = sem("z0_done")
        prod_done = sem("prod_done")
        sum_done = sem("sum_done")
        raw_done = sem("raw_done")
        less_max_ready = sem("less_max_ready")
        exp_ready = sem("exp_ready")
        rinv_done = sem("rinv_done")
        p_ready = sem("p_ready")
        pool_product = sem("pool_product")
        pv_pool = sem("pv_pool")
        pv_dve = sem("pv_dve")
        total_done = sem("total_done")
        x1_done = sem("x1_done")
        bn_ready = sem("bn_ready")

        def valid(t):
            return not isinstance(t, int) or 0 <= t < T

        def pairs(par, b):
            return prod[par][:, :, PAIRS[b]:PAIRS[b + 1]].rearrange("p d (q k) -> p q k d", q=QR)

        def ctx_tile(t, nk):
            return C[:, ds(t, 1), 0:HD * nk].rearrange("p a (k d) -> p (a k) d", d=HD)

        def weighted(eng, t, par, blocks):
            for b in blocks:
                nk = QR * (b + 1)
                ins = eng.tensor_tensor(
                    prod2[par][:, 0:nk, QR * HD * b:QR * HD * (b + 1)].rearrange("p k (q d) -> p k q d", q=QR),
                    sm[par][:, QR * b:QR * (b + 1), 0:nk].rearrange("p q k -> p k q").unsqueeze(3)
                    .broadcast_to((P, nk, QR, HD)),
                    ctx_tile(t, nk).unsqueeze(2).broadcast_to((P, nk, QR, HD)), ALU.mult)
            return ins

        def add_pairs(eng, par, blocks):
            for b in blocks:
                v = prod2[par][:, 0:QR * (b + 1), QR * HD * b:QR * HD * (b + 1)].rearrange("p (k o) j -> p k o j", o=2)
                ins = eng.tensor_tensor(v[:, :, 0, :], v[:, :, 0, :], v[:, :, 1, :], ALU.add)
            return ins

        DVE_BLOCKS, POOL_BLOCKS = (0, 1), (2, 3)
        FILL = 4
        w_ready = sem("w_ready")
        wt_done = sem("wt_done")
        wt_copied = sem("wt_copied")

        z_ready = sem("z_ready")
        zt_done = sem("zt_done")
        zt_copied = sem("zt_copied")
        amax_ready = sem("amax_ready")
        gall_ready = sem("gall_ready")
        scale_ready = sem("scale_ready")
        xm_ready = sem("xm_ready")
        xq_ready = sem("xq_ready")
        mm_done = sem("mm_done")
        mm_copied = sem("mm_copied")
        mm_maxed = sem("mm_maxed")
        gm_ready = sem("gm_ready")
        gk_ready = sem("gk_ready")
        sig_ready = sem("sig_ready")
        n_ready = sem("n_ready")
        g2_ready = sem("g2_ready")
        pm_ready = sem("pm_ready")
        j_ready = sem("j_ready")
        o_ready = sem("o_ready")
        om_ready = sem("om_ready")
        ok_ready = sem("ok_ready")
        down_done = sem("down_done")
        x2_done = sem("x2_done")
        sig = sb("sig", [P, 4, CH])
        Zall = arena[:, 0:T * D].rearrange("p (t d) -> p t d", t=T)
        pool_step = sem("pool_step")
        up_ready = sem("up_ready")
        work = sb("work", [P, 4 * KF * P])
        om, ok = [[work[:, KF * P * (2 * a + i):KF * P * (2 * a + i + 1)].rearrange("p (f n) -> p f n", f=KF)
                   for i in range(2)] for a in range(2)]
        gq = [work[:, CH * f:CH * f + CH] for f in range(KF)]

        HP = S // P
        NP6 = 6 * HD
        QPOS = {"high": (0, 3, 2), "mid": (3, 2, 2), "low": (1, 1, 1)}
        KPOS = {"high": (1, 3, 1), "mid": (0, 2, 5), "low": (4, 1, 1)}
        stackT = [[arena[0:NP6, 2048 * (2 * par + w):2048 * (2 * par + w) + 2048].bitcast(BF16)
                   .rearrange("p (h n) -> p h n", h=H) for w in range(2)] for par in range(2)]
        zTb = zT[:, 0, 0:KD * S].rearrange("p (k n) -> p k n", k=KD)
        cTb = zT[:, 0, KD * S:2 * KD * S].rearrange("p (k n) -> p k n", k=KD)
        zflat = zT[:].rearrange("p k n -> p (k n)")
        stack = zflat[:, 1024:1024 + 3072].bitcast(BF16).rearrange("p (w j c d) -> p w j c d", w=2, c=6, d=HD)
        qkf = wspace[:, 0:1024].rearrange("p (w h d) -> p w h d", w=2, h=HP)
        rest = wspace[:, 1024:2048]
        VW = 32
        V = [wspace[:, 2048 + KD * H * VW * par:2048 + KD * H * VW * (par + 1)]
             .rearrange("p (k h v) -> p k h v", k=HP, v=VW) for par in range(2)]
        sigw = sig[:].rearrange("p a b -> p (a b)")
        PT = [sigw[:, 512 * k:512 * k + 512].rearrange("p (k n) -> p k n", k=HP) for k in range(2)]
        PT += [work[:].rearrange("p (a k n) -> p a k n", a=2, k=2)[:, k, :, 2 * S:3 * S] for k in range(2)]
        negT = [sigw[0:96, 1024 + 128 * k:1152 + 128 * k].bitcast(BF16) for k in range(2)]
        zz = wspace[:, 4096:4608].rearrange("p (h d) -> p h d", h=HP)
        ct = [sigw[:, 1536:2048].rearrange("p (h d) -> p h d", h=HP),
              om[0].rearrange("p a b -> p (a b)")[:, 0:512].rearrange("p (h d) -> p h d", h=HP)]
        OT = small[:, 0:4 * S].rearrange("p (g n) -> p g n", g=4)
        on = om[1].rearrange("p a b -> p (a b)")[:, 0:512].rearrange("p (h d) -> p h d", h=HP)
        oT = ok[0].rearrange("p a b -> p (a b)")[:, 0:512].rearrange("p (k n) -> p k n", k=KD)
        yo = ok[1].rearrange("p a b -> p (a b)")[:, 0:512].rearrange("p (h d) -> p h d", h=HP)
        select_row = sb("select_row", [96, H, P], BF16)
        bqk = sb("bqk", [P, 2, D])
        bvo = sb("bvo", [P, 2, D])
        negm = sb("negm", [P, HP, H])
        nst = sb("nst", [P, HP, 96], BF16)
        den = sb("den", [P, HP, H])
        b_in = sem("b_in")
        ct_in = [sem(f"ct_in{k}") for k in range(2)]
        init_ready = sem("init_ready")
        v_clear = sem("v_clear")
        zz_ready = sem("zz_ready")
        pe6, pe7, ev6, ev7 = sem("pe6"), sem("pe7"), sem("ev6"), sem("ev7")
        high_ready = sem("high_ready")
        rest_ready = sem("rest_ready")
        mid_ready = sem("mid_ready")
        low_ready = sem("low_ready")
        k_high, k_mid = sem("k_high"), sem("k_mid")
        s1_done = sem("s1_done")
        max_done = sem("max_done")
        neg_ready = sem("neg_ready")
        neg_turned = sem("neg_turned")
        negt_ready = sem("negt_ready")
        s2_done = sem("s2_done")
        e_done = sem("e_done")
        pv_done = sem("pv_done")
        ot_ready = sem("ot_ready")
        x3_done = sem("x3_done")
        st_bank = [PS[:, k, :].rearrange("p (k n) -> p k n", k=HP) for k in range(2)]
        s_bank = [PS[:, 2 + k, :].rearrange("p (h n) -> p h n", h=HP) for k in range(2)]
        side = [PS[:, 6 + k, :] for k in range(2)]

        PLAN = {1: ("turn z", "turn ctx"), 3: ("project 0", "project 1"), 5: ("back 0", "back 1"),
                7: ("turn out", "values"), 8: ("output", "parts 0"), 9: ("parts 1",),
                10: ("parts 2",), 11: ("parts 3", "parts 4"), 12: ("parts 5",), 13: ("parts 6",), 15: ("parts 7",)}
        FINISH = ("back 0", "back 1", "turn out", "output")
        FIRST = [step for h in PLAN for step in PLAN[h] if step not in FINISH]
        BANK = {"turn z": 0, "turn ctx": 1, "project 0": 0, "project 1": 1, "back 0": 0, "back 1": 1, "values": 0,
                "turn out": 1, "output": 0}
        BANK.update({f"parts {m}": 1 - m % 2 for m in range(8)})
        EARLY = T - 2 * HP
        BANK.update({f"rows {q}": 1 for q in range(T // 2)})
        BANK.update({f"logits {q}": 0 for q in range(T // 2)})
        ROUTE = {9 + q: ([f"logits {q - 1}"] if q else []) + ([f"rows {q}"] if q < EARLY // 2 else [])
                 for q in range(EARLY // 2 + 1)}
        LATE = [f"{what} {q}" for what in ("rows", "logits") for q in range(EARLY // 2, T // 2)]
        PER = [sum(BANK[step] == k for h in PLAN for step in PLAN[h]) for k in range(2)]
        LAG = 4
        NG = H // LAG

        def planned(h, before, after):
            return ([step for step in PLAN.get(h, ()) if (before if step in FINISH else after)]
                    + ([] if after else ROUTE.get(h, [])))

        def ctx_turned(u):
            n1 = sum(BANK[step] for step in FIRST)
            n = sum(BANK[step] for h in PLAN for step in PLAN[h])
            if isinstance(u, int) and u < 2:
                return 1 + n1 * u
            return 2 * n1 + n * (u - 2) + 1

        def o_part(h):
            return PS[VW * (h % 4):VW * (h % 4) + VW, 4 + h // 8, S * (h // 4 % 2):S * (h // 4 % 2) + S]

        def lagged(v, par, h, lag):
            return (v, par, h - lag) if h >= lag else (v - 1, 1 - par, h - lag + H)

        NEGB = s_bank[1].rearrange("p h n -> p (h n)")[0:96, 0:P * HP // 2].bitcast(BF16)

        def parts(w, name):
            first, n, step = (QPOS, KPOS)[w][name]
            return stack[:, w, :, first:first + step * (n - 1) + 1:step, :]

        def pair(buf, f, cc):
            return buf[:, 2 * f:2 * f + 2, ds(cc * CH, CH)]

        def unit(buf, f, cc):
            return buf[:, f, ds(cc * CH, CH)]

        E, _, F1 = A["L1_ffn_W1"].shape
        K1 = F1 // P
        J = T + E - 1
        W1 = arena[:, 8192:8192 + E * KD * F1].rearrange("p (n f) -> p n f", f=F1)
        W2 = arena[:, 8192 + E * KD * F1:8192 + E * KD * F1 + E * K1 * D].rearrange("p (n d) -> p n d", d=D)
        b1B = arena[:, 0:E * F1].rearrange("p (e f) -> p e f", e=E)
        b2B = arena[:, E * F1:E * F1 + E * D].rearrange("p (e d) -> p e d", e=E)
        Z = zflat.rearrange("p (t d) -> p t d", d=D)
        rows_zx = nc.dram_tensor("rows_zx", [N + P, 2 * D], F32, kind="Internal").ap()
        out_rows = out.rearrange("b s d -> (b s) d")
        Wr = sb("Wr", [P, KD, E])
        brB = sb("brB", [P, E])
        zero = sb("zero", [P, D])
        before = sb("before", [P, P])
        ones = sb("ones", [P, P])
        iota_e = sb("iota_e", [P, E])
        iota_j = sb("iota_j", [P, J])
        sigf = sig[:].rearrange("p a b -> p (a b)")
        zr = [wspace[:, 512 * k:512 * k + 512].rearrange("p (k n) -> p k n", k=KD) for k in range(2)]
        lg = wspace[:, 1024:1024 + T * E].rearrange("p (t e) -> p t e", e=E)
        eq, onehot, cum_a, cum_b, place = [
            sigf[:, 512 + 128 * k:640 + 128 * k].rearrange("p (t e) -> p t e", e=E) for k in range(1, 6)]
        over = sigf[:, 1280:1280 + J * E].rearrange("p (j e) -> p j e", e=E)
        top = sb("top", [P, T])
        first = sb("first", [P, T])
        tiles = sb("tiles", [P, 4, E])
        posf = sb("posf", [P, T])
        row_src = sb("row_src", [P, J], I32)
        row_dst = sb("row_dst", [P, J], I32)
        place_tile = sb("place_tile", [P, T])
        iota_r, iota_t, iota_p = zero[:, 0:P], zero[:, P:P + T], zero[:, P + T:P + T + 1]
        at_row = wspace[:, 1024:1024 + T * P // 2].bitcast(BF16).rearrange("p (t r) -> p t r", t=T)
        at_tile = wspace[:, 2048:2048 + T * 3 * (J + 1) // 2].bitcast(BF16)[:, 0:T * 3 * J]\
            .rearrange("p (t c j) -> p t c j", t=T, c=3)
        row_of = sigf[:, 1480:1480 + J]
        ef = sb("ef", [P, J])
        expert = sb("expert", [P, J], I32)
        ezx = [small[:, 2 * D * k:2 * D * (k + 1)] for k in range(2)]
        ez = [ezx[k][:, 0:D] for k in range(2)]
        xb = [om[k].rearrange("p a b -> p (a b)")[:, 0:D] for k in range(2)]
        ezT = [om[k].rearrange("p a b -> p (a b)")[:, D:2 * D].rearrange("p (k n) -> p k n", k=KD) for k in range(2)]
        ys = [om[k].rearrange("p a b -> p (a b)")[:, 2 * D:3 * D] for k in range(2)]
        hn = [ok[k].rearrange("p a b -> p (a b)")[:, 0:F1] for k in range(2)]
        hT = [wspace[:, F1 * k:F1 * k + F1].rearrange("p (f n) -> p f n", f=K1) for k in range(2)]
        e_in = sem("e_in")
        be_in = sem("be_in")
        zero_set = sem("zero_set")
        zero_out = sem("zero_out")
        zr_ready = sem("zr_ready")
        onehot_ready, rank_done, pos_ready = sem("onehot_ready"), sem("rank_done"), sem("pos_ready")
        iota_ready, places_ready, rows_done, zx_out, xb_done = (
            sem("iota_ready"), sem("places_ready"), sem("rows_done"), sem("zx_out"), sem("xb_done"))
        ez_in = [sem(f"ez_in{k}") for k in range(2)]
        et_done, et_copied, h_done, h_copied = sem("et_done"), sem("et_copied"), sem("h_done"), sem("h_copied")
        ht_done, ht_copied, y_done, y_copied = sem("ht_done"), sem("ht_copied"), sem("y_done"), sem("y_copied")
        y_out = [sem(f"y_out{k}") for k in range(2)]

        def turned_copy(copy, par, m, k):
            return copy(stackT[par][m // 4][:, 4 * (m % 4):4 * (m % 4) + 4, :].rearrange("p h n -> p (h n)"),
                        side[k][0:NP6, :].bitcast(BF16))

        @block.gpsimd
        def _(pool):
            g = Count(pool, pool_setup)
            g.mark(pool.memset(ident[:], 0.0))
            g.mark(pool.memset(causal, 0.0))
            g.wait()
            g.mark(pool.affine_select(out=ident[:], in_=ident[:], compare_op=ALU.not_equal, fill=1.0, base=0,
                                      pattern=[[-1, P]], channel_multiplier=1))
            for b in range(NB):
                cz = causal[:, PAIRS[b]:PAIRS[b + 1]].rearrange("p (q k) -> p q k", q=QR)
                g.mark(pool.affine_select(out=cz, in_=cz, compare_op=ALU.is_ge, fill=MASKED, base=QR * b,
                                          pattern=[[1, QR], [-1, QR * (b + 1)]], channel_multiplier=0))
            g.mark(pool.memset(magic[:], MAGIC))
            assert NQ % T == 0
            g.mark(pool.memset(select_row[:], 0.0))
            g.wait()
            for k in range(2):
                g.mark(pool.affine_select(out=select_row[:], in_=select_row[:], compare_op=ALU.not_equal, fill=1.0,
                                          base=-32 * k, pattern=[[-1, H], [0, P]], channel_multiplier=1))
                g.wait()
            pool.memset(zero[:], 0.0).then_inc(zero_set, 1)
            g.mark(pool.memset(before[:], 1.0))
            g.mark(pool.memset(ones[:], 1.0))
            g.wait()
            g.mark(pool.affine_select(out=before[:], in_=before[:], compare_op=ALU.is_ge, fill=0.0, base=-1,
                                      pattern=[[1, P]], channel_multiplier=-1))
            g.mark(pool.iota(iota_e[:], [[1, E]], base=0, channel_multiplier=0, allow_small_or_imprecise_dtypes=True))
            g.mark(pool.iota(iota_j[:], [[1, J]], base=0, channel_multiplier=0, allow_small_or_imprecise_dtypes=True))
            g.wait()
            pool.tensor_copy(identb[:], ident[:]).then_inc(const_ready, 1)

            pool.wait_ge(zero_out, 16)
            pool.iota(iota_r, [[1, P]], base=0, channel_multiplier=0, allow_small_or_imprecise_dtypes=True)
            pool.iota(iota_t, [[1, T]], base=0, channel_multiplier=0, allow_small_or_imprecise_dtypes=True)
            pool.iota(iota_p, [[0, 1]], base=0, channel_multiplier=1, allow_small_or_imprecise_dtypes=True)\
                .then_inc(iota_ready, 1)

            def weight_values(t, par):
                if not valid(t):
                    return
                pool.wait_ge(rinv_done, t + 1)
                pool.tensor_tensor(sm[par], sm[par], rinv[:, par, :].unsqueeze(2).broadcast_to((P, H, H)),
                                   ALU.mult).then_inc(p_ready, 1)
                wait(pool, total_done, t - 1)
                pool.wait_ge(p_ready, t + 1)
                weighted(pool, t, par, POOL_BLOCKS).then_inc(pool_product, 1)
                pool.wait_ge(pool_product, t + 1)
                add_pairs(pool, par, POOL_BLOCKS).then_inc(pv_pool, 1)

            for t in range(2):
                weight_values(t, t % 2)
            with pool.Fori(1, T // 2) as i:
                for k in range(2):
                    weight_values(2 * i + k, k)

            def all_max(k, slot):
                pool.wait_ge(amax_ready, k + 1)
                pool.partition_all_reduce(gall[:, slot:slot + 1], gmax[:, slot:slot + 1], P,
                                          RED.absmax).then_inc(gall_ready, 1)

            all_max(0, 0)
            all_max(1, 1)

            def gate_int(cc, f, u):
                pool.wait_ge(gm_ready, u + 1)
                apart(pool)
                pool.tensor_scalar(gq[f], gq[f], -MAGIC, 1.0, ALU.add, ALU.mult).then_inc(gk_ready, 1)

            def sixteen(f, u):
                pool.wait_ge(sig_ready, u + 1)
                sg = sig[:, f % 3, :]
                apart(pool)
                pool.tensor_scalar(sg, sg, 65536.0, MAGIC, ALU.mult, ALU.add).then_inc(pool_step, 1)
                pool.wait_ge(pool_step, u + 1)
                apart(pool)
                pool.tensor_scalar(sg, sg, -MAGIC, 1.0, ALU.add, ALU.mult).then_inc(n_ready, 1)

            def up_step(cc, f, u, before=True):
                gate_int(cc, f, u)
                if before:
                    sixteen((f - 2) % KF, u - 2)

            for f in range(KF):
                up_step(0, f, f, before=f > 1)
            with pool.Fori(1, NCH) as cc:
                for f in range(KF):
                    up_step(cc, f, cc * KF + f)
            for f in (KF - 2, KF - 1):
                sixteen(f, UNITS - KF + f)
            all_max(2, 3)
            all_max(3, 2)
            pool.wait_ge(scale_ready, 3)
            for cc in range(NCH):
                for f in range(KF // 2):
                    u = cc * (KF // 2) + f
                    v = pair(U, f, cc)
                    pool.tensor_scalar(v, v, qs[:, 5:6], magic[:], ALU.mult, ALU.add).then_inc(up_ready, 1)
                    pool.wait_ge(up_ready, 2 * u + 1)
                    pool.tensor_scalar(v, v, -MAGIC, 1.0, ALU.add, ALU.mult).then_inc(up_ready, 1)
            all_max(4, 0)

            pool.wait_ge(x2_done, T)
            pool.memset(wspace[:, 2048:2048 + 2 * KD * H * VW], 0.0).then_inc(v_clear, 1)
            pool.wait_ge(v_clear, 1)
            for par in range(2):
                pool.memset(V[par][:, :, :, HD:HD + 1], 1.0).then_inc(init_ready, 1)
            steps = Steps(), Steps()

            def key_parts(v):
                pool.wait_ge(ev6, steps[0].now())
                pool.wait_ge(ev7, steps[1].now())
                apart(pool)
                pool.tensor_copy(parts(1, "high"), qkf[:, 1].rearrange("p h (j d) -> p (h j) d", d=HD).unsqueeze(2)
                                 .broadcast_to((P, HP * H, 3, HD))).then_inc(k_high, 1)
                pool.wait_ge(rest_ready, 2 * v + 2)
                apart(pool)
                pool.tensor_copy(parts(1, "mid"), rest[:, 512:1024].rearrange("p (j d) -> p j d", d=HD)
                                 .unsqueeze(2).broadcast_to((P, HP * H, 2, HD))).then_inc(k_mid, 1)

            def round_(v, before=True, after=True):
                for h in range(H):
                    for step in planned(h, before, after):
                        steps[BANK[step]].next()
                    if after and h == 4:
                        key_parts(v + 1)

            for step in FIRST:
                steps[BANK[step]].next()
            round_(0, before=False)
            with pool.Fori(0, B // 2 - 1) as i:
                for k in range(2):
                    steps[k].enter(i, 2 * PER[k])
                round_(2 * i + 1)
                round_(2 * i + 2)
                for k in range(2):
                    steps[k].leave(B // 2 - 1)

            pool.wait_ge(pos_ready, 1)
            pool.wait_ge(zx_out, 16 * 8)
            for j in range(J + 4):
                if j < J:
                    wait(pool, et_done, j - 1)
                    wait(pool, xb_done, j - 1)
                    pool.indirect_dma_start(ezx[j % 2], None, rows_zx,
                                            bass.IndirectOffsetOnAxis(ap=row_src[:, j:j + 1], axis=0))\
                        .then_inc(ez_in[j % 2], 16)
                if j >= 4:
                    pool.wait_ge(y_copied, j - 3)
                    pool.indirect_dma_start(out_rows, bass.IndirectOffsetOnAxis(ap=row_dst[:, j - 4:j - 3], axis=0),
                                            ys[j % 2], None, bounds_check=N - 1, oob_is_err=False)\
                        .then_inc(y_out[j % 2], 16)
            pool.wait_ge(y_out[0], 16 * ((J + 1) // 2))
            pool.wait_ge(y_out[1], 16 * (J // 2))

        @block.sync
        def _(sp):
            for q in range(4):
                sp.dma_start(X[:, 4 * q:4 * q + 4, :], x_dram[:, 4 * q:4 * q + 4, :]).then_inc(x_in[q], 16)
            for q in range(4):
                sp.dma_start(C[:, 4 * q:4 * q + 4, :], ctx_dram[:, 4 * q:4 * q + 4, :]).then_inc(c_in[q], 16)
            sp.dma_start(rawg, A["L0_ffn_w_gate"].rearrange("(f p) i -> p f i", p=P)).then_inc(w_in, 16)
            sp.dma_start(rawu, A["L0_ffn_w_up"].rearrange("(f p) i -> p f i", p=P)).then_inc(w_in, 16)
            sp.dma_start(rawd, A["L0_ffn_w_down"].rearrange("(o p) i -> p o i", p=P)).then_inc(w_in, 16)
            for k, name in enumerate(("Wq", "Wk", "Wv", "Wo")):
                sp.dma_start(rawa[:, k], A["L1_xattn_" + name].rearrange("(o p) i -> p o i", p=P)).then_inc(wa_in, 16)

            for k, name in enumerate(("bq", "bk")):
                sp.dma_start(bqk[:, k, :], A["L1_xattn_" + name].partition_broadcast(P)).then_inc(b_in, 16)
            for k, name in enumerate(("bv", "bo")):
                sp.dma_start(bvo[:, k, :], A["L1_xattn_" + name].partition_broadcast(P)).then_inc(b_in, 16)

            sp.dma_start(Wr[:], A["L1_ffn_Wr"].rearrange("(k p) e -> p k e", p=P)).then_inc(b_in, 16)
            sp.dma_start(brB[:], A["L1_ffn_br"].partition_broadcast(P)).then_inc(b_in, 16)
            sp.wait_ge(zero_set, 1)
            sp.dma_start(rows_zx[N:N + P, :].rearrange("p (c d) -> p c d", c=2),
                         zero[:].unsqueeze(1).broadcast_to((P, 2, D)))\
              .then_inc(zero_out, 16)

            def load_ctx(b, par):
                if not (isinstance(b, int) and b < 2):
                    sp.wait_ge(pe7, ctx_turned(b - 2))
                sp.dma_start(ct[par], ctx_dram[:, ds(HP * b, HP), :]).then_inc(ct_in[par], 16)

            sp.wait_ge(x2_done, T)
            load_ctx(0, 0)
            load_ctx(1, 1)
            w1_dram = A["L1_ffn_W1"].rearrange("e (k p) f -> p (e k) f", p=P)
            w2_dram = A["L1_ffn_W2"].rearrange("e (k p) d -> p (e k) d", p=P)
            sp.dma_start(W1, w1_dram).then_inc(e_in, 16)
            sp.dma_start(W2, w2_dram).then_inc(e_in, 16)
            load_ctx(2, 0)
            load_ctx(3, 1)
            with sp.Fori(2, B // 2) as i:
                load_ctx(2 * i, 0)
                load_ctx(2 * i + 1, 1)

            zx = rows_zx[0:N, :].rearrange("(t p) d -> p t d", p=P)

            def store_rows(q):
                sp.wait_ge(x3_done, B - 2 if q < EARLY // 4 else B)
                sp.dma_start(zx[:, 4 * q:4 * q + 4, D:2 * D], X[:, 4 * q:4 * q + 4, :]).then_inc(zx_out, 16)
                sp.wait_ge(zr_ready, 4 * q + 4)
                sp.dma_start(zx[:, 4 * q:4 * q + 4, 0:D], Z[:, 4 * q:4 * q + 4, :]).then_inc(zx_out, 16)

            for q in range(EARLY // 4):
                store_rows(q)
            sp.wait_ge(e_done, H * B)
            sp.dma_start(b1B.rearrange("p e f -> p (e f)"),
                         A["L1_ffn_b1"].rearrange("e f -> (e f)").partition_broadcast(P)).then_inc(be_in, 16)
            sp.dma_start(b2B.rearrange("p e d -> p (e d)"),
                         A["L1_ffn_b2"].rearrange("e d -> (e d)").partition_broadcast(P)).then_inc(be_in, 16)

            for q in range(EARLY // 4, 4):
                store_rows(q)

        TW = [(attnT[:, w, i, P * o:P * o + P], rawa[:, w, o, P * i:P * i + P])
              for w in range(4) for i in range(KD) for o in range(KD)]
        NA = len(TW) // 4
        for dst, src in ((gateT, rawg), (upT, rawu)):
            TW += [(dst[:, i, P * f:P * f + P], src[:, f, P * i:P * i + P]) for i in range(KD) for f in range(KF)]
        TW += [(downT[:, f, P * o:P * o + P], rawd[:, o, P * f:P * f + P]) for f in range(KF) for o in range(KD)]
        NW = len(TW) // 4
        flat = {0: attnT[:].rearrange("p w i o -> p (w i o)"), NA * 512: gateT.rearrange("p i f -> p (i f)"),
                NA * 512 + KD * F0: upT.rearrange("p i f -> p (i f)"),
                NA * 512 + 2 * KD * F0: downT.rearrange("p f o -> p (f o)")}

        def weight_group(n):
            start = max(s for s in flat if s <= 512 * n)
            return flat[start][:, 512 * n - start:512 * n - start + 512]

        @block.scalar
        def _(act):
            act.wait_ge(var_ready, 1)
            act.activation(rstd[:], var[:], ACT.Sqrt).then_inc(sd_ready, 1)

            def z_tile(t, par):
                if not valid(t):
                    return
                wait(act, prod_done, t - 1)
                act.activation(z[par][:], X[:, ds(t, 1), :].rearrange("p a d -> p (a d)"), ACT.Identity,
                               bias=shift[:, ds(t, 1)], scale=rstd[:, ds(t, 1)]).then_inc(z0_done, 1)

            def unpack(t, par):
                if not valid(t):
                    return
                act.wait_ge(sum_done, t + 1)
                wait(act, less_max_ready, t - 1)
                for b in range(NB):
                    ins = act.activation(sraw[par][:, QR * b:QR * (b + 1), 0:QR * (b + 1)],
                                         PS[:, par, PAIRS[b]:PAIRS[b + 1]].rearrange("p (q k) -> p q k", q=QR),
                                         ACT.Identity, scale=float(HD) ** -0.5)
                ins.then_inc(raw_done, 1)

            def exp(t, par):
                if valid(t):
                    act.wait_ge(less_max_ready, t + 1)
                    act.activation(sm[par], sm[par], ACT.Exp).then_inc(exp_ready, 1)

            def keep(t, par):
                if valid(t):
                    act.wait_ge(total_done, t + 1)
                    act.activation(X[:, ds(t, 1), :].rearrange("p a d -> p (a d)"), PS[:, 2 + par, 0:D],
                                   ACT.Identity).then_inc(x1_done, 1)

            def step(i, k):
                unpack(i - 1, 1 - k)
                z_tile(i + 1, 1 - k)
                exp(i - 1, 1 - k)
                keep(i - 3, 1 - k)

            act.wait_ge(shift_ready, 1)
            act.wait_ge(init_ready, 1)
            z_tile(0, 0)
            for i in range(FILL):
                step(i, i % 2)
            with act.Fori(FILL // 2, T // 2 - 1) as i:
                for k in range(2):
                    step(2 * i + k, k)

            def copy_weights(n):
                act.wait_ge(wt_done, n + 1)
                act.copy(weight_group(n), PS[:, 4 + n % 4, :]).then_inc(wt_copied, 1)

            for i in range(T - 2, T + 1):
                step(i, i % 2)
            for n in range(NA):
                copy_weights(n)
            for i in range(T + 1, T + FILL):
                step(i, i % 2)

            act.wait_ge(var_ready, 2)
            act.activation(rstd[:], var[:], ACT.Sqrt).then_inc(sd_ready, 1)
            for n in range(NA, NW):
                copy_weights(n)
            for h in range(T // 2):
                act.wait_ge(zt_done, h + 1)
                act.copy(zT[:, :, h * 2 * P:(h + 1) * 2 * P],
                         PS[:, h % 4, :].rearrange("p (k n) -> p k n", k=KD)).then_inc(zt_copied, 1)
            act.wait_ge(scale_ready, 1)
            act.wait_ge(zt_copied, T // 2)
            for cc in range(NCH):
                v = zT[:, :, cc * CH:cc * CH + CH]
                act.activation(v, v, ACT.Identity, bias=magic[:], scale=qs[:, 1:2]).then_inc(xm_ready, 1)

            def evacuate(buf, u, cc, f):
                act.wait_ge(mm_done, u + 1)
                apart(act)
                act.activation(unit(buf, f, cc), PS[:, f, :], ACT.Copy, scale=qs[:, 0:1]).then_inc(mm_copied, 1)

            with act.Fori(0, NCH) as cc:
                for f in range(KF):
                    evacuate(G, cc * KF + f, cc, f)
            act.wait_ge(scale_ready, 2)
            act.wait_ge(mm_copied, UNITS)

            def gate_part(cc, f, u):
                wait(act, g2_ready, u - KF + 1)
                act.activation(gq[f], unit(G, f, cc), ACT.Identity, bias=magic[:], scale=qs[:, 3:4])\
                   .then_inc(gm_ready, 1)

            def sigmoid(cc, f, u):
                act.wait_ge(gk_ready, u + 1)
                wait(act, g2_ready, u - 2)
                apart(act)
                act.activation(sig[:, f % 3, :], gq[f], ACT.Sigmoid, scale=qs[:, 2:3]).then_inc(sig_ready, 1)

            def up_step(cc, f, u, before=True):
                evacuate(U, UNITS + u, cc, f)
                gate_part(cc, f, u)
                if before:
                    sigmoid(cc if f else cc - 1, (f - 1) % KF, u - 1)

            for f in range(KF):
                up_step(0, f, f, before=f > 0)
            with act.Fori(1, NCH) as cc:
                for f in range(KF):
                    up_step(cc, f, cc * KF + f)
            sigmoid(NCH - 1, KF - 1, UNITS - 1)

            act.wait_ge(scale_ready, 4)
            act.wait_ge(mm_copied, 2 * UNITS)
            with act.Fori(0, NCH) as cc:
                for f in range(KF // 2):
                    v = pair(G, f, cc)
                    act.activation(v, v, ACT.Identity, bias=magic[:], scale=qs[:, 7:8]).then_inc(pm_ready, 1)
            act.wait_ge(scale_ready, 5)

            def product(i, par):
                t = 2 * i + par
                wait(act, ok_ready, t - 1)
                apart(act)
                act.activation(om[par], G[:, :, ds(t * P, P)], ACT.Identity, bias=magic[:],
                               scale=qs[:, 9:10]).then_inc(om_ready, 1)

            product(0, 0)
            product(0, 1)
            with act.Fori(1, T // 2) as i:
                product(i, 0)
                product(i, 1)

            act.wait_ge(var_ready, 3)
            act.activation(rstd[:], var[:], ACT.Sqrt).then_inc(sd_ready, 1)

            steps = Steps(), Steps()
            pe_side, ev_side = (pe6, pe7), (ev6, ev7)

            def side_step(step, v, par):
                k = BANK[step]
                n = steps[k].next()
                if step == "turn z":
                    act.wait_ge(pe6, n)
                    act.copy(zTb, side[0].rearrange("p (k n) -> p k n", k=KD)).then_inc(ev6, 1)
                elif step == "turn ctx":
                    act.wait_ge(pe7, n)
                    act.copy(cTb, side[1].rearrange("p (k n) -> p k n", k=KD)).then_inc(ev7, 1)
                elif step == "turn out":
                    act.wait_ge(pe7, n)
                    act.copy(oT, side[1].rearrange("p (k n) -> p k n", k=KD)).then_inc(ev7, 1)
                elif step.startswith("rows"):
                    act.wait_ge(pe7, n)
                    act.copy(zr[int(step[5:]) % 2], side[1].rearrange("p (k n) -> p k n", k=KD)).then_inc(ev7, 1)
                elif step.startswith("parts") and k == 1:
                    act.wait_ge(pe7, n)
                    turned_copy(act.copy, par, int(step[6:]), 1).then_inc(ev7, 1)

            def high_parts(h):
                act.wait_ge(ev6, steps[0].now())
                act.wait_ge(ev7, steps[1].now())
                act.copy(parts(0, "high")[:, H * h:H * (h + 1)], qkf[:, 0, h].rearrange("p (j d) -> p j d", d=HD)
                         .unsqueeze(2).broadcast_to((P, H, 3, HD))).then_inc(high_ready, 1)

            def mid_parts(v):
                act.wait_ge(rest_ready, 2 * v + 1)
                act.copy(parts(0, "mid"), rest[:, 0:512].rearrange("p (j d) -> p j d", d=HD)
                         .unsqueeze(2).broadcast_to((P, HP * H, 2, HD))).then_inc(mid_ready, 1)

            def deviation(k, a=0, b=T):
                act.wait_ge(var_ready, k)
                act.activation(rstd[:, a:b], var[:, a:b], ACT.Sqrt).then_inc(sd_ready, 1)

            def exp(b, h):
                c = H * b + h
                act.wait_ge(s2_done, c + 1)
                wait(act, pv_done, c - 3)
                act.activation(PT[h % 4], st_bank[h % 2], ACT.Exp, scale=float(HD) ** -0.5).then_inc(e_done, 1)

            def take_half(b, half):
                act.wait_ge(pv_done, H * b + 8 * (half + 1))
                act.copy(OT[:, 2 * half:2 * half + 2, :].rearrange("p g n -> p (g n)"), PS[:, 4 + half, :])\
                   .then_inc(ot_ready, 1)

            def round_(v, par, before=True, after=True):
                for h in range(H):
                    b, _, hb = lagged(v, par, h, LAG)
                    if h == 4 and before:
                        take_half(v - 1, 1)
                    if h >= LAG or before:
                        exp(b, hb)
                    if not after and h == 2:
                        deviation(4, 0, EARLY)
                    for step in planned(h, before, after):
                        side_step(step, v + 1, 1 - par)
                    if after and h in (3, 4):
                        high_parts(h - 3)
                    if after and h == 6:
                        mid_parts(v + 1)
                    if h == 12:
                        take_half(v, 0)

            for step in FIRST:
                side_step(step, 0, 0)
                if step == "project 1":
                    for h in range(HP):
                        high_parts(h)
                    act.copy(parts(1, "high"), qkf[:, 1].rearrange("p h (j d) -> p (h j) d", d=HD).unsqueeze(2)
                             .broadcast_to((P, HP * H, 3, HD))).then_inc(k_high, 1)
                    mid_parts(0)
                    act.wait_ge(rest_ready, 2)
                    act.copy(parts(1, "mid"), rest[:, 512:1024].rearrange("p (j d) -> p j d", d=HD)
                             .unsqueeze(2).broadcast_to((P, HP * H, 2, HD))).then_inc(k_mid, 1)
            round_(0, 0, before=False)
            with act.Fori(0, B // 2 - 1) as i:
                for k in range(2):
                    steps[k].enter(i, 2 * PER[k])
                round_(2 * i + 1, 1)
                round_(2 * i + 2, 0)
                for k in range(2):
                    steps[k].leave(B // 2 - 1)
            round_(B - 1, 1, after=False)
            for h in range(H - LAG, H):
                exp(B - 1, h)
            take_half(B - 1, 1)
            for step in FINISH:
                side_step(step, B + 1, 1)

            deviation(5, EARLY, T)
            for step in LATE:
                side_step(step, 0, 0)

            def rows(j, par):
                act.wait_ge(et_done, j + 1)
                wait(act, h_done, j - 1)
                act.copy(ezT[par], PS[:, par, 0:D].rearrange("p (k n) -> p k n", k=KD)).then_inc(et_copied, 1)

            def hidden(j, par):
                act.wait_ge(ht_done, j + 1)
                wait(act, y_done, j - 1)
                act.activation(hT[par], PS[:, 4 + par, :].rearrange("p (f n) -> p f n", f=K1), ACT.Relu)\
                   .then_inc(ht_copied, 1)

            rows(0, 0)
            rows(1, 1)
            hidden(0, 0)
            rows(2, 0)
            hidden(1, 1)
            with act.Fori(1, J // 2) as i:
                rows(2 * i + 1, 1)
                hidden(2 * i, 0)
                rows(2 * i + 2, 0)
                hidden(2 * i + 1, 1)
            hidden(J - 1, 0)

        @block.vector
        def _(dve):
            st = Count(dve, dve_step)

            def norm_stats(k, a=0, b=T):
                st.wait()
                mean_, tmp_, var_, rstd_ = mean[:, a:b], tmp[:, a:b], var[:, a:b], rstd[:, a:b]
                st.mark(dve.tensor_tensor(mean_, stats[:, a:b, 1], stats[:, a:b, 4], ALU.add))
                st.mark(dve.tensor_tensor(tmp_, stats[:, a:b, 1], stats[:, a:b, 4], ALU.subtract))
                st.mark(dve.tensor_tensor(var_, stats[:, a:b, 2], stats[:, a:b, 5], ALU.add))
                st.wait()
                st.mark(dve.tensor_tensor(tmp_, tmp_, tmp_, ALU.mult))
                st.mark(dve.tensor_scalar(mean_, mean_, 0.5, None, ALU.mult))
                st.mark(dve.tensor_scalar(var_, var_, 1.0 / D, EPS, ALU.mult, ALU.add))
                st.wait()
                dve.scalar_tensor_tensor(out=var_, in0=tmp_, scalar=0.25, in1=var_, op0=ALU.mult,
                                         op1=ALU.add).then_inc(var_ready, 1)
                dve.wait_ge(sd_ready, k)
                st.mark(dve.reciprocal(rstd_, rstd_))
                st.wait()
                st.mark(dve.tensor_tensor(tmp_, rstd_, rstd_, ALU.mult))
                st.wait()
                st.mark(dve.tensor_tensor(tmp_, tmp_, var_, ALU.mult))
                st.wait()
                st.mark(dve.tensor_scalar(tmp_, tmp_, -0.5, 1.5, ALU.mult, ALU.add))
                st.wait()
                st.mark(dve.tensor_tensor(rstd_, rstd_, tmp_, ALU.mult))
                st.wait()

            def normalise(t, dst):
                return dve.tensor_scalar(dst, X[:, ds(t, 1), :].rearrange("p a d -> p (a d)"), mean[:, ds(t, 1)],
                                         rstd[:, ds(t, 1)], ALU.subtract, ALU.mult)

            def x_tile(t):
                return X[:, ds(t, 1), :].rearrange("p a d -> p (a d)")

            for k in range(2):
                ins = dve.memset(sraw[k], MASKED)
            ins.then_inc(init_ready, 1)
            for t in range(T):
                if t % 4 == 0:
                    dve.wait_ge(x_in[t // 4], 16)
                st.mark(dve.bn_stats(stats[:, t, :], X[:, t, :]))
            norm_stats(1)
            dve.scalar_tensor_tensor(out=shift[:], in0=mean[:], scalar=-1.0, in1=rstd[:], op0=ALU.mult,
                                     op1=ALU.mult).then_inc(shift_ready, 1)
            for q in range(4):
                dve.wait_ge(c_in[q], 16)

            def products(t, par):
                if not valid(t):
                    return
                dve.wait_ge(z0_done, t + 1)
                wait(dve, sum_done, t - 1)
                zt = z[par][:].rearrange("p (q d) -> p q d", q=H)
                for b in range(NB):
                    nk = QR * (b + 1)
                    ins = dve.tensor_tensor(
                        pairs(par, b), zt[:, QR * b:QR * b + QR, :].unsqueeze(2).broadcast_to((P, QR, nk, HD)),
                        ctx_tile(t, nk).unsqueeze(1).broadcast_to((P, QR, nk, HD)), ALU.mult)
                ins.then_inc(prod_done, 1)

            def bn(t):
                if valid(t):
                    dve.wait_ge(x1_done, t + 1)
                    dve.bn_stats(stats[:, ds(t, 1), :].rearrange("p a d -> p (a d)"), x_tile(t)).then_inc(bn_ready, 1)

            GC = NQ // T

            def step(i, k):
                c, t, par = i - FILL, i - 1, 1 - k
                if valid(c):
                    chunk = raw[:, ds(GC * c, GC), :]
                    ws, wi = wscale[:, ds(GC * c, GC)], winv[:, ds(GC * c, GC)]
                    w = st.mark(dve.tensor_reduce(ws, chunk, AX.X, ALU.max, apply_absolute_value=True))
                products(i, k)
                if valid(c):
                    dve.wait_ge(dve_step, w)
                    w = st.mark(dve.tensor_scalar(ws, ws, 1.0 / 7.0, 1e-12, ALU.mult, ALU.max))
                if valid(t):
                    dve.wait_ge(raw_done, t + 1)
                    m = st.mark(dve.tensor_reduce(rmax[:], sraw[par], AX.X, ALU.max))
                if valid(c):
                    dve.wait_ge(dve_step, w)
                    w = st.mark(dve.reciprocal(wi, ws))
                if valid(t):
                    dve.wait_ge(dve_step, m)
                    wait(dve, pv_pool, t - 1)
                    dve.tensor_tensor(sm[par], sraw[par], rmax[:].unsqueeze(2).broadcast_to((P, H, H)),
                                      ALU.subtract).then_inc(less_max_ready, 1)
                if valid(c):
                    dve.wait_ge(dve_step, w)
                    w = st.mark(dve.tensor_tensor(chunk, chunk, wi.unsqueeze(2).broadcast_to((P, GC, QB)), ALU.mult))
                if valid(i - 2):
                    dve.wait_ge(p_ready, i - 1)
                    wait(dve, total_done, i - 3)
                    v = st.mark(weighted(dve, i - 2, k, DVE_BLOCKS))
                if valid(c):
                    dve.wait_ge(dve_step, w)
                    w = st.mark(dve.tensor_scalar(chunk, chunk, MAGIC, MAGIC, ALU.add, ALU.subtract))
                if valid(t):
                    dve.wait_ge(exp_ready, t + 1)
                    m = st.mark(dve.tensor_reduce(rsum[:], sm[par], AX.X, ALU.add))
                if valid(i - 2):
                    dve.wait_ge(dve_step, v)
                    add_pairs(dve, k, DVE_BLOCKS).then_inc(pv_dve, 1)
                if valid(c):
                    dve.wait_ge(dve_step, w)
                    dve.tensor_tensor(chunk, chunk, ws.unsqueeze(2).broadcast_to((P, GC, QB)),
                                      ALU.mult).then_inc(w_ready, 1)
                if valid(t):
                    dve.wait_ge(dve_step, m)
                    wait(dve, p_ready, t - 1)
                    dve.reciprocal(rinv[:, par, :], rsum[:]).then_inc(rinv_done, 1)
                bn(i - FILL)

            for i in range(FILL):
                step(i, i % 2)
            dve.wait_ge(w_in, 48)
            with dve.Fori(FILL // 2, T // 2 - 1) as i:
                st.enter(i, FILL // 2, 2 * 8)
                for k in range(2):
                    step(2 * i + k, k)
                st.leave(T // 2 - 1 - FILL // 2)
            for i in range(T - 2, T + FILL):
                step(i, i % 2)
            dve.wait_ge(bn_ready, T)

            norm_stats(2)

            for t in range(T):
                normalise(t, Zall[:, t, :]).then_inc(z_ready, 1)
                if t % 4 == 3:
                    dve.wait_ge(z_ready, t + 1)
                    st.mark(dve.tensor_reduce(amax[:, 0, t // 4:t // 4 + 1], Zall[:, t - 3:t + 1, :], AX.XY, ALU.max,
                                              apply_absolute_value=True))
            st.wait()

            def quant_scale(k, slot, n, factor=None):
                dve.tensor_reduce(gmax[:, slot:slot + 1], amax[:, slot, 0:n], AX.X, ALU.max).then_inc(amax_ready, 1)
                dve.wait_ge(gall_ready, k + 1)
                s, inv = qs[:, 2 * k:2 * k + 1], qs[:, 2 * k + 1:2 * k + 2]
                if factor is not None:
                    st.mark(dve.tensor_tensor(gall[:, slot:slot + 1], gall[:, slot:slot + 1], factor, ALU.mult))
                    st.wait()
                st.mark(dve.tensor_scalar(s, gall[:, slot:slot + 1], 1.0 / QMAX, 1e-12, ALU.mult, ALU.max))
                st.wait()
                if factor is None:
                    dve.reciprocal(inv, s).then_inc(scale_ready, 1)
                else:
                    st.mark(dve.reciprocal(inv, s))
                    st.wait()
                    dve.tensor_tensor(inv, inv, factor, ALU.mult).then_inc(scale_ready, 1)

            quant_scale(0, 0, T // 4)
            for cc in range(NCH):
                dve.wait_ge(xm_ready, cc + 1)
                v = zT[:, :, cc * CH:cc * CH + CH]
                dve.tensor_scalar(v, v, MAGIC, None, ALU.subtract).then_inc(xq_ready, 1)

            def largest(slot, buf, u, cc, f):
                dve.wait_ge(mm_copied, u + 1)
                dve.tensor_reduce(amax[:, slot, ds(cc * KF + f, 1)], unit(buf, f, cc), AX.X, ALU.max,
                                  apply_absolute_value=True).then_inc(mm_maxed, 1)

            with dve.Fori(0, NCH) as cc:
                for f in range(KF):
                    largest(1, G, cc * KF + f, cc, f)
            dve.wait_ge(mm_maxed, UNITS)
            dve.tensor_reduce(gmax[:, 1:2], amax[:, 1, 0:UNITS], AX.X, ALU.max).then_inc(amax_ready, 1)
            dve.wait_ge(gall_ready, 2)
            st.mark(dve.tensor_scalar(qs[:, 2:3], gall[:, 1:2], 1.0 / QMAX, 1e-12, ALU.mult, ALU.max))
            st.wait()
            dve.reciprocal(qs[:, 3:4], qs[:, 2:3]).then_inc(scale_ready, 1)

            def gated(cc, f, u):
                dve.wait_ge(n_ready, u + 1)
                dve.scalar_tensor_tensor(out=unit(G, f, cc), in0=sig[:, f % 3, :], scalar=65535.0, in1=gq[f],
                                         op0=ALU.min, op1=ALU.mult).then_inc(g2_ready, 1)

            def gated_max(cc, f, u):
                dve.wait_ge(g2_ready, u + 1)
                st.mark(dve.tensor_reduce(amax[:, 2, ds(u, 1)], unit(G, f, cc), AX.X, ALU.max,
                                          apply_absolute_value=True))

            def up_step(cc, f, u, before=True):
                late = cc if f > 2 else cc - 1, (f - 3) % KF, u - 3
                if before:
                    gated(*late)
                largest(3, U, UNITS + u, cc, f)
                if before:
                    gated_max(*late)

            for f in range(KF):
                up_step(0, f, f, before=f > 2)
            with dve.Fori(1, NCH) as cc:
                st.enter(cc, 1, KF)
                for f in range(KF):
                    up_step(cc, f, cc * KF + f)
                st.leave(NCH - 1)
            dve.wait_ge(mm_maxed, 2 * UNITS)
            dve.tensor_reduce(gmax[:, 3:4], amax[:, 3, 0:UNITS], AX.X, ALU.max).then_inc(amax_ready, 1)
            for f in (KF - 3, KF - 2, KF - 1):
                gated(NCH - 1, f, UNITS - KF + f)
                gated_max(NCH - 1, f, UNITS - KF + f)
            st.wait()
            st.mark(dve.tensor_scalar(qs[:, 11:12], qs[:, 2:3], 2.0 ** -16, None, ALU.mult))
            dve.tensor_reduce(gmax[:, 2:3], amax[:, 2, 0:UNITS], AX.X, ALU.max).then_inc(amax_ready, 1)
            dve.wait_ge(gall_ready, 4)
            st.wait()
            st.mark(dve.tensor_tensor(gall[:, 2:3], gall[:, 2:3], qs[:, 11:12], ALU.mult))
            st.wait()
            st.mark(dve.tensor_scalar(qs[:, 6:7], gall[:, 2:3], 1.0 / QMAX, 1e-12, ALU.mult, ALU.max))
            st.mark(dve.tensor_scalar(qs[:, 4:5], gall[:, 3:4], 1.0 / QMAX, 1e-12, ALU.mult, ALU.max))
            st.wait()
            st.mark(dve.reciprocal(qs[:, 7:8], qs[:, 6:7]))
            dve.reciprocal(qs[:, 5:6], qs[:, 4:5]).then_inc(scale_ready, 1)
            st.wait()
            dve.tensor_tensor(qs[:, 7:8], qs[:, 7:8], qs[:, 11:12], ALU.mult).then_inc(scale_ready, 1)

            def join(cc, f, u):
                dve.wait_ge(pm_ready, u + 1)
                dve.wait_ge(up_ready, 2 * u + 2)
                vg = pair(G, f, cc)
                dve.scalar_tensor_tensor(out=vg, in0=vg, scalar=MAGIC, in1=pair(U, f, cc), op0=ALU.subtract,
                                         op1=ALU.mult).then_inc(j_ready, 1)

            def join_max(cc, f, u):
                dve.wait_ge(j_ready, u + 1)
                dve.tensor_reduce(amax[:, 0, ds(u, 1)], pair(G, f, cc), AX.XY, ALU.max,
                                  apply_absolute_value=True).then_inc(o_ready, 1)

            def joined(cc, f, first=False):
                u = cc * (KF // 2) + f
                join(cc, f, u)
                if not first:
                    join_max(cc if f else cc - 1, (f - 1) % (KF // 2), u - 1)

            for f in range(KF // 2):
                joined(0, f, first=(f == 0))
            with dve.Fori(1, NCH) as cc:
                for f in range(KF // 2):
                    joined(cc, f)
            join_max(NCH - 1, KF // 2 - 1, UNITS // 2 - 1)
            st.mark(dve.tensor_tensor(qs[:, 12:13], qs[:, 4:5], qs[:, 6:7], ALU.mult))
            st.wait()
            dve.wait_ge(o_ready, UNITS // 2)
            quant_scale(4, 0, UNITS // 2, factor=qs[:, 12:13])

            def product_int(i, par):
                t = 2 * i + par
                dve.wait_ge(om_ready, t + 1)
                wait(dve, down_done, t - 1)
                dve.tensor_scalar(ok[par], om[par], MAGIC, None, ALU.subtract).then_inc(ok_ready, 1)

            def residual(t, par):
                dve.wait_ge(down_done, t + 1)
                dve.scalar_tensor_tensor(out=x_tile(t), in0=PS[:, 6 + par, 0:D], scalar=qs[:, 8:9], in1=x_tile(t),
                                         op0=ALU.mult, op1=ALU.add).then_inc(x2_done, 1)
                dve.wait_ge(x2_done, t + 1)
                st.mark(dve.bn_stats(stats[:, ds(t, 1), :].rearrange("p a d -> p (a d)"), x_tile(t)))

            product_int(0, 0)
            product_int(0, 1)
            residual(0, 0)
            with dve.Fori(1, T // 2) as i:
                st.enter(i, 1, 2)
                product_int(i, 0)
                residual(2 * i - 1, 1)
                product_int(i, 1)
                residual(2 * i, 0)
                st.leave(T // 2 - 1)
            residual(T - 1, 1)

            dve.memset(nst[:], 0.0).then_inc(init_ready, 1)
            norm_stats(3)
            dve.wait_ge(b_in, 96)

            steps = Steps(), Steps()
            pe_side, ev_side = (pe6, pe7), (ev6, ev7)

            def zs(b):
                wait(dve, pe6, steps[0].now())
                for h in range(HP):
                    ins = dve.tensor_scalar(zz[:, h, :], x_tile(HP * b + h), mean[:, ds(HP * b + h, 1)],
                                            rstd[:, ds(HP * b + h, 1)], ALU.subtract, ALU.mult)
                ins.then_inc(zz_ready, 1)

            def side_step(step, v, par):
                k = BANK[step]
                n = steps[k].next()
                if step in ("project 0", "project 1"):
                    wait(dve, high_ready, HP * v)
                    wait(dve, k_high, v)
                    dve.wait_ge(pe_side[k], n)
                    dve.tensor_tensor(qkf[:, :, k, :], side[k].rearrange("p (w d) -> p w d", w=2), bqk[:], ALU.add)\
                       .then_inc(ev_side[k], 1)
                elif step == "values":
                    dve.wait_ge(pe6, n)
                    if isinstance(v, int) and v == 0:
                        dve.wait_ge(init_ready, 4)
                    dve.tensor_tensor(V[par][:, :, :, 0:HD], side[0].rearrange("p (k h d) -> p k h d", k=HP, h=H),
                                      bvo[:, 0, :].rearrange("p (h d) -> p h d", h=H).unsqueeze(1)
                                      .broadcast_to((P, HP, H, HD)), ALU.add).then_inc(ev6, 1)
                elif step in ("back 0", "back 1"):
                    dve.wait_ge(pe_side[k], n)
                    o = side[k].rearrange("p (h v) -> p h v", v=VW)
                    st.mark(dve.reciprocal(den[:, k, :], o[:, :, HD]))
                    st.wait()
                    dve.tensor_tensor(on[:, k, :].rearrange("p (j d) -> p j d", d=HD), o[:, :, 0:HD],
                                      den[:, k, :].unsqueeze(2).broadcast_to((P, H, HD)), ALU.mult)\
                       .then_inc(ev_side[k], 1)
                elif step == "output":
                    dve.wait_ge(pe6, n)
                    dve.tensor_tensor(yo, side[0].rearrange("p (h d) -> p h d", h=HP),
                                      bvo[:, 1:2, :].broadcast_to((P, HP, D)), ALU.add).then_inc(ev6, 1)
                    dve.wait_ge(ev6, n)
                    xb = X[:, ds(HP * (v - 2), HP), :]
                    dve.tensor_tensor(xb, xb, yo, ALU.add).then_inc(x3_done, 1)
                    dve.wait_ge(x3_done, v - 1)
                    for h in range(HP):
                        st.mark(dve.bn_stats(stats[:, ds(HP * (v - 2) + h, 1), :].rearrange("p a d -> p (a d)"),
                                             x_tile(HP * (v - 2) + h)))
                elif step.startswith("logits"):
                    q = int(step[7:])
                    dve.wait_ge(pe6, n)
                    dve.tensor_tensor(lg[:, 2 * q:2 * q + 2, :], side[0][:, 0:2 * E].rearrange("p (t e) -> p t e", e=E),
                                      brB[:].unsqueeze(1).broadcast_to((P, 2, E)), ALU.add).then_inc(ev6, 1)
                elif step.startswith("parts") and k == 0:
                    dve.wait_ge(pe6, n)
                    turned_copy(dve.tensor_copy, par, int(step[6:]), 0).then_inc(ev6, 1)

            both = rest.rearrange("p (j d) -> p j d", d=HD)

            def rest_parts(v, w):
                dve.wait_ge(high_ready, HP * (v + 1)) if w == 0 else dve.wait_ge(k_high, v + 1)
                dve.tensor_tensor(both[:, 32 * w:32 * w + 32, :], qkf[:, w].rearrange("p h (j d) -> p (h j) d", d=HD),
                                  stack[:, w, :, 2, :], ALU.subtract).then_inc(rest_ready, 1)

            def low_parts(v, w):
                dve.wait_ge((mid_ready, k_mid)[w], v + 1)
                dve.wait_ge(rest_ready, 2 * v + 1 + w)
                dve.tensor_tensor(parts(w, "low")[:, :, 0, :], both[:, 32 * w:32 * w + 32, :],
                                  stack[:, w, :, 5, :], ALU.subtract).then_inc(low_ready, 1)

            def row_max(v, h):
                dve.wait_ge(s1_done, H * v + h + 1)
                dve.tensor_reduce(negm[:, :, h], s_bank[h % 2], AX.X, ALU.max, negate=True).then_inc(max_done, 1)

            def max_parts(v, g):
                part = [nst[:, :, 32 * k + LAG * g:32 * k + LAG * (g + 1)] for k in range(2)]
                m = negm[:, :, LAG * g:LAG * (g + 1)]
                dve.wait_ge(max_done, H * v + LAG * (g + 1))
                st.mark(dve.tensor_copy(part[0], m))
                st.wait()
                dve.tensor_tensor(part[1], m, part[0], ALU.subtract).then_inc(neg_ready, 1)

            def route_row(t):
                normalise(t, Z[:, t, :]).then_inc(zr_ready, 1)

            def round_(v, par, before=True, after=True):
                for h in range(H):
                    row_max(v, h)
                    if after and h == 0:
                        zs(v + 1)
                    if not after and h == 2:
                        norm_stats(4, 0, EARLY)
                    if not after and 2 < h < EARLY + 3:
                        route_row(h - 3)
                    g = h // LAG
                    if h % LAG == LAG - 1:
                        max_parts(v, g)
                    todo = planned(h, before, after)
                    first = len(todo) - 1 if h % LAG == LAG - 1 else len(todo)
                    first = max(first, 0)
                    for step in todo[:first]:
                        side_step(step, v + 1, 1 - par)
                    if h % LAG == LAG - 1:
                        dve.wait_ge(neg_turned, NG * v + g + 1)
                        dve.tensor_copy(negT[g % 2], NEGB).then_inc(negt_ready, 1)
                    for step in todo[first:]:
                        side_step(step, v + 1, 1 - par)
                    if after and h in (4, 5):
                        rest_parts(v + 1, h - 4)
                    if after and h in (6, 7):
                        low_parts(v + 1, h - 6)

            zs(0)
            for step in FIRST:
                side_step(step, 0, 0)
                if step == "project 1":
                    for w in range(2):
                        rest_parts(0, w)
                    for w in range(2):
                        low_parts(0, w)
            round_(0, 0, before=False)
            with dve.Fori(0, B // 2 - 1) as i:
                for k in range(2):
                    steps[k].enter(i, 2 * PER[k])
                st.enter(i, 0, 2 * (NG + 2 + HP))
                round_(2 * i + 1, 1)
                round_(2 * i + 2, 0)
                st.leave(B // 2 - 1)
                for k in range(2):
                    steps[k].leave(B // 2 - 1)
            round_(B - 1, 1, after=False)
            for step in FINISH:
                side_step(step, B + 1, 1)

            norm_stats(5, EARLY, T)
            for t in range(EARLY, T):
                route_row(t)
            for step in LATE:
                side_step(step, 0, 0)
            dve.wait_ge(ev6, steps[0].now())
            st.mark(dve.tensor_reduce(top[:], lg, AX.X, ALU.max))
            st.wait()
            st.mark(dve.tensor_tensor(eq, lg, top[:].unsqueeze(2).broadcast_to((P, T, E)), ALU.is_ge))
            st.wait()
            st.mark(dve.scalar_tensor_tensor(out=eq, in0=eq, scalar=-float(E), in1=iota_e[:].unsqueeze(1)
                                             .broadcast_to((P, T, E)), op0=ALU.mult, op1=ALU.add))
            st.wait()
            st.mark(dve.tensor_reduce(first[:], eq, AX.X, ALU.min))
            st.wait()
            st.mark(dve.tensor_scalar(first[:], first[:], float(E), None, ALU.add))
            st.wait()
            dve.tensor_tensor(onehot, iota_e[:].unsqueeze(1).broadcast_to((P, T, E)),
                              first[:].unsqueeze(2).broadcast_to((P, T, E)), ALU.is_equal).then_inc(onehot_ready, 1)
            dve.wait_ge(rank_done, 1)
            st.mark(dve.tensor_copy(cum_a, PS[:, 3, P:2 * P].rearrange("p (t e) -> p t e", e=E)))
            st.wait()
            st.mark(dve.tensor_copy(place, cum_a))
            a, b = cum_a, cum_b
            step = 1
            while step < T:
                st.mark(dve.tensor_copy(b[:, 0:step, :], a[:, 0:step, :]))
                st.mark(dve.tensor_tensor(b[:, step:T, :], a[:, step:T, :], a[:, 0:T - step, :], ALU.add))
                st.wait()
                a, b = b, a
                step *= 2
            st.mark(dve.tensor_tensor(place, a, place, ALU.subtract))
            n_tiles, n_cum, n_tmp, n_base = (tiles[:, k, :] for k in range(4))
            st.mark(dve.tensor_scalar(n_tiles, a[:, T - 1, :], 1.0 / P, (P - 1.0) / P - 0.5 + 0.5 / P, ALU.mult, ALU.add))
            st.wait()
            st.mark(dve.tensor_scalar(n_tiles, n_tiles, MAGIC, MAGIC, ALU.add, ALU.subtract))
            st.wait()
            st.mark(dve.tensor_copy(n_cum, n_tiles))
            st.wait()
            a, b = n_cum, n_tmp
            step = 1
            while step < E:
                st.mark(dve.tensor_copy(b[:, 0:step], a[:, 0:step]))
                st.mark(dve.tensor_tensor(b[:, step:E], a[:, step:E], a[:, 0:E - step], ALU.add))
                st.wait()
                a, b = b, a
                step *= 2
            st.mark(dve.tensor_tensor(n_base, a, n_tiles, ALU.subtract))
            st.mark(dve.tensor_tensor(over, a.unsqueeze(1).broadcast_to((P, J, E)),
                                      iota_j[:].unsqueeze(2).broadcast_to((P, J, E)), ALU.is_le))
            st.wait()
            st.mark(dve.tensor_scalar(n_base, n_base, float(P), None, ALU.mult))
            st.mark(dve.tensor_tensor(place, place, PS[:, 3, 0:P].rearrange("p (t e) -> p t e", e=E), ALU.add))
            st.mark(dve.tensor_reduce(ef[:], over, AX.X, ALU.add))
            st.wait()
            st.mark(dve.tensor_tensor(place, place, n_base.unsqueeze(1).broadcast_to((P, T, E)), ALU.add))
            st.mark(dve.tensor_scalar(ef[:], ef[:], E - 1.0, None, ALU.min))
            st.wait()
            st.mark(dve.tensor_tensor(place, place, onehot, ALU.mult))
            st.mark(dve.tensor_copy(expert[:], ef[:]))
            st.wait()
            st.mark(dve.tensor_reduce(posf[:], place, AX.X, ALU.add))
            st.wait()
            st.mark(dve.tensor_scalar(place_tile[:], posf[:], 1.0 / P, 0.5 / P - 0.5, ALU.mult, ALU.add))
            st.wait()
            st.mark(dve.tensor_scalar(place_tile[:], place_tile[:], MAGIC, MAGIC, ALU.add, ALU.subtract))
            st.wait()
            dve.wait_ge(iota_ready, 1)
            st.mark(dve.scalar_tensor_tensor(out=posf[:], in0=place_tile[:], scalar=-float(P), in1=posf[:],
                                             op0=ALU.mult, op1=ALU.add))
            st.mark(dve.tensor_tensor(at_tile[:, :, 0, :], iota_j[:].unsqueeze(1).broadcast_to((P, T, J)),
                                      place_tile[:].unsqueeze(2).broadcast_to((P, T, J)), ALU.is_equal))
            st.wait()
            st.mark(dve.tensor_tensor(at_row, iota_r.unsqueeze(1).broadcast_to((P, T, P)),
                                      posf[:].unsqueeze(2).broadcast_to((P, T, P)), ALU.is_equal))
            st.mark(dve.tensor_tensor(at_tile[:, :, 1, :], at_tile[:, :, 0, :],
                                      iota_t.unsqueeze(2).broadcast_to((P, T, J)), ALU.mult))
            dve.tensor_scalar(at_tile[:, :, 2, :], at_tile[:, :, 0, :], iota_p, None, ALU.mult)\
               .then_inc(places_ready, 1)
            dve.wait_ge(rows_done, 1)
            found, its_tile, its_row = (PS[:, 3, J * k:J * (k + 1)] for k in range(3))
            st.mark(dve.tensor_scalar(row_of, its_tile, float(P), 2.0 * N, ALU.mult, ALU.add))
            st.wait()
            st.mark(dve.tensor_tensor(row_of, row_of, its_row, ALU.add))
            st.wait()
            st.mark(dve.scalar_tensor_tensor(out=row_of, in0=found, scalar=-2.0 * N, in1=row_of, op0=ALU.mult,
                                             op1=ALU.add))
            st.wait()
            st.mark(dve.tensor_copy(row_dst[:], row_of))
            st.wait()
            st.mark(dve.tensor_scalar(row_of, row_of, float(N), None, ALU.min))
            st.wait()
            dve.tensor_copy(row_src[:], row_of).then_inc(pos_ready, 1)
            dve.wait_ge(be_in, 32)

            def expert_of(j):
                return dve.value_load(expert[0:1, ds(j, 1)], min_val=0, max_val=E - 1)

            def hidden(j, par, e):
                dve.wait_ge(h_done, j + 1)
                wait(dve, ht_done, j - 1)
                dve.tensor_tensor(hn[par], PS[:, 2 + par, :], b1B[:, ds(e, 1), :].rearrange("p a f -> p (a f)"),
                                  ALU.add).then_inc(h_copied, 1)

            def take_x(j, i, par, e):
                dve.wait_ge(ez_in[par], 16 * (i + 1))
                wait(dve, y_copied, j - 1)
                dve.tensor_tensor(xb[par], ezx[par][:, D:2 * D], b2B[:, ds(e, 1), :].rearrange("p a f -> p (a f)"),
                                  ALU.add).then_inc(xb_done, 1)

            def result(j, i, par):
                dve.wait_ge(y_done, j + 1)
                dve.wait_ge(xb_done, j + 1)
                if not (isinstance(j, int) and j < 2):
                    dve.wait_ge(y_out[par], 16 * i)
                dve.tensor_tensor(ys[par], PS[:, 6 + par, 0:D], xb[par], ALU.add).then_inc(y_copied, 1)

            def start(j, i, par, e):
                take_x(j, i, par, e)
                hidden(j, par, e)

            start(0, 0, 0, expert_of(0))
            start(1, 0, 1, expert_of(1))
            result(0, 0, 0)
            start(2, 1, 0, expert_of(2))
            result(1, 0, 1)
            start(3, 1, 1, expert_of(3))
            result(2, 1, 0)
            with dve.Fori(2, J // 2) as i:
                e_even, e_odd = (expert_of(2 * i + k) for k in (0, 1))
                start(2 * i, i, 0, e_even)
                result(2 * i - 1, i - 1, 1)
                start(2 * i + 1, i, 1, e_odd)
                result(2 * i, i, 0)
            start(J - 1, J // 2, 0, expert_of(J - 1))
            result(J - 2, J // 2 - 1, 1)
            result(J - 1, J // 2, 0)

        @block.tensor
        def _(pe):
            def turn_weights(n):
                wait(pe, wt_copied, n - 3)
                for m in range(4):
                    ins = pe.transpose(PS[:, 4 + n % 4, P * m:P * m + P], TW[4 * n + m][1], ident[:])
                ins.then_inc(wt_done, 1)

            pe.wait_ge(const_ready, 1)

            def sum_products(t, par):
                if not valid(t):
                    return
                pe.wait_ge(prod_done, t + 1)
                wait(pe, raw_done, t - 1)
                pe.matmul(PS[:, par, 0:PAIRS[NB]], ident[:], causal[:, 0:PAIRS[NB]], start=True, stop=False)
                for d in range(HD):
                    ins = pe.matmul(PS[:, par, 0:PAIRS[NB]], ident[:], prod[par][:, d, :], start=False,
                                    stop=(d == HD - 1))
                ins.then_inc(sum_done, 1)

            def sum_values(t, par):
                if not valid(t):
                    return
                pe.wait_ge(pv_pool, t + 1)
                pe.wait_ge(pv_dve, t + 1)
                wait(pe, x1_done, t - 1)
                pe.matmul(PS[:, 2 + par, 0:D], ident[:], X[:, ds(t, 1), :].rearrange("p a d -> p (a d)"), start=True,
                          stop=False)
                for k in range(0, H, 2):
                    lo = QR * HD * (k // QR)
                    ins = pe.matmul(PS[:, 2 + par, lo:D], ident[:], prod2[par][:, k, lo:D], start=False,
                                    stop=(k == H - 2))
                ins.then_inc(total_done, 1)

            def step(i, k):
                sum_products(i, k)
                sum_values(i - 2, k)

            for i in range(FILL):
                step(i, i % 2)
            with pe.Fori(FILL // 2, T // 2) as i:
                for k in range(2):
                    step(2 * i + k, k)
            step(T, 0)
            pe.wait_ge(wa_in, 64)
            for n in range(NA):
                turn_weights(n)
            step(T + 1, 1)
            pe.wait_ge(w_ready, T)
            for n in range(NA, NW):
                turn_weights(n)

            for t in range(T):
                pe.wait_ge(z_ready, t + 1)
                bank = PS[:, t // 2 % 4, :].rearrange("p (k h n) -> p k h n", k=KD, h=2)
                if t % 2 == 0:
                    wait(pe, zt_copied, t // 2 - 3)
                for k in range(KD):
                    ins = pe.transpose(bank[:, k, t % 2, :], Zall[:, t, P * k:P * k + P], ident[:])
                if t % 2:
                    ins.then_inc(zt_done, 1)
            pe.wait_ge(wt_copied, NW)

            def project(wT, cc, f, u):
                wait(pe, mm_copied, u - KF + 1)
                for k in range(KD):
                    ins = pe.matmul(PS[:, f, :], wT[:, k, P * f:P * f + P], zT[:, k, ds(cc * CH, CH)],
                                    start=(k == 0), stop=(k == KD - 1))
                ins.then_inc(mm_done, 1)

            pe.wait_ge(zt_copied, T // 2)
            for f in range(KF):
                pe.wait_ge(xq_ready, 1)
                project(gateT, 0, f, f)
            with pe.Fori(1, NCH) as cc:
                pe.wait_ge(xq_ready, cc + 1)
                for f in range(KF):
                    project(gateT, cc, f, cc * KF + f)
            with pe.Fori(0, NCH) as cc:
                for f in range(KF):
                    project(upT, cc, f, UNITS + cc * KF + f)

            def down(i, par):
                t = 2 * i + par
                pe.wait_ge(ok_ready, t + 1)
                wait(pe, x2_done, t - 1)
                for f in range(KF):
                    ins = pe.matmul(PS[:, 6 + par, 0:D], ok[par][:, f, :], downT[:, f, :], start=(f == 0),
                                    stop=(f == KF - 1))
                ins.then_inc(down_done, 1)

            down(0, 0)
            down(0, 1)
            with pe.Fori(1, T // 2) as i:
                down(i, 0)
                down(i, 1)

            steps = Steps(), Steps()
            pe_side, ev_side = (pe6, pe7), (ev6, ev7)

            def turn_both(k, tiles):
                for c in range(KD):
                    for h in range(HP):
                        ins = pe.transpose(side[k][:, S * c + P * h:S * c + P * h + P], tiles[:, h, P * c:P * c + P],
                                           ident[:])
                return ins

            def side_step(step, v, par, loads):
                k = BANK[step]
                wait(pe, ev_side[k], steps[k].now())
                if step == "turn z":
                    pe.wait_ge(zz_ready, v + 1)
                    ins = turn_both(0, zz)
                elif step == "turn ctx":
                    pe.wait_ge(ct_in[par], 16 * loads)
                    ins = turn_both(1, ct[par])
                elif step in ("project 0", "project 1"):
                    if k == 0:
                        pe.wait_ge(ev7, steps[1].now())
                    for w, src in ((0, zTb), (1, cTb)):
                        for c in range(KD):
                            ins = pe.matmul(side[k][:, D * w:D * w + D], src[:, c, P * k:P * k + P], attnT[:, w, c, :],
                                            start=(c == 0), stop=(c == KD - 1))
                elif step == "values":
                    for h in range(HP):
                        for c in range(KD):
                            ins = pe.matmul(side[0][:, D * h:D * h + D], cTb[:, c, P * h:P * h + P], attnT[:, 2, c, :],
                                            start=(c == 0), stop=(c == KD - 1))
                elif step.startswith("parts"):
                    m = int(step[6:])
                    pe.wait_ge(low_ready, 2 * v + 1 + m // 4)
                    bank = side[k][0:NP6, :].bitcast(BF16)
                    for q in range(4):
                        for h in range(HP):
                            j = h * H + 4 * (m % 4) + q
                            ins = pe.transpose(bank[:, S * q + P * h:S * q + P * h + P],
                                               stack[:, m // 4, j, :, :].rearrange("p c d -> p (c d)"), identb[:])
                elif step in ("back 0", "back 1"):
                    pe.wait_ge(ot_ready, 2 * (v - 1))
                    for g in range(4):
                        ins = pe.transpose(side[k][:, P * g:P * g + P], OT[:, g, P * k:P * k + P], ident[:])
                elif step == "turn out":
                    pe.wait_ge(ev6, steps[0].now())
                    ins = turn_both(1, on)
                elif step == "output":
                    pe.wait_ge(ev7, steps[1].now())
                    for h in range(HP):
                        for c in range(KD):
                            ins = pe.matmul(side[0][:, D * h:D * h + D], oT[:, c, P * h:P * h + P], attnT[:, 3, c, :],
                                            start=(c == 0), stop=(c == KD - 1))
                elif step.startswith("rows"):
                    q = int(step[5:])
                    pe.wait_ge(zr_ready, 2 * q + 2)
                    for c in range(KD):
                        for h in range(2):
                            ins = pe.transpose(side[1][:, 2 * P * c + P * h:2 * P * c + P * h + P],
                                               Z[:, 2 * q + h, P * c:P * c + P], ident[:])
                elif step.startswith("logits"):
                    q = int(step[7:])
                    pe.wait_ge(ev7, steps[1].now())
                    for h in range(2):
                        for c in range(KD):
                            ins = pe.matmul(side[0][:, E * h:E * h + E], zr[q % 2][:, c, P * h:P * h + P], Wr[:, c, :],
                                            start=(c == 0), stop=(c == KD - 1))
                ins.then_inc(pe_side[k], 1)
                steps[k].next()

            def first_scores(v, par, h):
                c = H * v + h
                wait(pe, max_done, c - 1)
                if h % LAG == 1:
                    wait(pe, negt_ready, NG * v + h // LAG)
                for q in range(HP):
                    ins = pe.matmul(s_bank[h % 2][:, q, :], stackT[par][0][:, h, P * q:P * q + P],
                                    stackT[par][1][:, h, :], start=True, stop=True)
                ins.then_inc(s1_done, 1)

            def second_scores(b, par, h):
                c = H * b + h
                wait(pe, e_done, c - 1)
                if h % LAG == 0:
                    pe.wait_ge(negt_ready, NG * b + h // LAG + 1)
                for k in range(HP):
                    pe.matmul(st_bank[h % 2][:, k, :], stackT[par][1][:, h, P * k:P * k + P], stackT[par][0][:, h, :],
                              start=True, stop=False)
                    ins = pe.matmul(st_bank[h % 2][:, k, :], select_row[:, h, :], negT[h // LAG % 2], start=False,
                                    stop=True)
                ins.then_inc(s2_done, 1)

            def weigh(b, par, h):
                pe.wait_ge(e_done, H * b + h + 2)
                if h % 8 == 0:
                    wait(pe, ot_ready, 2 * b - 1 + h // 8)
                for k in range(HP):
                    for g in (h, h + 1):
                        ins = pe.matmul(o_part(g), V[par][:, k, g, :], PT[g % 4][:, k, :], start=(k == 0),
                                        stop=(k == HP - 1))
                        if k == HP - 1:
                            ins.then_inc(pv_done, 1)

            def turn_maxima(v, g):
                pe.wait_ge(neg_ready, NG * v + g + 1)
                for h in range(HP):
                    ins = pe.transpose(NEGB[:, P * h:P * h + P], nst[:, h, :], identb[:])
                ins.then_inc(neg_turned, 1)

            def round_(v, par, loads, before=True, after=True):
                for h in range(H):
                    first_scores(v, par, h)
                    weighs = h % 2 == 0 and (h >= LAG + 2 or before)
                    if weighs and h % LAG == 0:
                        weigh(*lagged(v, par, h, LAG + 2))
                    if h >= LAG or before:
                        second_scores(*lagged(v, par, h, LAG))
                    if weighs and h % LAG:
                        weigh(*lagged(v, par, h, LAG + 2))
                    todo = planned(h, before, after)
                    first = 1 if h == LAG - 1 else len(todo)
                    for step in todo[:first]:
                        side_step(step, v + 1, 1 - par, loads)
                    if h % LAG == LAG - 1:
                        turn_maxima(v, h // LAG)
                    for step in todo[first:]:
                        side_step(step, v + 1, 1 - par, loads)

            pe.wait_ge(b_in, 96)
            for step in FIRST:
                side_step(step, 0, 0, 1)
            for k in range(2):
                pe.wait_ge(ev_side[k], steps[k].now())
            round_(0, 0, 1, before=False)
            with pe.Fori(0, B // 2 - 1) as i:
                for k in range(2):
                    steps[k].enter(i, 2 * PER[k])
                round_(2 * i + 1, 1, i + 2)
                round_(2 * i + 2, 0, i + 2)
                for k in range(2):
                    steps[k].leave(B // 2 - 1)
            for k in range(2):
                pe.wait_ge(ev_side[k], steps[k].now())
            round_(B - 1, 1, 0, after=False)
            for h in range(H - LAG, H):
                second_scores(B - 1, 1, h)
                if h % 2 == 0:
                    weigh(B - 1, 1, h - 2)
            weigh(B - 1, 1, H - 2)
            for step in FINISH:
                side_step(step, B + 1, 1, 0)

            for step in LATE:
                side_step(step, 0, 0, 0)
            pe.wait_ge(onehot_ready, 1)
            oh = onehot.rearrange("p t e -> p (t e)")
            pe.matmul(PS[:, 3, 0:P], before[:], oh, start=True, stop=True)
            pe.matmul(PS[:, 3, P:2 * P], ones[:], oh, start=True, stop=True).then_inc(rank_done, 1)
            pe.wait_ge(places_ready, 1)
            for t in range(T):
                ins = pe.matmul(PS[:, 3, 0:3 * J], at_row[:, t, :], at_tile[:, t].rearrange("p c j -> p (c j)"),
                                start=(t == 0), stop=(t == T - 1))
            ins.then_inc(rows_done, 1)

            def rows(j, i, par):
                pe.wait_ge(ez_in[par], 16 * (i + 1))
                wait(pe, et_copied, j - 1)
                for k in range(KD):
                    ins = pe.transpose(PS[:, par, P * k:P * k + P], ez[par][:, P * k:P * k + P], ident[:])
                ins.then_inc(et_done, 1)

            def expert_of(j):
                return pe.value_load(expert[0:1, ds(j, 1)], min_val=0, max_val=E - 1)

            def hidden(j, par, e):
                pe.wait_ge(et_copied, j + 1)
                wait(pe, h_copied, j - 1)
                for k in range(KD):
                    ins = pe.matmul(PS[:, 2 + par, :], ezT[par][:, k, :], W1[:, ds(e * KD + k, 1), :].rearrange("p a f -> p (a f)"),
                                    start=(k == 0), stop=(k == KD - 1))
                ins.then_inc(h_done, 1)

            def turn_hidden(j, par):
                pe.wait_ge(h_copied, j + 1)
                wait(pe, ht_copied, j - 1)
                for f in range(K1):
                    ins = pe.transpose(PS[:, 4 + par, P * f:P * f + P], hn[par][:, P * f:P * f + P], ident[:])
                ins.then_inc(ht_done, 1)

            def result(j, par, e):
                pe.wait_ge(ht_copied, j + 1)
                wait(pe, y_copied, j - 1)
                for f in range(K1):
                    ins = pe.matmul(PS[:, 6 + par, 0:D], hT[par][:, f, :], W2[:, ds(e * K1 + f, 1), :].rearrange("p a d -> p (a d)"),
                                    start=(f == 0), stop=(f == K1 - 1))
                ins.then_inc(y_done, 1)

            pe.wait_ge(e_in, 32)
            pe.wait_ge(pos_ready, 1)
            rows(0, 0, 0)
            hidden(0, 0, expert_of(0))
            rows(1, 0, 1)
            turn_hidden(0, 0)
            hidden(1, 1, expert_of(1))
            rows(2, 1, 0)
            result(0, 0, expert_of(0))
            turn_hidden(1, 1)
            hidden(2, 0, expert_of(2))
            with pe.Fori(1, J // 2) as i:
                e_before, e_even = expert_of(2 * i - 1), expert_of(2 * i)
                rows(2 * i + 1, i, 1)
                result(2 * i - 1, 1, e_before)
                turn_hidden(2 * i, 0)
                e_odd = expert_of(2 * i + 1)
                hidden(2 * i + 1, 1, e_odd)
                rows(2 * i + 2, i + 1, 0)
                result(2 * i, 0, e_even)
                turn_hidden(2 * i + 1, 1)
                e_after = expert_of(2 * i + 2)
                hidden(2 * i + 2, 0, e_after)
            result(J - 2, 1, expert_of(J - 2))
            turn_hidden(J - 1, 0)
            result(J - 1, 0, expert_of(J - 1))


_INS = ['x', 'ctx_1024', 'L0_ffn_w_gate', 'L0_ffn_w_up', 'L0_ffn_w_down', 'L1_xattn_Wq', 'L1_xattn_bq', 'L1_xattn_Wk',
        'L1_xattn_bk', 'L1_xattn_Wv', 'L1_xattn_bv', 'L1_xattn_Wo', 'L1_xattn_bo', 'L1_ffn_W1', 'L1_ffn_b1',
        'L1_ffn_W2', 'L1_ffn_b2', 'L1_ffn_Wr', 'L1_ffn_br']


def kernel(**inputs):
    import numpy as _np
    import concourse.bacc as _bacc
    from concourse import mybir as _mybir
    from concourse.bass_utils import run_bass_kernel_spmd as _run

    nc = _bacc.Bacc("TRN2", target_bir_lowering=False, num_devices=1)
    arrays, args = {}, {}
    for name in _INS:
        a = _np.ascontiguousarray(inputs[name])
        arrays[f"in_{name}_dram"] = a
        args[name] = nc.dram_tensor(f"in_{name}_dram", a.shape, _mybir.dt.from_np(a.dtype), kind="ExternalInput").ap()
    out = nc.dram_tensor("out_0_dram", inputs["x"].shape, _mybir.dt.float32, kind="ExternalOutput").ap()
    build(nc, args, out)
    r = _run(nc, [arrays], core_ids=[0])
    return r.results[0]["out_0_dram"]
```
